# Optimizing a Trainium2 kernel written in Bass

```python
import numpy as np
import jax
import jax.numpy as jnp

def _softmax(x, axis=-1):
    return jax.nn.softmax(x, axis=axis)

def _gelu(x):
    return jax.nn.gelu(x, approximate=True)

def _silu(x):
    return jax.nn.silu(x)

def _sigmoid(x):
    return jax.nn.sigmoid(x)

def _layernorm(x, axis=-1, eps=1e-05):
    m = jnp.mean(x, axis=axis, keepdims=True)
    v = jnp.var(x, axis=axis, keepdims=True)
    return (x - m) / jnp.sqrt(v + eps)

def _scatter_add(tgt, idx, src, axis=0):
    return tgt.at[idx].add(src)

def _segment_sum(src, seg, n):
    return jax.ops.segment_sum(src, seg, n)
kernel_name = 'mk_seq_postln_d2_jaxref_r8_99eb1a'

def setup_inputs(seed: int=0):
    np.random.seed(seed)
    _w = jnp.asarray

    def _L0_attn_setup():
        import jax, jax.numpy as jnp
        import numpy as np
        B, T, HID = (4, 256, 128)
        H, D, V = (8, 64, 128)
        EPS = 1e-05

        def _rotary(x, T, D):
            inv_freq = 1.0 / 10000.0 ** (jnp.arange(0, D, 2, dtype=jnp.float32) / D)
            t = jnp.arange(T, dtype=jnp.float32)
            freqs = t[:, None] * inv_freq[None, :]
            emb = jnp.concatenate([freqs, freqs], axis=-1)
            cos = jnp.cos(emb)[None, None, :, :]
            sin = jnp.sin(emb)[None, None, :, :]
            x1, x2 = jnp.split(x, 2, axis=-1)
            rot = jnp.concatenate([-x2, x1], axis=-1)
            return x * cos + rot * sin
        key = jax.random.key(seed)
        ks = jax.random.split(key, 7)
        sc = 0.02
        return {'x': jax.random.normal(ks[0], (B, T, HID), dtype=jnp.float32), 'Wq': jax.random.normal(ks[1], (H * D, HID), dtype=jnp.float32) * sc, 'Wk': jax.random.normal(ks[2], (H * D, HID), dtype=jnp.float32) * sc, 'Wv': jax.random.normal(ks[3], (H * V, HID), dtype=jnp.float32) * sc, 'Wg': jax.random.normal(ks[4], (H * V, HID), dtype=jnp.float32) * sc, 'Wo': jax.random.normal(ks[5], (HID, H * V), dtype=jnp.float32) * sc, 'gn_weight': jnp.ones((H * V,), dtype=jnp.float32), 'gn_bias': jnp.zeros((H * V,), dtype=jnp.float32)}
    _L0_attn_in = _L0_attn_setup()

    def _L0_ffn_setup():
        import jax, jax.numpy as jnp
        import numpy as np
        D_MODEL = 128
        N_HEADS = 16
        HEAD_DIM = D_MODEL // N_HEADS
        KV_LATENT = 64
        N_EXPERTS = 4
        D_HIDDEN = 4 * D_MODEL
        B, T = (2, 128)

        def rmsnorm(x, w, eps=1e-06):
            return w * (x * jax.lax.rsqrt(jnp.mean(x * x, axis=-1, keepdims=True) + eps))

        def layernorm(x, g, b, eps=1e-05):
            mu = jnp.mean(x, axis=-1, keepdims=True)
            var = jnp.mean((x - mu) ** 2, axis=-1, keepdims=True)
            return (x - mu) * jax.lax.rsqrt(var + eps) * g + b

        def apply_rope(x):
            t, d = (x.shape[2], x.shape[3])
            half = d // 2
            pos = jnp.arange(t, dtype=x.dtype)[:, None]
            inv_freq = 1.0 / 10000.0 ** (jnp.arange(half, dtype=x.dtype) / half)
            ang = pos * inv_freq[None, :]
            sin, cos = (jnp.sin(ang), jnp.cos(ang))
            x1, x2 = (x[..., :half], x[..., half:])
            return jnp.concatenate([x1 * cos - x2 * sin, x1 * sin + x2 * cos], axis=-1)

        def mla_attention(x, Wq, Wdkv, Wuk, Wuv, Wo, ln_g, ln_b):
            b, t, _ = x.shape
            q = (x @ Wq.T).reshape(b, t, N_HEADS, HEAD_DIM).transpose(0, 2, 1, 3)
            latent = layernorm(x @ Wdkv.T, ln_g, ln_b)
            k = (latent @ Wuk.T).reshape(b, t, N_HEADS, HEAD_DIM).transpose(0, 2, 1, 3)
            v = (latent @ Wuv.T).reshape(b, t, N_HEADS, HEAD_DIM).transpose(0, 2, 1, 3)
            q = apply_rope(q)
            k = apply_rope(k)
            scores = jnp.einsum('bhqd,bhkd->bhqk', q, k) / np.sqrt(HEAD_DIM)
            causal = jnp.tril(jnp.ones((t, t), dtype=bool))
            scores = jnp.where(causal, scores, -jnp.inf)
            attn = jax.nn.softmax(scores, axis=-1)
            out = jnp.einsum('bhqk,bhkd->bhqd', attn, v).transpose(0, 2, 1, 3).reshape(b, t, D_MODEL)
            return out @ Wo.T

        def moe(x, gate_w, gate_b, W1, b1, W2, b2):
            logits = x @ gate_w.T + gate_b
            top = jnp.argmax(logits, axis=-1)
            onehot = jax.nn.one_hot(top, N_EXPERTS, dtype=x.dtype)
            h = jax.nn.relu(jnp.einsum('btd,ehd->bteh', x, W1) + b1)
            y = jnp.einsum('bteh,edh->bted', h, W2) + b2
            return jnp.einsum('bted,bte->btd', y, onehot)
        key = jax.random.key(seed)
        ks = jax.random.split(key, 16)
        s = lambda fan_in: 1.0 / np.sqrt(fan_in)
        return {'x': jax.random.normal(ks[0], (B, T, D_MODEL), jnp.float32), 'norm1_w': jnp.ones((D_MODEL,), jnp.float32), 'norm2_w': jnp.ones((D_MODEL,), jnp.float32), 'Wq': jax.random.normal(ks[1], (D_MODEL, D_MODEL), jnp.float32) * s(D_MODEL), 'Wdkv': jax.random.normal(ks[2], (KV_LATENT, D_MODEL), jnp.float32) * s(D_MODEL), 'Wuk': jax.random.normal(ks[3], (D_MODEL, KV_LATENT), jnp.float32) * s(KV_LATENT), 'Wuv': jax.random.normal(ks[4], (D_MODEL, KV_LATENT), jnp.float32) * s(KV_LATENT), 'Wo': jax.random.normal(ks[5], (D_MODEL, D_MODEL), jnp.float32) * s(D_MODEL), 'ln_g': jnp.ones((KV_LATENT,), jnp.float32), 'ln_b': jnp.zeros((KV_LATENT,), jnp.float32), 'gate_w': jax.random.normal(ks[6], (N_EXPERTS, D_MODEL), jnp.float32) * s(D_MODEL), 'gate_b': jnp.zeros((N_EXPERTS,), jnp.float32), 'W1': jax.random.normal(ks[7], (N_EXPERTS, D_HIDDEN, D_MODEL), jnp.float32) * s(D_MODEL), 'b1': jnp.zeros((N_EXPERTS, D_HIDDEN), jnp.float32), 'W2': jax.random.normal(ks[8], (N_EXPERTS, D_MODEL, D_HIDDEN), jnp.float32) * s(D_HIDDEN), 'b2': jnp.zeros((N_EXPERTS, D_MODEL), jnp.float32)}
    _L0_ffn_in = _L0_ffn_setup()

    def _L1_attn_setup():
        import jax, jax.numpy as jnp
        import numpy as np
        NEG = -1000000000.0

        def _attention(x, Wq, bq, Wk, bk, Wv, bv, Wo, num_heads=16):
            B, N, E = x.shape
            H = num_heads
            D = E // H
            scale = D ** (-0.5)
            q = (jnp.einsum('bne,fe->bnf', x, Wq) + bq).reshape(B, N, H, D).transpose(0, 2, 1, 3)
            k = (jnp.einsum('bne,fe->bnf', x, Wk) + bk).reshape(B, N, H, D).transpose(0, 2, 1, 3)
            v = (jnp.einsum('bne,fe->bnf', x, Wv) + bv).reshape(B, N, H, D).transpose(0, 2, 1, 3)
            scores = jnp.einsum('bhqd,bhkd->bhqk', q, k) * scale
            scores = scores.at[:, :, 0, -1].set(NEG)
            scores = scores.at[:, :, -1, 0].set(NEG)
            weights = jax.nn.softmax(scores, axis=-1)
            out = jnp.einsum('bhqk,bhkd->bhqd', weights, v)
            out = out.transpose(0, 2, 1, 3).reshape(B, N, E)
            return jnp.einsum('bne,fe->bnf', out, Wo)
        key = jax.random.key(seed)
        ks = jax.random.split(key, 8)
        B, N, E = (4, 256, 128)
        s = E ** (-0.5)
        return {'x': jax.random.normal(ks[0], (B, N, E), jnp.float32), 'Wq': jax.random.normal(ks[1], (E, E), jnp.float32) * s, 'bq': jax.random.normal(ks[2], (E,), jnp.float32) * 0.02, 'Wk': jax.random.normal(ks[3], (E, E), jnp.float32) * s, 'bk': jax.random.normal(ks[4], (E,), jnp.float32) * 0.02, 'Wv': jax.random.normal(ks[5], (E, E), jnp.float32) * s, 'bv': jax.random.normal(ks[6], (E,), jnp.float32) * 0.02, 'Wo': jax.random.normal(ks[7], (E, E), jnp.float32) * s}
    _L1_attn_in = _L1_attn_setup()

    def _L1_ffn_setup():
        import jax, jax.numpy as jnp
        import numpy as np
        EPS = 1e-05

        @jax.custom_vjp
        def ste_quantize(w):
            scale = jnp.maximum(jnp.mean(jnp.abs(w)), EPS)
            return jnp.clip(jnp.round(w / scale), -1.0, 1.0)

        def _ste_fwd(w):
            return (ste_quantize(w), None)

        def _ste_bwd(_, g):
            return (g,)
        ste_quantize.defvjp(_ste_fwd, _ste_bwd)
        key = jax.random.key(seed)
        k1, k2 = jax.random.split(key)
        x = jax.random.normal(k1, (8, 1024, 128), dtype=jnp.float32)
        weight = jax.random.normal(k2, (128, 128), dtype=jnp.float32) * 0.02
        return {'x': x, 'weight': weight}
    _L1_ffn_in = _L1_ffn_setup()
    _d = {'L0_attn_x': _L0_attn_in['x'], 'L0_attn_Wq': _L0_attn_in['Wq'], 'L0_attn_Wk': _L0_attn_in['Wk'], 'L0_attn_Wv': _L0_attn_in['Wv'], 'L0_attn_Wg': _L0_attn_in['Wg'], 'L0_attn_Wo': _L0_attn_in['Wo'], 'L0_attn_gn_weight': _L0_attn_in['gn_weight'], 'L0_attn_gn_bias': _L0_attn_in['gn_bias'], 'L0_ffn_norm1_w': _L0_ffn_in['norm1_w'], 'L0_ffn_norm2_w': _L0_ffn_in['norm2_w'], 'L0_ffn_Wq': _L0_ffn_in['Wq'], 'L0_ffn_Wdkv': _L0_ffn_in['Wdkv'], 'L0_ffn_Wuk': _L0_ffn_in['Wuk'], 'L0_ffn_Wuv': _L0_ffn_in['Wuv'], 'L0_ffn_Wo': _L0_ffn_in['Wo'], 'L0_ffn_ln_g': _L0_ffn_in['ln_g'], 'L0_ffn_ln_b': _L0_ffn_in['ln_b'], 'L0_ffn_gate_w': _L0_ffn_in['gate_w'], 'L0_ffn_gate_b': _L0_ffn_in['gate_b'], 'L0_ffn_W1': _L0_ffn_in['W1'], 'L0_ffn_b1': _L0_ffn_in['b1'], 'L0_ffn_W2': _L0_ffn_in['W2'], 'L0_ffn_b2': _L0_ffn_in['b2'], 'L1_attn_Wq': _L1_attn_in['Wq'], 'L1_attn_bq': _L1_attn_in['bq'], 'L1_attn_Wk': _L1_attn_in['Wk'], 'L1_attn_bk': _L1_attn_in['bk'], 'L1_attn_Wv': _L1_attn_in['Wv'], 'L1_attn_bv': _L1_attn_in['bv'], 'L1_attn_Wo': _L1_attn_in['Wo'], 'L1_ffn_weight': _L1_ffn_in['weight']}
    _x0 = _d['L0_attn_x']
    _d['L0_attn_x'] = jax.random.normal(jax.random.fold_in(jax.random.key(seed), 1), (2, 1024, 128), dtype=_x0.dtype)
    del _x0
    return _d

def reference(L0_attn_x, L0_attn_Wq, L0_attn_Wk, L0_attn_Wv, L0_attn_Wg, L0_attn_Wo, L0_attn_gn_weight, L0_attn_gn_bias, L0_ffn_norm1_w, L0_ffn_norm2_w, L0_ffn_Wq, L0_ffn_Wdkv, L0_ffn_Wuk, L0_ffn_Wuv, L0_ffn_Wo, L0_ffn_ln_g, L0_ffn_ln_b, L0_ffn_gate_w, L0_ffn_gate_b, L0_ffn_W1, L0_ffn_b1, L0_ffn_W2, L0_ffn_b2, L1_attn_Wq, L1_attn_bq, L1_attn_Wk, L1_attn_bk, L1_attn_Wv, L1_attn_bv, L1_attn_Wo, L1_ffn_weight):

    def _L0_attn_ref(x, Wq, Wk, Wv, Wg, Wo, gn_weight, gn_bias):
        import jax, jax.numpy as jnp
        import numpy as np
        B, T, HID = (4, 256, 128)
        H, D, V = (8, 64, 128)
        EPS = 1e-05

        def _rotary(x, T, D):
            inv_freq = 1.0 / 10000.0 ** (jnp.arange(0, D, 2, dtype=jnp.float32) / D)
            t = jnp.arange(T, dtype=jnp.float32)
            freqs = t[:, None] * inv_freq[None, :]
            emb = jnp.concatenate([freqs, freqs], axis=-1)
            cos = jnp.cos(emb)[None, None, :, :]
            sin = jnp.sin(emb)[None, None, :, :]
            x1, x2 = jnp.split(x, 2, axis=-1)
            rot = jnp.concatenate([-x2, x1], axis=-1)
            return x * cos + rot * sin
        Bx, Tx, _ = x.shape
        q = jnp.einsum('bti,oi->bto', x, Wq).reshape(Bx, Tx, H, D).transpose(0, 2, 1, 3)
        k = jnp.einsum('bti,oi->bto', x, Wk).reshape(Bx, Tx, H, D).transpose(0, 2, 1, 3)
        v = jnp.einsum('bti,oi->bto', x, Wv).reshape(Bx, Tx, H, V).transpose(0, 2, 1, 3)
        g = jnp.einsum('bti,oi->bto', x, Wg)
        q = _rotary(q, Tx, D)
        k = _rotary(k, Tx, D)
        gamma = 1.0 - jnp.exp2(-5.0 - jnp.arange(H, dtype=jnp.float32))
        s = jnp.log2(gamma)
        n = jnp.arange(Tx, dtype=jnp.float32)
        rel = n[:, None] - n[None, :]
        causal = rel >= 0
        decay = jnp.where(causal[None, :, :], jnp.exp2(rel[None, :, :] * s[:, None, None]), 0.0)
        scores = jnp.einsum('bhtd,bhsd->bhts', q, k) * D ** (-0.5)
        scores = scores * decay[None]
        o = jnp.einsum('bhts,bhsv->bhtv', scores, v)
        o = o.transpose(0, 2, 1, 3)
        mean = jnp.mean(o, axis=-1, keepdims=True)
        var = jnp.var(o, axis=-1, keepdims=True)
        o = (o - mean) * jax.lax.rsqrt(var + EPS)
        o = o * gn_weight.reshape(H, V) + gn_bias.reshape(H, V)
        o = o.reshape(Bx, Tx, H * V)
        o = o * jax.nn.silu(g)
        return jnp.einsum('btc,oc->bto', o, Wo)

    def _L0_ffn_ref(x, norm1_w, norm2_w, Wq, Wdkv, Wuk, Wuv, Wo, ln_g, ln_b, gate_w, gate_b, W1, b1, W2, b2):
        import jax, jax.numpy as jnp
        import numpy as np
        D_MODEL = 128
        N_HEADS = 16
        HEAD_DIM = D_MODEL // N_HEADS
        KV_LATENT = 64
        N_EXPERTS = 4
        D_HIDDEN = 4 * D_MODEL
        B, T = (2, 128)

        def rmsnorm(x, w, eps=1e-06):
            return w * (x * jax.lax.rsqrt(jnp.mean(x * x, axis=-1, keepdims=True) + eps))

        def layernorm(x, g, b, eps=1e-05):
            mu = jnp.mean(x, axis=-1, keepdims=True)
            var = jnp.mean((x - mu) ** 2, axis=-1, keepdims=True)
            return (x - mu) * jax.lax.rsqrt(var + eps) * g + b

        def apply_rope(x):
            t, d = (x.shape[2], x.shape[3])
            half = d // 2
            pos = jnp.arange(t, dtype=x.dtype)[:, None]
            inv_freq = 1.0 / 10000.0 ** (jnp.arange(half, dtype=x.dtype) / half)
            ang = pos * inv_freq[None, :]
            sin, cos = (jnp.sin(ang), jnp.cos(ang))
            x1, x2 = (x[..., :half], x[..., half:])
            return jnp.concatenate([x1 * cos - x2 * sin, x1 * sin + x2 * cos], axis=-1)

        def mla_attention(x, Wq, Wdkv, Wuk, Wuv, Wo, ln_g, ln_b):
            b, t, _ = x.shape
            q = (x @ Wq.T).reshape(b, t, N_HEADS, HEAD_DIM).transpose(0, 2, 1, 3)
            latent = layernorm(x @ Wdkv.T, ln_g, ln_b)
            k = (latent @ Wuk.T).reshape(b, t, N_HEADS, HEAD_DIM).transpose(0, 2, 1, 3)
            v = (latent @ Wuv.T).reshape(b, t, N_HEADS, HEAD_DIM).transpose(0, 2, 1, 3)
            q = apply_rope(q)
            k = apply_rope(k)
            scores = jnp.einsum('bhqd,bhkd->bhqk', q, k) / np.sqrt(HEAD_DIM)
            causal = jnp.tril(jnp.ones((t, t), dtype=bool))
            scores = jnp.where(causal, scores, -jnp.inf)
            attn = jax.nn.softmax(scores, axis=-1)
            out = jnp.einsum('bhqk,bhkd->bhqd', attn, v).transpose(0, 2, 1, 3).reshape(b, t, D_MODEL)
            return out @ Wo.T

        def moe(x, gate_w, gate_b, W1, b1, W2, b2):
            logits = x @ gate_w.T + gate_b
            top = jnp.argmax(logits, axis=-1)
            onehot = jax.nn.one_hot(top, N_EXPERTS, dtype=x.dtype)
            h = jax.nn.relu(jnp.einsum('btd,ehd->bteh', x, W1) + b1)
            y = jnp.einsum('bteh,edh->bted', h, W2) + b2
            return jnp.einsum('bted,bte->btd', y, onehot)
        x = x + mla_attention(rmsnorm(x, norm1_w), Wq, Wdkv, Wuk, Wuv, Wo, ln_g, ln_b)
        x = x + moe(rmsnorm(x, norm2_w), gate_w, gate_b, W1, b1, W2, b2)
        return x

    def _L1_attn_ref(x, Wq, bq, Wk, bk, Wv, bv, Wo):
        import jax, jax.numpy as jnp
        import numpy as np
        NEG = -1000000000.0

        def _attention(x, Wq, bq, Wk, bk, Wv, bv, Wo, num_heads=16):
            B, N, E = x.shape
            H = num_heads
            D = E // H
            scale = D ** (-0.5)
            q = (jnp.einsum('bne,fe->bnf', x, Wq) + bq).reshape(B, N, H, D).transpose(0, 2, 1, 3)
            k = (jnp.einsum('bne,fe->bnf', x, Wk) + bk).reshape(B, N, H, D).transpose(0, 2, 1, 3)
            v = (jnp.einsum('bne,fe->bnf', x, Wv) + bv).reshape(B, N, H, D).transpose(0, 2, 1, 3)
            scores = jnp.einsum('bhqd,bhkd->bhqk', q, k) * scale
            scores = scores.at[:, :, 0, -1].set(NEG)
            scores = scores.at[:, :, -1, 0].set(NEG)
            weights = jax.nn.softmax(scores, axis=-1)
            out = jnp.einsum('bhqk,bhkd->bhqd', weights, v)
            out = out.transpose(0, 2, 1, 3).reshape(B, N, E)
            return jnp.einsum('bne,fe->bnf', out, Wo)
        return _attention(x, Wq, bq, Wk, bk, Wv, bv, Wo, num_heads=16)

    def _L1_ffn_ref(x, weight):
        import jax, jax.numpy as jnp
        import numpy as np
        EPS = 1e-05

        @jax.custom_vjp
        def ste_quantize(w):
            scale = jnp.maximum(jnp.mean(jnp.abs(w)), EPS)
            return jnp.clip(jnp.round(w / scale), -1.0, 1.0)

        def _ste_fwd(w):
            return (ste_quantize(w), None)

        def _ste_bwd(_, g):
            return (g,)
        ste_quantize.defvjp(_ste_fwd, _ste_bwd)
        w_ternary = ste_quantize(weight)
        scale = jnp.maximum(jnp.mean(jnp.abs(weight)), EPS)
        return jnp.einsum('bsi,oi->bso', x, w_ternary * scale)
    x = L0_attn_x
    x = _layernorm(x + _L0_attn_ref(x, L0_attn_Wq, L0_attn_Wk, L0_attn_Wv, L0_attn_Wg, L0_attn_Wo, L0_attn_gn_weight, L0_attn_gn_bias), axis=-1)
    x = _layernorm(x + _L0_ffn_ref(x, L0_ffn_norm1_w, L0_ffn_norm2_w, L0_ffn_Wq, L0_ffn_Wdkv, L0_ffn_Wuk, L0_ffn_Wuv, L0_ffn_Wo, L0_ffn_ln_g, L0_ffn_ln_b, L0_ffn_gate_w, L0_ffn_gate_b, L0_ffn_W1, L0_ffn_b1, L0_ffn_W2, L0_ffn_b2), axis=-1)
    x = _layernorm(x + _L1_attn_ref(x, L1_attn_Wq, L1_attn_bq, L1_attn_Wk, L1_attn_bk, L1_attn_Wv, L1_attn_bv, L1_attn_Wo), axis=-1)
    x = _layernorm(x + _L1_ffn_ref(x, L1_ffn_weight), axis=-1)
    return x

_drawn_inputs = setup_inputs


def setup_inputs(seed=0):
    import zlib

    import numpy as np

    out = dict(_drawn_inputs(seed))
    spreads = {'L0_attn_gn_weight': (1.0, 0.2),
     'L0_attn_gn_bias': (0.0, 0.296),
     'L0_ffn_norm1_w': (1.0, 0.2),
     'L0_ffn_norm2_w': (1.0, 0.2),
     'L0_ffn_ln_g': (1.0, 0.2),
     'L0_ffn_ln_b': (0.0, 0.1),
     'L0_ffn_gate_b': (0.0, 0.1),
     'L0_ffn_b1': (0.0, 0.1),
     'L0_ffn_b2': (0.0, 0.1)}
    factors = {'L1_attn_bq': 26.307, 'L1_attn_bk': 64.0}
    for name, (base, spread) in spreads.items():
        noise = np.random.default_rng([zlib.crc32(name.encode()), seed]).standard_normal(out[name].shape)
        drawn = base * np.exp(spread * noise) if base else spread * noise
        out[name] = jnp.asarray(drawn.astype(out[name].dtype))
    for name, factor in factors.items():
        out[name] = (out[name] * factor).astype(out[name].dtype)
    return out
```

```python
from contextlib import ExitStack

import concourse.bass as bass
from concourse import mybir
import numpy as np

F32 = mybir.dt.float32
BF16 = mybir.dt.bfloat16
I32 = mybir.dt.int32
ALU = mybir.AluOpType
ACT = mybir.ActivationFunctionType
AX = mybir.AxisListType

P = 128
B, T = 2, 1024
NT = T // P
NTILE = B * NT
RH, RD, RV = 8, 64, 128
AH, AD = 16, 8
HG = 4
NG = AH // HG
VW = 32
KV = 64
NE, HID = 4, 512
EM = HID // P
PARTS = 3
SROWS = PARTS * PARTS * AD
MROWS = SROWS + PARTS
RSQRT_SEED = float(0x5F3759DF)
MASKED = -1e30
TWO_ONES = float(np.array([0x3F803F80], np.uint32).view(np.float32)[0])
NEG = -1e9
QSCALE = AD ** -0.5


def constants():
    f = np.float32
    c = {}
    c["c_ident"] = np.eye(P, dtype=f)
    t = np.arange(T, dtype=f)
    inv = (1.0 / np.power(f(10000.0), np.arange(0, RD, 2, dtype=f) / f(RD))).astype(f)
    ang = (t[:, None] * inv[None, :]).astype(f)
    by_tile = lambda a: np.ascontiguousarray(a.reshape(NT, P, -1).transpose(1, 0, 2))
    c["c_rcos"] = by_tile(np.cos(ang).astype(f))
    c["c_rsin"] = by_tile(np.sin(ang).astype(f))
    gamma = 1.0 - np.exp2(-5.0 - np.arange(RH, dtype=np.float64))
    i = np.arange(P, dtype=np.float64)
    slots = [2 * (s % 4) + s // 4 for s in range(RH)]
    c["c_gq"] = (gamma[None, :] ** (i[:, None] + 1) * RD ** -0.5).astype(f)
    c["c_gk"] = (gamma[None, :] ** (P - 1 - i[:, None])).astype(f)
    dm = np.zeros((P, RH, P))
    for s, h in enumerate(slots):
        dm[:, s, :] = (gamma[h] ** -(i[:, None] + 1)) * (i[None, :] >= i[:, None])
    c["c_decay"] = dm.astype(f)
    gc = np.zeros((P, 4, P))
    for h in range(RH):
        gc[(h % 2) * RD:(h % 2 + 1) * RD, h // 2, :] = gamma[h] ** P
    c["c_gchunk"] = gc.astype(f)
    half = AD // 2
    inv = (1.0 / np.power(f(10000.0), np.arange(half, dtype=f) / f(half))).astype(f)
    ang = (t[:, None] * inv[None, :]).astype(f)
    cos = np.cos(ang).astype(f).T
    sin = np.sin(ang).astype(f).T
    cos8 = np.concatenate([cos, cos])
    sin8 = np.concatenate([-sin, sin])
    c["c_kcos"] = np.tile(cos8, (AH, 1)).astype(f)
    c["c_ksin"] = np.tile(sin8, (AH, 1)).astype(f)
    m = np.zeros((P, 4, P), dtype=f)
    m[:, 0] = np.where(i[None, :] > i[:, None], MASKED, 0)
    m[:, 1] = np.where(i[:, None] > i[None, :], MASKED, 0)
    m[0, 2, P - 1] = NEG
    m[P - 1, 3, 0] = NEG
    c["c_mask"] = m
    return c


def swap_halves(w):
    return w.reshape(AH, 2, AD // 2, -1)[:, ::-1].reshape(AH * AD, -1)


def layout(x):
    a = {k: np.asarray(v) for k, v in x.items()}
    slots = [2 * (s % 4) + s // 4 for s in range(RH)]
    c = np.ascontiguousarray
    d = dict(constants())
    d["x"] = a["L0_attn_x"].reshape(B * T, P)
    d["r_wqk"] = c(np.concatenate([a["L0_attn_Wq"], a["L0_attn_Wk"]]).T)
    byslot = lambda w: w.reshape(RH, RV, -1)[slots]
    d["r_wv"] = c(byslot(a["L0_attn_Wv"]).reshape(RH * RV, P).T)
    d["r_wg"] = c(byslot(a["L0_attn_Wg"]).reshape(RH * RV, P).T)
    d["r_wo"] = c(byslot(c(a["L0_attn_Wo"].T)).transpose(1, 0, 2))
    gn = np.stack([a["L0_attn_gn_weight"], a["L0_attn_gn_bias"]])
    d["r_gn"] = c(gn.reshape(2, RH, RV)[:, slots].transpose(2, 0, 1))
    n1, n2 = a["L0_ffn_norm1_w"], a["L0_ffn_norm2_w"]
    wq, wuk = a["L0_ffn_Wq"], a["L0_ffn_Wuk"]
    d["k_wq"] = c(np.stack([wq.T, swap_halves(wq).T], axis=1))
    d["k_wdkv"] = c(a["L0_ffn_Wdkv"].T)
    d["k_wuk"] = c(np.stack([wuk.T, swap_halves(wuk).T], axis=1))
    d["k_wuv"] = c(a["L0_ffn_Wuv"].T)
    d["k_wo"] = c(a["L0_ffn_Wo"].T)
    d["k_norm"] = c(np.stack([n1, n2], axis=1))
    d["k_ln"] = c(np.stack([a["L0_ffn_ln_g"], a["L0_ffn_ln_b"]], axis=1))
    d["e_gate"] = c(a["L0_ffn_gate_w"].T)
    d["e_gateb"] = a["L0_ffn_gate_b"].reshape(1, NE)
    d["e_w1"] = c(a["L0_ffn_W1"].reshape(NE * HID, P).T)
    d["e_b1"] = c(a["L0_ffn_b1"].reshape(NE * EM, P).T)
    w2 = a["L0_ffn_W2"].reshape(NE, P, EM, P)
    d["e_w2"] = c(w2.transpose(3, 0, 2, 1).reshape(P, NE * EM, P))
    d["e_b2"] = a["L0_ffn_b2"].reshape(1, NE * P)
    d["a_wqkv"] = c(np.stack([a["L1_attn_Wq"].T, a["L1_attn_Wk"].T, a["L1_attn_Wv"].T], axis=1))
    d["a_bqk"] = c(np.stack([a["L1_attn_bq"], a["L1_attn_bk"]], axis=1))
    d["a_bv"] = a["L1_attn_bv"].reshape(1, P)
    d["a_wo"] = c(a["L1_attn_Wo"].T)
    d["t_w"] = c(a["L1_ffn_weight"].T)
    return {k: np.ascontiguousarray(v) for k, v in d.items()}


class Arena:

    def __init__(self, tensor, words):
        self.tensor, self.words, self.at, self.most = tensor, words, 0, 0

    def tile(self, *shape, dtype=F32, rows=P):
        n = int(np.prod(shape))
        words = n if dtype != BF16 else (n + 1) // 2
        a = self.tensor[0:rows, self.at:self.at + words]
        self.at += words
        self.most = max(self.most, self.at)
        assert self.at <= self.words, (self.at, self.words)
        if dtype != F32:
            a = a.bitcast(dtype)
        if len(shape) == 1:
            return a
        names = " ".join("abcde"[:len(shape)])
        sizes = {k: s for k, s in zip("abcde", shape)}
        return a.rearrange(f"p ({names}) -> p {names}", **sizes)


def build(nc, d, out, phases=5):
    ctx = ExitStack()
    with ctx:
        words = 52000
        A = Arena(ctx.enter_context(nc.sbuf_tensor("arena", [P, words], F32)), words)
        PS = ctx.enter_context(nc.psum_tensor("banks", [P, 8, 512], F32))

        def sem(name):
            return ctx.enter_context(nc.semaphore(name))

        def bank(b):
            return PS[:, b, :]

        def pair(q):
            return PS[:, 2 * q:2 * q + 2, :].rearrange("p b n -> p (b n)")

        scratch = nc.dram_tensor("parts_dram", [2, B, 2, PARTS, P, T], BF16, kind="Internal").ap()

        X = A.tile(NTILE, P)
        ident = A.tile(P)
        identb = A.tile(P, dtype=BF16)
        masks = A.tile(4, P, dtype=BF16)
        stats = A.tile(NTILE, 6)
        mv = A.tile(NTILE, 2)
        newt = A.tile(2, 16)
        rstd = A.tile(16)
        epst = A.tile(2)
        sq = A.tile(P)
        U = A.tile(NTILE, P)
        common_end = A.at

        wqk, wv, wg = A.tile(2 * RH * RD), A.tile(RH * RV), A.tile(RH * RV)
        wo = A.tile(RH, P)
        gn = A.tile(2, RH)
        decay, gchunk = A.tile(RH * P), A.tile(4 * P)
        rcos, rsin = A.tile(NT, RD // 2), A.tile(NT, RD // 2)
        gq, gk = A.tile(RH), A.tile(RH)
        XT = A.tile(NTILE, P)
        rc, rs = A.tile(2 * RH * RD), A.tile(2 * RH * RD)
        rot = A.tile(2 * RH * RD)
        qd = [A.tile(RH * RD) for _ in range(2)]
        kr = [A.tile(RH * RD) for _ in range(2)]
        kd = [A.tile(RH * RD) for _ in range(2)]
        qkT = A.tile(8, P)
        vv = [A.tile(RH, P) for _ in range(2)]
        sm = A.tile(RH, P)
        state = [A.tile(4 * P) for _ in range(2)]
        stdec = A.tile(4 * P)
        oc = [A.tile(RH, P) for _ in range(2)]
        osum, gvar, grs, gnt = A.tile(RH), A.tile(RH), A.tile(RH), A.tile(2, RH)
        on = A.tile(RH, P)
        sig = A.tile(RH, P)
        ga = A.tile(RH, P)
        uu = A.tile(RH, P)
        maskf = A.tile(4, P)
        A.at = common_end

        phase_end = sem("phase_end")
        load = {k: sem("load_" + k) for k in ("x", "qk", "rest", "gv", "wo", "mask")}
        dve_step, pool_step, act_step = sem("dve_step"), sem("pool_step"), sem("act_step")
        xT_done, xT_copied = sem("xT_done"), sem("xT_copied")
        qk_done, rot_muls, rot_ready = sem("qk_done"), sem("rot_muls"), sem("rot_ready")
        v_done, v_copied = sem("v_done"), sem("v_copied")
        qkT_done, qkT_copied = sem("qkT_done"), sem("qkT_copied")
        sc_done, sc_masked = sem("sc_done"), sem("sc_masked")
        delta_done, state_dec, state_ready = sem("delta_done"), sem("state_dec"), sem("state_ready")
        o_done, o_centred, o_squared = sem("o_done"), sem("o_centred"), sem("o_squared")
        o_rstd, o_normed = sem("o_rstd"), sem("o_normed")
        g_done, g_silu = sem("g_done"), sem("g_silu")
        onT_done, onT_affine, u_ready = sem("onT_done"), sem("onT_affine"), sem("u_ready")
        y_done, y_added = sem("y_done"), sem("y_added")
        ln_rstd, ln_done = sem("ln_rstd"), sem("ln_done")
        stored = sem("stored")

        counts = {}

        def chain(eng, s):
            def link(ins):
                counts[s.name] = counts.get(s.name, 0) + 1
                ins.then_inc(s, 1)
                eng.wait_ge(s, counts[s.name])
            return link

        def barrier(eng, n):
            eng.drain().then_inc(phase_end, 1)
            eng.wait_ge(phase_end, 5 * n)

        def rsqrt(eng, link, y, v, tmp):
            link(eng.tensor_scalar(y.bitcast(I32), v.bitcast(I32), -0.5, RSQRT_SEED, ALU.mult, ALU.add))
            for k in range(3):
                link(eng.tensor_tensor(tmp, y, y, ALU.mult))
                link(eng.tensor_tensor(tmp, tmp, v, ALU.mult))
                link(eng.tensor_scalar(tmp, tmp, -0.5, 1.5, ALU.mult, ALU.add))
                ins = eng.tensor_tensor(y, y, tmp, ALU.mult)
                if k < 2:
                    link(ins)
            return ins

        def heads(a, n=RH):
            return a.rearrange("p (h v) -> p h v", h=n)

        def spread(a, n, w):
            return a.unsqueeze(2).to_broadcast([P, n, w])

        def layer_norm(dve, link, eps):
            v_ = nc.vector
            link(v_.tensor_scalar(rstd, mv[:, :, 1], eps, None, ALU.add))
            link(rsqrt_of(v_, link))
            for i in range(NTILE):
                ins = v_.tensor_scalar(X[:, i, :], X[:, i, :], mv[:, i, 0:1], newt[:, 1, i:i + 1],
                                       ALU.subtract, ALU.mult)
            link(ins)

        def rsqrt_of(v_, link):
            return rsqrt(v_, link, newt[:, 1, :], rstd, newt[:, 0, :])

        block = ctx.enter_context(nc.Block())

        @block.sync
        def _(sp):
            sp.dma_start(ident, d["c_ident"]).then_inc(load["x"], 16)
            sp.dma_start(X, d["x"].rearrange("(n p) d -> p n d", p=P)).then_inc(load["x"], 16)
            sp.dma_start(wqk, d["r_wqk"]).then_inc(load["qk"], 16)
            sp.dma_start(rcos, d["c_rcos"]).then_inc(load["qk"], 16)
            sp.dma_start(rsin, d["c_rsin"]).then_inc(load["qk"], 16)
            sp.dma_start(gq, d["c_gq"]).then_inc(load["qk"], 16)
            sp.dma_start(gk, d["c_gk"]).then_inc(load["qk"], 16)
            sp.dma_start(wv, d["r_wv"]).then_inc(load["gv"], 16)
            sp.dma_start(wg, d["r_wg"]).then_inc(load["gv"], 16)
            sp.dma_start(decay, d["c_decay"].rearrange("p s t -> p (s t)")).then_inc(load["rest"], 16)
            sp.dma_start(gchunk, d["c_gchunk"].rearrange("p s t -> p (s t)")).then_inc(load["rest"], 16)
            sp.dma_start(wo, d["r_wo"]).then_inc(load["wo"], 16)
            sp.dma_start(gn, d["r_gn"]).then_inc(load["wo"], 16)
            sp.dma_start(maskf, d["c_mask"]).then_inc(load["mask"], 16)
            barrier(sp, 1)

        def ready(e, s, n):
            if n >= 1:
                e.wait_ge(s, n)

        @block.tensor
        def _(pe):
            pe.wait_ge(load["x"], 32)
            for q in range(4):
                for k in range(4):
                    i = 4 * q + k
                    ins = nc.tensor.transpose(bank(q)[:, k * P:(k + 1) * P], X[:, i, :], ident)
                ins.then_inc(xT_done, 1)
            pe.wait_ge(load["qk"], 80)
            for n in range(NTILE + 3):
                if n < NTILE:
                    ready(pe, xT_copied, 4 if n == 0 else 0)
                    ready(pe, rot_muls, n)
                    ready(pe, sc_masked, n - 1)
                    for c in range(2):
                        ins = nc.tensor.matmul(bank(c), XT[:, n, :], wqk[:, c * 512:(c + 1) * 512],
                                               start=True, stop=True)
                    ins.then_inc(qk_done, 1)
                i = n - 1
                if 0 <= i < NTILE:
                    pe.wait_ge(rot_ready, i + 1)
                    ready(pe, y_added, i - 2)
                    ready(pe, state_ready, i)
                    for p4 in range(4):
                        nc.tensor.transpose(bank(6)[:, p4 * P:(p4 + 1) * P], qd[i % 2][:, p4 * P:(p4 + 1) * P], ident)
                    for p4 in range(4):
                        ins = nc.tensor.transpose(bank(7)[:, p4 * P:(p4 + 1) * P], kr[i % 2][:, p4 * P:(p4 + 1) * P], ident)
                    ins.then_inc(qkT_done, 1)
                if n < NTILE:
                    if n == 0:
                        pe.wait_ge(load["gv"], 32)
                    ready(pe, v_copied, n)
                    ready(pe, o_centred, n - 1)
                    for c in range(2):
                        ins = nc.tensor.matmul(bank(2 + c), XT[:, n, :], wv[:, c * 512:(c + 1) * 512],
                                               start=True, stop=True)
                    ins.then_inc(v_done, 1)
                if 0 <= i < NTILE:
                    first = i % NT == 0
                    pe.wait_ge(qkT_copied, i + 1)
                    pe.wait_ge(rot_muls, min(n, NTILE - 1) + 1)
                    for par in range(2):
                        rows = slice(par * RD, (par + 1) * RD)
                        for p4 in range(4):
                            ins = nc.tensor.matmul(bank(par)[:, p4 * P:(p4 + 1) * P], qkT[rows, 4 + p4, :],
                                                   qkT[rows, p4, :], start=True, stop=True)
                    ins.then_inc(sc_done, 1)
                    if i % NT < NT - 1:
                        for par in range(2):
                            rows = slice(par * RD, (par + 1) * RD)
                            for p4 in range(4):
                                ins = nc.tensor.matmul(
                                    PS[rows, 6, p4 * P:(p4 + 1) * P],
                                    kd[i % 2][:, (2 * p4 + par) * RD:(2 * p4 + par + 1) * RD],
                                    vv[i % 2][:, 4 * par + p4, :], start=True, stop=True)
                        ins.then_inc(delta_done, 1)
                    else:
                        ins = nc.tensor.matmul(bank(6)[:, 0:P], ident, ident, start=True, stop=True)
                        ins.then_inc(delta_done, 1)
                    pe.wait_ge(v_copied, min(n, NTILE - 1) + 1)
                    pe.wait_ge(sc_masked, i + 1)
                    ready(pe, state_ready, i)
                    for par in range(2):
                        rows = slice(par * RD, (par + 1) * RD)
                        for p4 in range(4):
                            s = 4 * par + p4
                            ins = nc.tensor.matmul(bank(2 + par)[:, p4 * P:(p4 + 1) * P], sm[:, s, :],
                                                   vv[i % 2][:, s, :], start=True, stop=first)
                            if not first:
                                ins = nc.tensor.matmul(bank(2 + par)[:, p4 * P:(p4 + 1) * P], qkT[rows, p4, :],
                                                       state[(i - 1) % 2][rows, p4 * P:(p4 + 1) * P],
                                                       start=False, stop=True)
                    ins.then_inc(o_done, 1)
                i = n - 2
                if 0 <= i < NTILE:
                    ready(pe, onT_affine, i)
                    for s in range(RH):
                        ins = nc.tensor.matmul(bank(4 + s // 4)[:, (s % 4) * P:(s % 4 + 1) * P],
                                               wg[:, s * P:(s + 1) * P], XT[:, i, :], start=True, stop=True)
                    ins.then_inc(g_done, 1)
                    pe.wait_ge(g_silu, i + 1)
                    pe.wait_ge(o_normed, i + 1)
                    for s in range(RH):
                        ins = nc.tensor.transpose(bank(4 + s // 4)[:, (s % 4) * P:(s % 4 + 1) * P], on[:, s, :], ident)
                    ins.then_inc(onT_done, 1)
                i = n - 3
                if 0 <= i < NTILE:
                    if i == 0:
                        pe.wait_ge(load["wo"], 32)
                    pe.wait_ge(u_ready, i + 1)
                    ready(pe, y_added, i)
                    pe.wait_ge(qkT_copied, min(n, NTILE))
                    for s in range(RH):
                        ins = nc.tensor.matmul(bank(7)[:, 0:P], uu[:, s, :], wo[:, s, :],
                                               start=(s == 0), stop=(s == RH - 1))
                    ins.then_inc(y_done, 1)
            barrier(pe, 1)

        @block.vector
        def _(dve):
            v_ = nc.vector
            link = chain(dve, dve_step)
            dve.wait_ge(load["qk"], 80)
            for n in range(NTILE + 3):
                if n < NTILE:
                    dve.wait_ge(qk_done, n + 1)
                    ready(dve, rot_ready, n)
                    c = n % NT
                    qk3 = pair(0).rearrange("p (g e) -> p g e", e=RD // 2)
                    qk4 = pair(0).rearrange("p (h z e) -> p h z e", h=2 * RH, z=2)
                    rs4 = rs.rearrange("p (h z e) -> p h z e", h=2 * RH, z=2)
                    cosb = rcos[:, c:c + 1, :].to_broadcast([P, 4 * RH, RD // 2])
                    sinb = rsin[:, c:c + 1, :].to_broadcast([P, 2 * RH, RD // 2])
                    v_.tensor_tensor(rc.rearrange("p (g e) -> p g e", e=RD // 2), qk3, cosb, ALU.mult)
                    v_.scalar_tensor_tensor(out=rs4[:, :, 0, :], in0=qk4[:, :, 1, :], scalar=-1.0, in1=sinb,
                                            op0=ALU.mult, op1=ALU.mult)
                    v_.tensor_tensor(rs4[:, :, 1, :], qk4[:, :, 0, :], sinb, ALU.mult).then_inc(rot_muls, 1)
                i = n - 2
                if 0 <= i < NTILE:
                    dve.wait_ge(o_rstd, i + 1)
                    ready(dve, onT_done, i)
                    v_.tensor_tensor(on, oc[i % 2], spread(grs, RH, P), ALU.mult).then_inc(o_normed, 1)
                i = n - 1
                if 0 <= i < NTILE:
                    if i == 0:
                        dve.wait_ge(load["rest"], 32)
                    dve.wait_ge(sc_done, i + 1)
                    ready(dve, o_done, i)
                    v_.tensor_tensor(sm.rearrange("p s t -> p (s t)"), pair(0), decay, ALU.mult).then_inc(sc_masked, 1)
                    dve.wait_ge(delta_done, i + 1)
                    if i % NT == 0:
                        ready(dve, o_done, i)
                        v_.tensor_copy(state[i % 2], bank(6)).then_inc(state_ready, 1)
                    elif i % NT < NT - 1:
                        dve.wait_ge(state_dec, i + 1)
                        v_.tensor_tensor(state[i % 2], stdec, bank(6), ALU.add).then_inc(state_ready, 1)
                    else:
                        v_.memset(epst[:, 0:1], 0.0).then_inc(state_ready, 1)
                    dve.wait_ge(o_done, i + 1)
                    o3 = heads(pair(1))
                    link(v_.tensor_reduce(osum, o3, AX.X, ALU.add))
                    link(v_.tensor_scalar(osum, osum, 1.0 / RV, None, ALU.mult))
                    ready(dve, o_squared, i - 1)
                    v_.tensor_tensor(oc[i % 2], o3, spread(osum, RH, P), ALU.subtract).then_inc(o_centred, 1)
                i = n - 2
                if 0 <= i < NTILE:
                    dve.wait_ge(onT_affine, i + 1)
                    ready(dve, y_done, i)
                    v_.tensor_tensor(uu, ga, sig, ALU.mult).then_inc(u_ready, 1)
                i = n - 3
                if 0 <= i < NTILE:
                    dve.wait_ge(y_done, i + 1)
                    v_.tensor_tensor(X[:, i, :], bank(7)[:, 0:P], X[:, i, :], ALU.add).then_inc(y_added, 1)
                    dve.wait_ge(y_added, i + 1)
                    link(v_.bn_stats(stats[:, i, :], X[:, i, :]))
                    link(v_.bn_aggr(mv[:, i, :], stats[:, i, :]))
            layer_norm(dve, link, 1e-5)
            barrier(dve, 1)

        @block.gpsimd
        def _(pool):
            g_ = nc.gpsimd
            link = chain(pool, pool_step)
            pool.wait_ge(load["qk"], 80)
            for n in range(NTILE + 1):
                if n < NTILE:
                    pool.wait_ge(rot_muls, n + 1)
                    link(g_.tensor_tensor(rot, rc, rs, ALU.add))
                    ready(pool, qkT_done, n - 1)
                    g_.tensor_tensor(heads(qd[n % 2]), heads(rot[:, 0:512]), spread(gq, RH, RD), ALU.mult)
                    g_.tensor_scalar(kr[n % 2], rot[:, 512:1024], 1.0, None, ALU.mult)
                    ready(pool, delta_done, n - 1)
                    g_.tensor_tensor(heads(kd[n % 2]), heads(rot[:, 512:1024]), spread(gk, RH, RD),
                                     ALU.mult).then_inc(rot_ready, 1)
                i = n - 1
                if 0 <= i < NTILE:
                    if i == 0:
                        pool.wait_ge(load["rest"], 32)
                    if i % NT:
                        ready(pool, state_ready, i)
                        g_.tensor_tensor(stdec, state[(i - 1) % 2], gchunk, ALU.mult).then_inc(state_dec, 1)
                    else:
                        pool.wait_ge(rot_ready, n)
                        g_.memset(gnt[:, 1, 0:1], 0.0).then_inc(state_dec, 1)
                    pool.wait_ge(o_squared, i + 1)
                    link(g_.tensor_scalar(gvar, gvar, 1.0 / RV, 1e-5, ALU.mult, ALU.add))
                    ready(pool, o_normed, i)
                    rsqrt(g_, link, grs, gvar, gnt[:, 0, :]).then_inc(o_rstd, 1)
            pool.wait_ge(load["mask"], 16)
            g_.tensor_copy(masks, maskf)
            g_.tensor_copy(identb, ident)
            barrier(pool, 1)

        @block.scalar
        def _(act):
            s_ = nc.scalar
            link = chain(act, act_step)
            for q in range(4):
                act.wait_ge(xT_done, q + 1)
                s_.activation(XT[:, 4 * q:4 * q + 4, :], bank(q).rearrange("p (k t) -> p k t", k=4),
                              ACT.Copy).then_inc(xT_copied, 1)
            act.wait_ge(load["wo"], 32)
            for n in range(NTILE + 2):
                i = n - 1
                if 0 <= i < NTILE:
                    act.wait_ge(qkT_done, i + 1)
                    ready(act, o_done, i)
                    s_.activation(qkT.rearrange("p s t -> p (s t)"), pair(3), ACT.Copy).then_inc(qkT_copied, 1)
                if n < NTILE:
                    act.wait_ge(v_done, n + 1)
                    ready(act, o_done, n - 1)
                    ready(act, delta_done, n - 1)
                    s_.activation(vv[n % 2].rearrange("p s t -> p (s t)"), pair(1), ACT.Copy).then_inc(v_copied, 1)
                i = n - 2
                if 0 <= i < NTILE:
                    act.wait_ge(g_done, i + 1)
                    ready(act, u_ready, i)
                    s_.activation(sig.rearrange("p s t -> p (s t)"), pair(2), ACT.Silu).then_inc(g_silu, 1)
                i = n - 1
                if 0 <= i < NTILE:
                    act.wait_ge(o_centred, i + 1)
                    ready(act, o_rstd, i)
                    for s in range(RH):
                        ins = s_.activation(sq, oc[i % 2][:, s, :], ACT.Square, accum_out=gvar[:, s:s + 1])
                        if s < RH - 1:
                            link(ins)
                    ins.then_inc(o_squared, 1)
                i = n - 2
                if 0 <= i < NTILE:
                    act.wait_ge(onT_done, i + 1)
                    for s in range(RH):
                        ins = s_.activation(ga[:, s, :], bank(4 + s // 4)[:, (s % 4) * P:(s % 4 + 1) * P],
                                            ACT.Identity, scale=gn[:, 0, s:s + 1], bias=gn[:, 1, s:s + 1])
                    ins.then_inc(onT_affine, 1)
            barrier(act, 1)

        Qs = A.tile(NG, HG, T, dtype=BF16)
        Ks = A.tile(NG, HG, T, dtype=BF16)
        Pr = [A.tile(HG, T) for _ in range(2)]
        V = A.tile(B, NT, AH, VW)
        mx = [A.tile(2, HG * NT) for _ in range(2)]
        nm1 = A.tile(P, rows=HG * NT)
        nmp = [A.tile(PARTS, P, dtype=BF16, rows=HG * NT) for _ in range(2)]
        osb = A.tile(2, 512)
        rden = A.tile(NT // 2, HG)
        On = A.tile(NT, P)
        OT = A.tile(T)
        proj = {"ss": A.tile(NT), "rr": A.tile(NT), "tmp": A.tile(NT)}
        hT, rot1, rot2, qk, rem = (A.tile(T) for _ in range(5))
        parts = A.tile(PARTS, T, dtype=BF16)
        latT = A.tile(T, rows=KV)
        wq2, wuk2 = A.tile(2, P), A.tile(2, P, rows=KV)
        wdkv, wuv = A.tile(KV), A.tile(P, rows=KV)
        wout = A.tile(P)
        norms, lnp = A.tile(2), A.tile(2, rows=KV)
        lst, lmv = A.tile(NT, 6), A.tile(NT, 2)
        latent_at = A.at
        tab_cos, tab_sin = A.tile(T), A.tile(T)
        A.at = latent_at
        wqkv, bqk, bv = A.tile(3, P), A.tile(2), A.tile(P)

        load2, load4 = sem("load_latent"), sem("load_biased")
        pj = {e: sem("proj_" + e) for e in ("pe", "act", "dve", "pool")}
        to_dram = sem("parts_stored")
        stack = [sem(f"stack_loaded_{k}") for k in range(NG)]
        mrow = [sem(f"max_rows_loaded_{k}") for k in range(2)]
        ones_set = sem("ones_set")
        ring_full, ring_used = sem("ring_full"), sem("ring_used")
        score_done, exp_done, av_done = sem("score_done"), sem("exp_done"), sem("av_done")
        o_copied, mx_ready, m_split = sem("o_copied"), sem("mx_ready"), sem("m_split")
        LEAD = 11

        def order():
            units = B * NG * NT
            seq = [("A", u) for u in range(LEAD)]
            seq.insert(NT + 1, ("M", 0))
            for s in range(units + NT):
                n, j = divmod(s, NT)
                if s < units:
                    seq.append(("S", s))
                u = s + LEAD
                if u < units:
                    seq.append(("A", u))
                if u < units + NT and u % NT == 0 and 1 < u // NT <= B * NG:
                    seq.append(("M", u // NT - 1))
                if 0 < s <= units:
                    seq.append(("V", s - 1))
                if j == 1 and n:
                    seq += [("O", (n - 1, 0)), ("O", (n - 1, 1))]
                if j == 3 and n and n % NG == 0:
                    seq += [("N", (n // NG - 1, 0)), ("N", (n // NG - 1, 1))]
                if j == 5 and n and n % NG == 0:
                    seq += [("Y", (n // NG - 1, 0)), ("Y", (n // NG - 1, 1))]
            return seq

        def ring_places(layer):
            place, r = {}, 0
            for kind, k in order():
                if kind == "A":
                    for h in range(HG):
                        for c in range(chunks(layer, k % NT)):
                            place[kind, k, h, c] = r
                            r += 1
                elif kind in "MONY":
                    place[kind, k] = r
                    r += 1
            return place, r

        def chunks(layer, qt):
            return 2 if layer or qt >= 4 else 1

        places = [ring_places(k) for k in range(2)]
        ring_base = [0, places[0][1]]
        UNITS = B * NG * NT

        def attention(layer):
            place = {k: v + ring_base[layer] for k, v in places[layer][0].items()}
            q0 = layer * UNITS * HG
            s0 = layer * UNITS
            n0 = layer * B * NG
            causal = layer == 0

            def qrange(kt, c):
                lo = max(kt * P, c * 512) if causal else c * 512
                return lo, (c + 1) * 512

            @block.sync
            def _(sp):
                for b in range(B):
                    for w in range(2):
                        sp.wait_ge(pj["dve"], at("dve", "part2", layer, 2 * b + w))
                        sp.dma_start(scratch[layer, b, w].rearrange("i p t -> p i t"), parts).then_inc(to_dram, 16)
                        sp.wait_ge(to_dram, 16 * (layer * 4 + 2 * b + w + 1))
                    for g in range(NG):
                        n = b * NG + g
                        if n0 + n >= NG:
                            sp.wait_ge(score_done, q0 + HG * NT * (n - NG + 1))
                        if n == 0:
                            sp.wait_ge(ones_set, layer + 1)
                        for i in range(PARTS):
                            for j in range(PARTS):
                                rows = slice((PARTS * i + j) * AD, (PARTS * i + j + 1) * AD)
                                for w, dst, part in ((0, Qs, i), (1, Ks, j)):
                                    src = scratch[layer, b, w, part].rearrange("(h d) t -> d h t", d=AD)
                                    sp.dma_start(dst[rows, g], src[:, g * HG:(g + 1) * HG, :]) \
                                      .then_inc(stack[g], 16)
                barrier(sp, 2 + 2 * layer)

            @block.gpsimd
            def _(pool):
                for n in range(B * NG):
                    pool.wait_ge(m_split, n0 + n + 1)
                    if n0 + n >= NG:
                        pool.wait_ge(score_done, q0 + HG * NT * (n - NG + 1))
                    for i in range(PARTS):
                        row = Qs[SROWS + i:SROWS + i + 1, n % NG].rearrange("o h (j q) -> o (h j) q", q=P)
                        nc.gpsimd.dma_start(row, nmp[n % 2][:, i, :]).then_inc(mrow[n % 2], 16)
                barrier(pool, 2 + 2 * layer)

            @block.tensor
            def _(pe):
                for e in ("dve", "act"):
                    pe.wait_ge(pj[e], at(e, stages[layer, e][-1], layer, 2 * (B - 1)))
                for kind, k in order():
                    if kind == "A":
                        n, qt = divmod(k, NT)
                        if qt == 0:
                            pe.wait_ge(stack[n % NG], 288 * ((n0 + n) // NG + 1))
                        for h in range(HG):
                            for c in range(chunks(layer, qt)):
                                r = place["A", k, h, c]
                                ready(pe, ring_used, r - 1)
                                end = min((c + 1) * 512, (qt + 1) * P) if causal else (c + 1) * 512
                                bk = bank(6 + r % 2)
                                diag = causal and end == (qt + 1) * P and end <= (c + 1) * 512 and qt // 4 == c
                                corner = not causal and (qt, c) in ((0, 1), (NT - 1, 0))
                                ins = nc.tensor.matmul(
                                    bk[:, 0:end - c * 512], Qs[0:SROWS, n % NG, h, qt * P:(qt + 1) * P],
                                    Ks[0:SROWS, n % NG, h, c * 512:end], start=True, stop=not (diag or corner))
                                if diag:
                                    o = qt * P - c * 512
                                    ins = nc.tensor.matmul(bk[:, o:o + P], identb, masks[:, 0, :],
                                                           start=False, stop=True)
                                if corner:
                                    o, m = (384, 2) if qt == 0 else (0, 3)
                                    ins = nc.tensor.matmul(bk[:, o:o + P], identb, masks[:, m, :],
                                                           start=False, stop=True)
                                ins.then_inc(ring_full, 1)
                    elif kind == "M":
                        r = place[kind, k]
                        pe.wait_ge(mx_ready, n0 + k + 1)
                        ready(pe, ring_used, r - 1)
                        nc.tensor.transpose(PS[0:HG * NT, 6 + r % 2, 0:P], mx[k % 2][:, 0, :], ident) \
                          .then_inc(ring_full, 1)
                    elif kind == "S":
                        n, kt = divmod(k, NT)
                        if kt == 0:
                            pe.wait_ge(mrow[n % 2], 48 * ((n0 + n) // 2 + 1))
                        for h in range(HG):
                            q = HG * k + h
                            ready(pe, exp_done, q0 + q - 1)
                            for c in range(2):
                                lo, hi = qrange(kt, c)
                                if lo >= hi:
                                    continue
                                diag = causal and lo == kt * P and kt // 4 == c
                                corner = not causal and (kt, c) in ((0, 1), (NT - 1, 0))
                                ins = nc.tensor.matmul(
                                    pair(q % 2)[:, lo:hi], Ks[0:MROWS, n % NG, h, kt * P:(kt + 1) * P],
                                    Qs[0:MROWS, n % NG, h, lo:hi], start=True, stop=not (diag or corner))
                                if diag:
                                    ins = nc.tensor.matmul(pair(q % 2)[:, lo:lo + P], identb, masks[:, 1, :],
                                                           start=False, stop=True)
                                if corner:
                                    o, m = (T - P, 2) if kt == 0 else (0, 3)
                                    ins = nc.tensor.matmul(pair(q % 2)[:, o:o + P], identb, masks[:, m, :],
                                                           start=False, stop=True)
                            ins.then_inc(score_done, 1)
                    elif kind == "V":
                        n, kt = divmod(k, NT)
                        b, g = divmod(n, NG)
                        pe.wait_ge(exp_done, q0 + HG * (k + 1))
                        if kt == 0:
                            ready(pe, o_copied, n0 + n)
                        if kt == 0 and g == 0:
                            pe.wait_ge(pj["dve"], at("dve", "v", layer, 2 * b))
                        for c in range(2):
                            lo, hi = qrange(kt, c)
                            if lo >= hi:
                                continue
                            last = kt == (4 * c + 3 if causal else NT - 1)
                            for h in range(HG):
                                ins = nc.tensor.matmul(
                                    PS[h * VW:(h + 1) * VW, 4 + c, lo - c * 512:hi - c * 512],
                                    V[:, b, kt, HG * g + h, :], Pr[k % 2][:, h, lo:hi],
                                    start=(kt == 0), stop=last)
                        ins.then_inc(av_done, 1)
                    elif kind == "O":
                        n, c = k
                        r = place[kind, k]
                        pe.wait_ge(o_copied, n0 + n + 1)
                        ready(pe, ring_used, r - 1)
                        for t in range(4):
                            ins = nc.tensor.transpose(bank(6 + r % 2)[:, t * P:(t + 1) * P],
                                                      osb[:, c, t * P:(t + 1) * P], ident)
                        ins.then_inc(ring_full, 1)
                    elif kind == "N":
                        b, c = k
                        r = place[kind, k]
                        pe.wait_ge(ring_used, max(r - 1, place["O", (NG * (b + 1) - 1, 1)] + 1))
                        for t in range(4):
                            ins = nc.tensor.transpose(bank(6 + r % 2)[:, t * P:(t + 1) * P], On[:, 4 * c + t, :], ident)
                        ins.then_inc(ring_full, 1)
                    elif kind == "Y":
                        b, c = k
                        r = place[kind, k]
                        pe.wait_ge(ring_used, max(r - 1, place["N", k] + 1))
                        for t in range(4):
                            ins = nc.tensor.matmul(bank(6 + r % 2)[:, t * P:(t + 1) * P],
                                                   OT[:, c * 512 + t * P:c * 512 + (t + 1) * P], wout,
                                                   start=True, stop=True)
                        ins.then_inc(ring_full, 1)
                barrier(pe, 2 + 2 * layer)

            @block.scalar
            def _(act):
                for kind, k in order():
                    if kind == "S":
                        kt = k % NT
                        lo = kt * P if causal else 0
                        ready(act, av_done, s0 + k - 1)
                        for h in range(HG):
                            q = HG * k + h
                            act.wait_ge(score_done, q0 + q + 1)
                            nc.scalar.activation(Pr[k % 2][:, h, lo:T], pair(q % 2)[:, lo:T],
                                                 ACT.Exp).then_inc(exp_done, 1)
                    elif kind == "V" and k % NT == NT - 1:
                        n = k // NT
                        act.wait_ge(av_done, s0 + k + 1)
                        if n:
                            act.wait_ge(ring_full, place["O", (n - 1, 1)] + 1)
                        nc.scalar.activation(osb.rearrange("p c q -> p (c q)"), pair(2), ACT.Copy) \
                          .then_inc(o_copied, 1)
                barrier(act, 2 + 2 * layer)

            @block.vector
            def _(dve):
                v_ = nc.vector
                link = chain(dve, dve_step)
                for kind, k in order():
                    if kind == "A":
                        n, qt = divmod(k, NT)
                        for h in range(HG):
                            for c in range(chunks(layer, qt)):
                                r = place["A", k, h, c]
                                end = min(512, (qt + 1) * P - c * 512) if causal else 512
                                dve.wait_ge(ring_full, r + 1)
                                v_.tensor_reduce(mx[n % 2][:, c, h * NT + qt:h * NT + qt + 1],
                                                 bank(6 + r % 2)[:, 0:end], AX.X, ALU.max).then_inc(ring_used, 1)
                        if qt == NT - 1:
                            dve.wait_ge(ring_used, r + 1)
                            both = [mx[n % 2][:, c, :].rearrange("p (h q) -> p h q", h=HG)[:, :, (4 if causal else 0):]
                                    for c in range(2)]
                            v_.tensor_tensor(both[0], both[0], both[1], ALU.max).then_inc(mx_ready, 1)
                    elif kind == "M":
                        r = place[kind, k]
                        dve.wait_ge(ring_full, r + 1)
                        ready(dve, mrow[k % 2], 48 * ((n0 + k) // 2))
                        row = PS[0:HG * NT, 6 + r % 2, 0:P]
                        part = [nmp[k % 2][:, i, :] for i in range(PARTS)]
                        link(v_.tensor_scalar(part[0], row, -1.0, None, ALU.mult))
                        v_.scalar_tensor_tensor(out=nm1, in0=row, scalar=-1.0, in1=part[0],
                                                op0=ALU.mult, op1=ALU.subtract).then_inc(ring_used, 1)
                        dve.wait_ge(ring_used, r + 1)
                        link(v_.tensor_copy(part[1], nm1))
                        v_.tensor_tensor(part[2], nm1, part[1], ALU.subtract).then_inc(m_split, 1)
                    elif kind == "O":
                        n, c = k
                        g = n % NG
                        r = place[kind, k]
                        dve.wait_ge(ring_full, r + 1)
                        o4 = bank(6 + r % 2).rearrange("p (t h e) -> p t h e", t=4, h=HG)
                        link(v_.reciprocal(rden, o4[:, :, :, AD]))
                        dst = On[:, 4 * c:4 * c + 4, HG * AD * g:HG * AD * (g + 1)]
                        v_.tensor_tensor(dst.rearrange("p t (h e) -> p t h e", h=HG), o4[:, :, :, 0:AD],
                                         rden.unsqueeze(3).to_broadcast([P, 4, HG, AD]),
                                         ALU.mult).then_inc(ring_used, 1)
                        dve.wait_ge(ring_used, r + 1)
                    elif kind == "N":
                        b, c = k
                        r = place[kind, k]
                        dve.wait_ge(ring_full, r + 1)
                        v_.tensor_copy(OT[:, c * 512:(c + 1) * 512], bank(6 + r % 2)).then_inc(ring_used, 1)
                    elif kind == "Y":
                        b, c = k
                        r = place[kind, k]
                        dve.wait_ge(ring_full, r + 1)
                        t = slice(b * NT + 4 * c, b * NT + 4 * c + 4)
                        y = bank(6 + r % 2).rearrange("p (t e) -> p t e", t=4)
                        v_.tensor_tensor((X if layer else U)[:, t, :], y, X[:, t, :], ALU.add).then_inc(ring_used, 1)
                        if layer:
                            dve.wait_ge(ring_used, r + 1)
                            for i in range(t.start, t.stop):
                                link(v_.bn_stats(stats[:, i, :], X[:, i, :]))
                                link(v_.bn_aggr(mv[:, i, :], stats[:, i, :]))
                if layer:
                    layer_norm(dve, link, 1e-5)
                barrier(dve, 2 + 2 * layer)

        stages = {
            (0, "pe"): ("hT", "q", "lat", "latT", "v", "k"),
            (0, "act"): ("square", "hT", "part0q", "part1q", "latT", "part0k", "part1k"),
            (0, "dve"): ("h", "q", "rem1q", "part2q", "lat", "v", "k", "rem1k", "part2k"),
            (0, "pool"): ("q", "k"),
            (1, "pe"): ("hT", "q", "k", "v"),
            (1, "act"): ("hT", "part0q", "part1q", "k", "part0k", "part1k"),
            (1, "dve"): ("q", "rem1q", "part2q", "rem1k", "part2k", "v"),
        }

        def at(engine, stage, layer, item):
            names = stages[layer, engine]
            if stage not in names:
                stage += "qk"[item % 2]
            before = B * len(stages[0, engine]) if layer else 0
            return before + item // 2 * len(names) + names.index(stage) + 1

        def split(act_or_dve, eng, what, layer, b, w):
            item = 2 * b + w
            if act_or_dve == "act":
                if w or b:
                    eng.wait_ge(to_dram, 16 * (4 * layer + item))
                if layer and w:
                    eng.wait_ge(pj["act"], at("act", "k", layer, 2 * b))
                elif layer:
                    eng.wait_ge(pj["dve"], at("dve", "q", layer, 2 * b))
                else:
                    eng.wait_ge(pj["pool"], at("pool", "qk"[w], layer, 2 * b))
                nc.scalar.activation(parts[:, 0, :], qk, ACT.Copy).then_inc(pj["act"], 1)
                eng.wait_ge(pj["dve"], at("dve", "rem1", layer, item))
                nc.scalar.activation(parts[:, 1, :], rem, ACT.Copy).then_inc(pj["act"], 1)
            else:
                eng.wait_ge(pj["act"], at("act", "part0", layer, item))
                nc.vector.tensor_tensor(rem, qk, parts[:, 0, :], ALU.subtract).then_inc(pj["dve"], 1)
                eng.wait_ge(pj["act"], at("act", "part1", layer, item))
                nc.vector.tensor_tensor(parts[:, 2, :], rem, parts[:, 1, :], ALU.subtract).then_inc(pj["dve"], 1)

        def set_ones(pool, layer):
            nc.gpsimd.memset(Ks[64:96].rearrange("p g h t -> p (g h t)").bitcast(F32), TWO_ONES) \
              .then_inc(ones_set, 1)
            pool.wait_ge(ones_set, layer + 1)

        def pad_values(v_, link):
            link(v_.memset(V[:, :, :, :, AD:AD + 1].rearrange("p b t h e -> p (b t h) e"), 1.0))
            link(v_.memset(V[:, :, :, :, AD + 1:VW].rearrange("p b t h e -> p (b t h) e"), 0.0))

        def latent_projections():
            @block.sync
            def _(sp):
                for t, name in ((tab_cos, "c_kcos"), (tab_sin, "c_ksin"), (wq2, "k_wq"), (wdkv, "k_wdkv"),
                                (wuk2, "k_wuk"), (wuv, "k_wuv"), (wout, "k_wo"), (norms, "k_norm"), (lnp, "k_ln")):
                    sp.dma_start(t, d[name]).then_inc(load2, 16)

            @block.gpsimd
            def _(pool):
                g_ = nc.gpsimd
                set_ones(pool, 0)
                for b in range(B):
                    for w in range(2):
                        pool.wait_ge(pj["dve"], at("dve", "qk"[w], 0, 2 * b))
                        if b or w:
                            pool.wait_ge(pj["dve"], at("dve", "rem1", 0, 2 * b + w - 1))
                        g_.tensor_tensor(qk, rot1, rot2, ALU.add).then_inc(pj["pool"], 1)

            @block.tensor
            def _(pe):
                pe.wait_ge(load2, 144)
                A_ = lambda e, st, b: at(e, st, 0, 2 * b)
                for b in range(B):
                    pe.wait_ge(pj["dve"], A_("dve", "h", b))
                    for t in range(NT):
                        ins = nc.tensor.transpose(pair(0)[:, t * P:(t + 1) * P], rem[:, t * P:(t + 1) * P], ident)
                    ins.then_inc(pj["pe"], 1)
                    pe.wait_ge(pj["act"], A_("act", "hT", b))
                    for z in range(2):
                        for c in range(2):
                            ins = nc.tensor.matmul(pair(1 + z)[:, c * 512:(c + 1) * 512], wq2[:, z, :],
                                                   hT[:, c * 512:(c + 1) * 512], start=True, stop=True)
                    ins.then_inc(pj["pe"], 1)
                    for t in range(NT):
                        ins = nc.tensor.matmul(bank(6)[:, t * KV:(t + 1) * KV], hT[:, t * P:(t + 1) * P], wdkv,
                                               start=True, stop=True)
                    ins.then_inc(pj["pe"], 1)
                    pe.wait_ge(pj["dve"], A_("dve", "lat", b))
                    for t in range(NT):
                        ins = nc.tensor.transpose(pair(0)[0:KV, t * P:(t + 1) * P], osb.rearrange("p c q -> p (c q)")[:, t * KV:(t + 1) * KV], ident)
                    ins.then_inc(pj["pe"], 1)
                    pe.wait_ge(pj["act"], A_("act", "latT", b))
                    for t in range(NT):
                        ins = nc.tensor.matmul(pair(3)[:, t * P:(t + 1) * P], latT[:, t * P:(t + 1) * P], wuv,
                                               start=True, stop=True)
                    ins.then_inc(pj["pe"], 1)
                    for z in range(2):
                        for c in range(2):
                            ins = nc.tensor.matmul(pair(1 + z)[:, c * 512:(c + 1) * 512], wuk2[:, z, :],
                                                   latT[:, c * 512:(c + 1) * 512], start=True, stop=True)
                    ins.then_inc(pj["pe"], 1)

            @block.scalar
            def _(act):
                s_ = nc.scalar
                link = chain(act, act_step)
                A_ = lambda e, st, b: at(e, st, 0, 2 * b)
                act.wait_ge(load2, 144)
                for b in range(B):
                    if b:
                        act.wait_ge(pj["dve"], A_("dve", "h", b - 1))
                    for t in range(NT):
                        ins = s_.activation(sq, X[:, b * NT + t, :], ACT.Square, accum_out=proj["ss"][:, t:t + 1])
                        if t < NT - 1:
                            link(ins)
                    ins.then_inc(pj["act"], 1)
                    act.wait_ge(pj["pe"], A_("pe", "hT", b))
                    if b:
                        act.wait_ge(pj["pe"], A_("pe", "lat", b - 1))
                    s_.activation(hT, pair(0), ACT.Copy, scale=norms[:, 0:1]).then_inc(pj["act"], 1)
                    split("act", act, "q", 0, b, 0)
                    act.wait_ge(pj["pe"], A_("pe", "latT", b))
                    s_.activation(latT, pair(0)[0:KV, :], ACT.Identity, scale=lnp[:, 0:1],
                                  bias=lnp[:, 1:2]).then_inc(pj["act"], 1)
                    split("act", act, "k", 0, b, 1)

            @block.vector
            def _(dve):
                v_ = nc.vector
                link = chain(dve, dve_step)
                A_ = lambda e, st, b: at(e, st, 0, 2 * b)
                dve.wait_ge(load2, 144)
                pad_values(v_, link)
                for b in range(B):
                    dve.wait_ge(pj["act"], A_("act", "square", b))
                    link(v_.tensor_scalar(proj["ss"], proj["ss"], 1.0 / P, 1e-6, ALU.mult, ALU.add))
                    link(rsqrt(v_, link, proj["rr"], proj["ss"], proj["tmp"]))
                    for t in range(NT):
                        ins = v_.tensor_scalar(rem[:, t * P:(t + 1) * P], X[:, b * NT + t, :],
                                               proj["rr"][:, t:t + 1], None, ALU.mult)
                    ins.then_inc(pj["dve"], 1)
                    for w in range(2):
                        if w:
                            dve.wait_ge(pj["pe"], A_("pe", "lat", b))
                            for t in range(NT):
                                link(v_.bn_stats(lst[:, t, :], bank(6)[:, t * KV:(t + 1) * KV]))
                            for t in range(NT):
                                ins = v_.bn_aggr(lmv[:, t, :], lst[:, t, :])
                            link(ins)
                            link(v_.tensor_scalar(proj["ss"], lmv[:, :, 1], 1e-5, None, ALU.add))
                            link(rsqrt(v_, link, proj["rr"], proj["ss"], proj["tmp"]))
                            for t in range(NT):
                                ins = v_.tensor_scalar(osb.rearrange("p c q -> p (c q)")[:, t * KV:(t + 1) * KV], bank(6)[:, t * KV:(t + 1) * KV],
                                                       lmv[:, t, 0:1], proj["rr"][:, t:t + 1],
                                                       ALU.subtract, ALU.mult)
                            ins.then_inc(pj["dve"], 1)
                            dve.wait_ge(pj["pe"], A_("pe", "v", b))
                            v_.tensor_copy(V[:, b, :, :, 0:AD].rearrange("p t h e -> p (t h) e"),
                                           pair(3).rearrange("p (x e) -> p x e", e=AD)).then_inc(pj["dve"], 1)
                        dve.wait_ge(pj["pe"], A_("pe", "qk"[w], b))
                        if w or b:
                            dve.wait_ge(pj["pool"], at("pool", "qk"[(w + 1) % 2], 0, 2 * b - 2 * (1 - w)))
                        scale = 1.0 if w else QSCALE
                        v_.scalar_tensor_tensor(out=rot1, in0=pair(1), scalar=scale, in1=tab_cos,
                                                op0=ALU.mult, op1=ALU.mult)
                        v_.scalar_tensor_tensor(out=rot2, in0=pair(2), scalar=scale, in1=tab_sin,
                                                op0=ALU.mult, op1=ALU.mult).then_inc(pj["dve"], 1)
                        if w == 0:
                            dve.wait_ge(pj["pe"], A_("pe", "hT", b))
                        split("dve", dve, "", 0, b, w)

        def biased_projections():
            @block.gpsimd
            def _(pool):
                set_ones(pool, 1)

            @block.sync
            def _(sp):
                for t, name in ((wqkv, "a_wqkv"), (bqk, "a_bqk"), (wout, "a_wo")):
                    sp.dma_start(t, d[name]).then_inc(load4, 16)
                sp.dma_start(bv, d["a_bv"].to_broadcast([P, P])).then_inc(load4, 16)

            @block.tensor
            def _(pe):
                A_ = lambda e, st, b: at(e, st, 1, 2 * b)
                pe.wait_ge(load4, 64)
                for b in range(B):
                    if b:
                        pe.wait_ge(pj["act"], A_("act", "hT", b - 1))
                    for t in range(NT):
                        ins = nc.tensor.transpose(pair(0)[:, t * P:(t + 1) * P], X[:, b * NT + t, :], ident)
                    ins.then_inc(pj["pe"], 1)
                    pe.wait_ge(pj["act"], A_("act", "hT", b))
                    if b:
                        pe.wait_ge(pj["dve"], A_("dve", "v", b - 1))
                    for z in range(2):
                        for c in range(2):
                            ins = nc.tensor.matmul(pair(1 + z)[:, c * 512:(c + 1) * 512], wqkv[:, z, :],
                                                   hT[:, c * 512:(c + 1) * 512], start=True, stop=True)
                        ins.then_inc(pj["pe"], 1)
                    for t in range(NT):
                        ins = nc.tensor.matmul(pair(3)[:, t * P:(t + 1) * P], hT[:, t * P:(t + 1) * P],
                                               wqkv[:, 2, :], start=True, stop=True)
                    ins.then_inc(pj["pe"], 1)

            @block.scalar
            def _(act):
                s_ = nc.scalar
                A_ = lambda e, st, b: at(e, st, 1, 2 * b)
                act.wait_ge(load4, 64)
                for b in range(B):
                    act.wait_ge(pj["pe"], A_("pe", "hT", b))
                    if b:
                        act.wait_ge(pj["pe"], A_("pe", "v", b - 1))
                    s_.activation(hT, pair(0), ACT.Copy).then_inc(pj["act"], 1)
                    split("act", act, "q", 1, b, 0)
                    act.wait_ge(pj["pe"], A_("pe", "k", b))
                    s_.activation(qk, pair(2), ACT.Identity, bias=bqk[:, 1:2]).then_inc(pj["act"], 1)
                    split("act", act, "k", 1, b, 1)

            @block.vector
            def _(dve):
                v_ = nc.vector
                A_ = lambda e, st, b: at(e, st, 1, 2 * b)
                link = chain(dve, dve_step)
                pad_values(v_, link)
                dve.wait_ge(load4, 64)
                for b in range(B):
                    dve.wait_ge(pj["pe"], A_("pe", "q", b))
                    v_.tensor_scalar(qk, pair(1), bqk[:, 0:1], QSCALE, ALU.add, ALU.mult).then_inc(pj["dve"], 1)
                    split("dve", dve, "", 1, b, 0)
                    split("dve", dve, "", 1, b, 1)
                    dve.wait_ge(pj["pe"], A_("pe", "v", b))
                    v_.tensor_tensor(V[:, b, :, :, 0:AD], pair(3).rearrange("p (t h e) -> p t h e", t=NT, e=AD),
                                     bv.rearrange("p (h e) -> p h e", e=AD).unsqueeze(1)
                                     .to_broadcast([P, NT, AH, AD]), ALU.add).then_inc(pj["dve"], 1)

        A.at = common_end
        w1, w2 = A.tile(NE * HID), A.tile(NE * EM, P)
        b1, b2 = A.tile(NE * EM), A.tile(NE, P)
        gate, gateb = A.tile(NE), A.tile(NE)
        enorm = A.tile(2)
        hn = [A.tile(T) for _ in range(B)]
        h2T = [A.tile(T) for _ in range(B)]
        hid = [A.tile(NE * EM, 512) for _ in range(2)]
        base = A.tile(NTILE, P)
        bpick = A.tile(NE, P)
        ess, err, etmp = A.tile(NTILE), A.tile(NTILE), A.tile(NTILE)
        logit, top, left = A.tile(NTILE, NE), A.tile(NTILE), A.tile(NTILE)
        onehot = A.tile(NTILE, NE)
        load3 = sem("load_experts")
        e_squared, e_normed, e_turned, e_hT = (sem("e_" + k) for k in ("squared", "normed", "turned", "hT"))
        e_logits, e_onehot, e_based = (sem("e_" + k) for k in ("logits", "onehot", "based"))
        hid_done, hid_act, hid_dve = sem("hid_done"), sem("hid_act"), sem("hid_dve")
        ey_done, ey_used = sem("ey_done"), sem("ey_used")
        CH = B * T // 512
        HB = NE * EM

        def experts():
            @block.sync
            def _(sp):
                for t, src in ((w1, d["e_w1"]), (w2, d["e_w2"]), (b1, d["e_b1"]), (gate, d["e_gate"]),
                               (enorm, d["k_norm"]), (b2.rearrange("p e o -> p (e o)"), d["e_b2"].to_broadcast([P, NE * P])),
                               (gateb, d["e_gateb"].to_broadcast([P, NE]))):
                    sp.dma_start(t, src).then_inc(load3, 16)
                barrier(sp, 3)

            @block.scalar
            def _(act):
                s_ = nc.scalar
                link = chain(act, act_step)
                act.wait_ge(load3, 112)
                for i in range(NTILE):
                    ins = s_.activation(sq, U[:, i, :], ACT.Square, accum_out=ess[:, i:i + 1])
                    if i < NTILE - 1:
                        link(ins)
                ins.then_inc(e_squared, 1)
                for b in range(B):
                    act.wait_ge(e_turned, b + 1)
                    s_.activation(h2T[b], pair(b), ACT.Copy, scale=enorm[:, 1:2]).then_inc(e_hT, 1)
                for c in range(CH):
                    for k in range(0, HB, 2):
                        act.wait_ge(hid_done, c * HB + k + 1)
                        ready(act, ey_done, 4 * (c - 1))
                        s_.activation(hid[c % 2][:, k, :], bank(4 + k % 4), ACT.Relu,
                                      bias=b1[:, k:k + 1]).then_inc(hid_act, 1)
                barrier(act, 3)

            @block.gpsimd
            def _(pool):
                g_ = nc.gpsimd
                link = chain(pool, pool_step)
                pool.wait_ge(e_onehot, 1)
                for i in range(NTILE):
                    link(g_.tensor_tensor(base[:, i, :], X[:, i, :], U[:, i, :], ALU.add))
                    link(g_.tensor_tensor(bpick, b2, spread(onehot[:, i, :], NE, P), ALU.mult))
                    for e in range(NE):
                        ins = g_.tensor_tensor(base[:, i, :], base[:, i, :], bpick[:, e, :], ALU.add)
                        if e < NE - 1:
                            link(ins)
                    ins.then_inc(e_based, 1)
                    pool.wait_ge(e_based, i + 1)
                barrier(pool, 3)

            @block.tensor
            def _(pe):
                pe.wait_ge(load3, 112)
                for b in range(B):
                    pe.wait_ge(e_normed, b + 1)
                    for t in range(NT):
                        ins = nc.tensor.transpose(pair(b)[:, t * P:(t + 1) * P], hn[b][:, t * P:(t + 1) * P], ident)
                    ins.then_inc(e_turned, 1)
                for b in range(B):
                    pe.wait_ge(e_hT, b + 1)
                    for t in range(NT):
                        i = b * NT + t
                        ins = nc.tensor.matmul(bank(4)[:, i * NE:(i + 1) * NE], h2T[b][:, t * P:(t + 1) * P], gate,
                                               start=True, stop=True)
                ins.then_inc(e_logits, 1)
                pe.wait_ge(e_onehot, 1)
                for c in range(CH + 1):
                    for k in range(HB):
                        if c < CH:
                            r = c * HB + k
                            ready(pe, hid_dve if k % 2 else hid_act, r // 2 - 1)
                            nc.tensor.matmul(bank(4 + k % 4), w1[:, k * P:(k + 1) * P],
                                             h2T[c // 2][:, c % 2 * 512:(c % 2 + 1) * 512],
                                             start=True, stop=True).then_inc(hid_done, 1)
                        if c and k % 4 == 3:
                            t = 4 * (c - 1) + k // 4
                            if k == 3:
                                pe.wait_ge(hid_act, c * HB // 2)
                                pe.wait_ge(hid_dve, c * HB // 2)
                            ready(pe, ey_used, t - 3)
                            for m in range(HB):
                                e = m // EM
                                ins = nc.tensor.matmul(bank(t % 4)[:, e * P:(e + 1) * P],
                                                       hid[(c - 1) % 2][:, m, k // 4 * P:(k // 4 + 1) * P], w2[:, m, :],
                                                       start=(m % EM == 0), stop=(m % EM == EM - 1))
                            ins.then_inc(ey_done, 1)
                barrier(pe, 3)

            @block.vector
            def _(dve):
                v_ = nc.vector
                link = chain(dve, dve_step)
                dve.wait_ge(e_squared, 1)
                link(v_.tensor_scalar(ess, ess, 1.0 / P, 1e-6, ALU.mult, ALU.add))
                link(rsqrt(v_, link, err, ess, etmp))
                for b in range(B):
                    for t in range(NT):
                        i = b * NT + t
                        ins = v_.tensor_scalar(hn[b][:, t * P:(t + 1) * P], U[:, i, :], err[:, i:i + 1], None, ALU.mult)
                    ins.then_inc(e_normed, 1)
                dve.wait_ge(load3, 112)
                dve.wait_ge(e_logits, 1)
                link(v_.tensor_tensor(logit, bank(4)[:, 0:NTILE * NE].rearrange("p (i e) -> p i e", e=NE),
                                      gateb.unsqueeze(1).to_broadcast([P, NTILE, NE]), ALU.add))
                link(v_.tensor_reduce(top, logit, AX.X, ALU.max))
                link(v_.tensor_tensor(onehot, logit, spread(top, NTILE, NE), ALU.is_ge))
                link(v_.tensor_scalar(left, onehot[:, :, 0], -1.0, 1.0, ALU.mult, ALU.add))
                for e in range(1, NE):
                    ins = v_.tensor_tensor(onehot[:, :, e], onehot[:, :, e], left, ALU.mult)
                    if e < NE - 1:
                        link(ins)
                        link(v_.tensor_tensor(left, left, onehot[:, :, e], ALU.subtract))
                ins.then_inc(e_onehot, 1)
                for c in range(CH + 1):
                    for k in range(HB):
                        if c < CH and k % 2:
                            dve.wait_ge(hid_done, c * HB + k + 1)
                            ready(dve, ey_done, 4 * (c - 1))
                            v_.tensor_scalar(hid[c % 2][:, k, :], bank(4 + k % 4), b1[:, k:k + 1], 0.0,
                                             ALU.add, ALU.max).then_inc(hid_dve, 1)
                        if c and k % 4 == 3:
                            i = 4 * (c - 1) + k // 4
                            dve.wait_ge(ey_done, i + 1)
                            dve.wait_ge(e_based, i + 1)
                            for e in range(NE):
                                ins = v_.scalar_tensor_tensor(
                                    out=X[:, i, :] if e == NE - 1 else base[:, i, :], in0=bank(i % 4)[:, e * P:(e + 1) * P],
                                    scalar=onehot[:, i, e:e + 1], in1=base[:, i, :], op0=ALU.mult, op1=ALU.add)
                                if e < NE - 1:
                                    link(ins)
                            ins.then_inc(ey_used, 1)
                            dve.wait_ge(ey_used, i + 1)
                            link(v_.bn_stats(stats[:, i, :], X[:, i, :]))
                            link(v_.bn_aggr(mv[:, i, :], stats[:, i, :]))
                layer_norm(dve, link, 1e-5)
                barrier(dve, 3)

        A.at = common_end
        tw, twp, twn = A.tile(P), A.tile(P), A.tile(P)
        tsum, tsc, thalf = A.tile(1), A.tile(1), A.tile(1)
        ones = A.tile(P)
        t_xT = A.tile(NTILE, P)
        load5 = sem("load_ternary")
        t_abs, t_ones, t_sum, t_quant = (sem("t_" + k) for k in ("abs", "ones", "sum", "quant"))
        t_turned, t_copied, t_done, t_added = (sem("t_" + k) for k in ("turned", "copied", "done", "added"))

        def ternary():
            @block.sync
            def _(sp):
                sp.dma_start(tw, d["t_w"]).then_inc(load5, 16)

            @block.scalar
            def _(act):
                act.wait_ge(load5, 16)
                nc.scalar.activation(twp, tw, ACT.Abs, accum_out=tsum).then_inc(t_abs, 1)
                for q in range(4):
                    act.wait_ge(t_turned, q + 1)
                    nc.scalar.activation(t_xT[:, 4 * q:4 * q + 4, :], bank(q).rearrange("p (k t) -> p k t", k=4),
                                         ACT.Copy).then_inc(t_copied, 1)
                barrier(act, 5)

            @block.gpsimd
            def _(pool):
                nc.gpsimd.memset(ones, 1.0).then_inc(t_ones, 1)
                barrier(pool, 5)

            @block.tensor
            def _(pe):
                for q in range(4):
                    for k in range(4):
                        ins = nc.tensor.transpose(bank(q)[:, k * P:(k + 1) * P], X[:, 4 * q + k, :], ident)
                    ins.then_inc(t_turned, 1)
                pe.wait_ge(t_abs, 1)
                pe.wait_ge(t_ones, 1)
                nc.tensor.matmul(bank(4)[:, 0:1], ones, tsum, start=True, stop=True).then_inc(t_sum, 1)
                pe.wait_ge(t_quant, 1)
                for q in range(4):
                    pe.wait_ge(t_copied, q + 1)
                    for k in range(4):
                        ins = nc.tensor.matmul(bank(4 + q)[:, k * P:(k + 1) * P], t_xT[:, 4 * q + k, :], tw,
                                               start=True, stop=True)
                    ins.then_inc(t_done, 1)
                barrier(pe, 5)

            @block.vector
            def _(dve):
                v_ = nc.vector
                link = chain(dve, dve_step)
                dve.wait_ge(t_sum, 1)
                link(v_.tensor_scalar(tsc, bank(4)[:, 0:1], 1.0 / (P * P), 1e-5, ALU.mult, ALU.max))
                link(v_.tensor_scalar(thalf, tsc, 0.5, None, ALU.mult))
                v_.tensor_scalar(twp, tw, thalf, None, ALU.is_gt)
                link(v_.tensor_scalar(twn, tw, -1.0, thalf, ALU.mult, ALU.is_gt))
                link(v_.tensor_tensor(twp, twp, twn, ALU.subtract))
                v_.tensor_scalar(tw, twp, tsc, None, ALU.mult).then_inc(t_quant, 1)
                for q in range(4):
                    dve.wait_ge(t_done, q + 1)
                    t = slice(4 * q, 4 * q + 4)
                    v_.tensor_tensor(X[:, t, :], bank(4 + q).rearrange("p (k o) -> p k o", k=4), X[:, t, :],
                                     ALU.add).then_inc(t_added, 1)
                    dve.wait_ge(t_added, q + 1)
                    for i in range(t.start, t.stop):
                        link(v_.bn_stats(stats[:, i, :], X[:, i, :]))
                        link(v_.bn_aggr(mv[:, i, :], stats[:, i, :]))
                layer_norm(dve, link, 1e-5)
                barrier(dve, 5)

            @block.sync
            def _(sp):
                barrier(sp, 5)

        if phases >= 2:
            latent_projections()
            attention(0)
        if phases >= 3:
            experts()
        if phases >= 4:
            biased_projections()
            attention(1)
        if phases >= 5:
            ternary()

        @block.sync
        def _(sp):
            res = U if phases == 2 else X
            sp.dma_start(out.rearrange("(n p) d -> p n d", p=P), res).then_inc(stored, 16)
            sp.wait_ge(stored, 16)


_OUT = (B, T, P)


def kernel(**inputs):
    import concourse.bacc as _bacc
    from concourse.bass_utils import run_bass_kernel_spmd as _run

    nc = _bacc.Bacc("TRN2", target_bir_lowering=False, num_devices=1)
    arrays = layout(inputs)
    d = {k: nc.dram_tensor(k, v.shape, mybir.dt.from_np(v.dtype), kind="ExternalInput").ap()
         for k, v in arrays.items()}
    out = nc.dram_tensor("out", (B * T, P), F32, kind="ExternalOutput").ap()
    build(nc, d, out)
    r = _run(nc, [arrays], core_ids=[0])
    return r.results[0]["out"].reshape(_OUT)
```

```python
from contextlib import ExitStack

import concourse.bass as bass
from concourse import mybir
import numpy as np

F32 = mybir.dt.float32
BF16 = mybir.dt.bfloat16
I32 = mybir.dt.int32
ALU = mybir.AluOpType
ACT = mybir.ActivationFunctionType
AX = mybir.AxisListType

P = 128
B, T = 2, 1024
NT = T // P
NTILE = B * NT
RH, RD, RV = 8, 64, 128
AH, AD = 16, 8
HG = 4
NG = AH // HG
VW = 32
KV = 64
NE, HID = 4, 512
EM = HID // P
PARTS = 3
SROWS = PARTS * PARTS * AD
MROWS = SROWS + PARTS
RSQRT_SEED = float(0x5F3759DF)
MASKED = -1e30
TWO_ONES = float(np.array([0x3F803F80], np.uint32).view(np.float32)[0])
NEG = -1e9
QSCALE = AD ** -0.5
C = 512


def constants():
    f = np.float32
    c = {}
    c["c_ident"] = np.eye(P, dtype=f)
    t = np.arange(T, dtype=f)
    inv = (1.0 / np.power(f(10000.0), np.arange(0, RD, 2, dtype=f) / f(RD))).astype(f)
    ang = (t[:, None] * inv[None, :]).astype(f)
    by_tile = lambda a: np.ascontiguousarray(a.reshape(NT, P, -1).transpose(1, 0, 2))
    c["c_rcos"] = by_tile(np.cos(ang).astype(f))
    c["c_rsin"] = by_tile(np.sin(ang).astype(f))
    gamma = 1.0 - np.exp2(-5.0 - np.arange(RH, dtype=np.float64))
    i = np.arange(P, dtype=np.float64)
    slots = [2 * (s % 4) + s // 4 for s in range(RH)]
    c["c_gq"] = (gamma[None, :] ** (i[:, None] + 1) * RD ** -0.5).astype(f)
    c["c_gk"] = (gamma[None, :] ** (P - 1 - i[:, None])).astype(f)
    dm = np.zeros((P, RH, P))
    for s, h in enumerate(slots):
        dm[:, s, :] = (gamma[h] ** -(i[:, None] + 1)) * (i[None, :] >= i[:, None])
    c["c_decay"] = dm.astype(f)
    gc = np.zeros((P, 4, P))
    for h in range(RH):
        gc[(h % 2) * RD:(h % 2 + 1) * RD, h // 2, :] = gamma[h] ** P
    c["c_gchunk"] = gc.astype(f)
    half = AD // 2
    inv = (1.0 / np.power(f(10000.0), np.arange(half, dtype=f) / f(half))).astype(f)
    ang = (t[:, None] * inv[None, :]).astype(f)
    cos = np.cos(ang).astype(f).T
    sin = np.sin(ang).astype(f).T
    cos8 = np.concatenate([cos, cos])
    sin8 = np.concatenate([-sin, sin])
    c["c_kcos"] = np.tile(cos8, (AH, 1)).astype(f)
    c["c_ksin"] = np.tile(sin8, (AH, 1)).astype(f)
    m = np.zeros((P, 4, P), dtype=f)
    m[:, 0] = np.where(i[None, :] > i[:, None], MASKED, 0)
    m[:, 1] = np.where(i[:, None] > i[None, :], MASKED, 0)
    m[0, 2, P - 1] = NEG
    m[P - 1, 3, 0] = NEG
    c["c_mask"] = m
    c["c_ones"] = np.full((PARTS, NG * HG * T // 2), TWO_ONES, dtype=f)
    return c


def swap_halves(w):
    return w.reshape(AH, 2, AD // 2, -1)[:, ::-1].reshape(AH * AD, -1)


def layout(x):
    a = {k: np.asarray(v) for k, v in x.items()}
    slots = [2 * (s % 4) + s // 4 for s in range(RH)]
    c = np.ascontiguousarray
    d = dict(constants())
    d["x"] = a["L0_attn_x"].reshape(B * T, P)
    d["r_wqk"] = c(np.concatenate([a["L0_attn_Wq"], a["L0_attn_Wk"]]).T)
    byslot = lambda w: w.reshape(RH, RV, -1)[slots]
    d["r_wv"] = c(byslot(a["L0_attn_Wv"]).reshape(RH * RV, P).T)
    d["r_wg"] = c(byslot(a["L0_attn_Wg"]).reshape(RH * RV, P).T)
    d["r_wo"] = c(byslot(c(a["L0_attn_Wo"].T)).transpose(1, 0, 2))
    gn = np.stack([a["L0_attn_gn_weight"], a["L0_attn_gn_bias"]])
    d["r_gn"] = c(gn.reshape(2, RH, RV)[:, slots].transpose(2, 0, 1))
    n1, n2 = a["L0_ffn_norm1_w"], a["L0_ffn_norm2_w"]
    wq, wuk = a["L0_ffn_Wq"], a["L0_ffn_Wuk"]
    d["k_wq"] = c(np.stack([wq.T, swap_halves(wq).T], axis=1))
    d["k_wdkv"] = c(a["L0_ffn_Wdkv"].T)
    d["k_wuk"] = c(np.stack([wuk.T, swap_halves(wuk).T], axis=1))
    d["k_wuv"] = c(a["L0_ffn_Wuv"].T)
    d["k_wo"] = c(a["L0_ffn_Wo"].T)
    d["k_norm"] = c(np.stack([n1, n2], axis=1))
    d["k_ln"] = c(np.stack([a["L0_ffn_ln_g"], a["L0_ffn_ln_b"]], axis=1))
    d["e_gate"] = c(a["L0_ffn_gate_w"].T)
    d["e_gateb"] = a["L0_ffn_gate_b"].reshape(1, NE)
    d["e_w1"] = c(a["L0_ffn_W1"].reshape(NE * HID, P).T)
    d["e_b1"] = c(a["L0_ffn_b1"].reshape(NE * EM, P).T)
    w2 = a["L0_ffn_W2"].reshape(NE, P, EM, P)
    d["e_w2"] = c(w2.transpose(3, 0, 2, 1).reshape(P, NE * EM, P))
    d["e_b2"] = a["L0_ffn_b2"].reshape(1, NE * P)
    d["a_wqkv"] = c(np.stack([a["L1_attn_Wq"].T, a["L1_attn_Wk"].T, a["L1_attn_Wv"].T], axis=1))
    d["a_bqk"] = c(np.stack([a["L1_attn_bq"], a["L1_attn_bk"]], axis=1))
    d["a_bv"] = a["L1_attn_bv"].reshape(1, P)
    d["a_wo"] = c(a["L1_attn_Wo"].T)
    d["t_w"] = c(a["L1_ffn_weight"].T)
    return {k: np.ascontiguousarray(v) for k, v in d.items()}


class Arena:

    def __init__(self, tensor, words):
        self.tensor, self.words, self.at, self.most = tensor, words, 0, 0

    def tile(self, *shape, dtype=F32, rows=P):
        n = int(np.prod(shape))
        words = n if dtype != BF16 else (n + 1) // 2
        a = self.tensor[0:rows, self.at:self.at + words]
        self.at += words
        self.most = max(self.most, self.at)
        assert self.at <= self.words, (self.at, self.words)
        if dtype != F32:
            a = a.bitcast(dtype)
        if len(shape) == 1:
            return a
        names = " ".join("abcde"[:len(shape)])
        sizes = {k: s for k, s in zip("abcde", shape)}
        return a.rearrange(f"p ({names}) -> p {names}", **sizes)


def build(nc, d, out, phases=5):
    ctx = ExitStack()
    with ctx:
        words = 52000
        A = Arena(ctx.enter_context(nc.sbuf_tensor("arena", [P, words], F32)), words)
        PS = ctx.enter_context(nc.psum_tensor("banks", [P, 8, 512], F32))

        def sem(name):
            return ctx.enter_context(nc.semaphore(name))

        def bank(b):
            return PS[:, b, :]

        def pair(q):
            return PS[:, 2 * q:2 * q + 2, :].rearrange("p b n -> p (b n)")

        q_dram = nc.dram_tensor("q_parts", [2, B, P, PARTS, T], BF16, kind="Internal").ap()
        k_dram = nc.dram_tensor("k_parts", [2, B, PARTS, P, PARTS, T], BF16, kind="Internal").ap()

        X = A.tile(NTILE, P)
        ident = A.tile(P)
        identb = A.tile(P, dtype=BF16)
        masks = A.tile(4, P, dtype=BF16)
        stats = A.tile(NTILE, 6)
        mv = A.tile(NTILE, 2)
        newt = A.tile(2, 16)
        rstd = A.tile(16)
        epst = A.tile(2)
        sq = A.tile(P)
        xss, xrr = A.tile(NTILE), A.tile(NTILE)
        U = A.tile(NTILE, P)
        common_end = A.at

        wqk, wv, wg = A.tile(2 * RH * RD), A.tile(RH * RV), A.tile(RH * RV)
        wo = A.tile(RH, P)
        gn = A.tile(2, RH)
        decay, gchunk = A.tile(RH * P), A.tile(4 * P)
        rcos, rsin = A.tile(NT, RD // 2), A.tile(NT, RD // 2)
        gq, gk = A.tile(RH), A.tile(RH)
        XT = A.tile(NTILE, P)
        rc, rs = A.tile(2 * RH * RD), A.tile(2 * RH * RD)
        rot = [A.tile(2 * RH * RD) for _ in range(2)]
        qd = [A.tile(RH * RD) for _ in range(2)]
        kd = [A.tile(RH * RD) for _ in range(2)]
        qkT = A.tile(8, P)
        vv = [A.tile(RH, P) for _ in range(2)]
        sm = A.tile(RH, P)
        state = [A.tile(4 * P) for _ in range(2)]
        stdec = A.tile(4 * P)
        oc = [A.tile(RH, P) for _ in range(2)]
        osum, gvar, grs, gnt = A.tile(RH), A.tile(RH), A.tile(RH), A.tile(2, RH)
        on = A.tile(RH, P)
        sig = A.tile(RH, P)
        ga = A.tile(RH, P)
        uu = A.tile(RH, P)
        maskf = A.tile(4, P)
        retention_end = A.at

        A.at = common_end
        Qs = A.tile(NG, HG, T, dtype=BF16)
        Ks = A.tile(NG, HG, T, dtype=BF16)
        turned_at = A.at
        Pr = [A.tile(HG, T) for _ in range(2)]
        V = A.tile(B, NT, AH, VW)
        mx = [A.tile(2, HG * NT) for _ in range(2)]
        nm1 = A.tile(P, rows=HG * NT)
        nmp = [A.tile(PARTS, P, dtype=BF16, rows=HG * NT) for _ in range(2)]
        osb = A.tile(2, 512)
        rden = A.tile(NT // 2, HG)
        On = A.tile(NT, P)
        OT = A.tile(T)
        kq = [[A.tile(C) for _ in range(2)] for _ in range(2)]
        rem = [[A.tile(C) for _ in range(2)] for _ in range(2)]
        parts = [[A.tile(PARTS, C, dtype=BF16) for _ in range(2)] for _ in range(2)]
        lat = osb[:, 0, :].rearrange("p (t e) -> p t e", e=KV)
        latT = [On[0:KV, 4 * c:4 * c + 4, :].rearrange("p t e -> p (t e)") for c in range(2)]
        lvar, lrs, ltmp = A.tile(NT), A.tile(NT), A.tile(NT)
        at = A.at
        A.at = turned_at
        hn_, hT = [A.tile(4, P) for _ in range(2)], [A.tile(C) for _ in range(2)]
        rot1, rot2 = ([A.tile(C) for _ in range(2)] for _ in range(2))
        assert A.at <= turned_at + 2 * HG * T
        A.at = at
        assert A.at >= retention_end
        wq2, wuk2 = A.tile(2, P), A.tile(2, P, rows=KV)
        wdkv, wuv = A.tile(KV), A.tile(P, rows=KV)
        wout = A.tile(P)
        norms, lnp = A.tile(2), A.tile(2, rows=KV)
        lst, lmv = A.tile(NT, 6), A.tile(NT, 2)
        latent_at = A.at
        tab_cos, tab_sin = A.tile(T), A.tile(T)
        A.at = latent_at
        wqkv, bqk, bv = A.tile(3, P), A.tile(2), A.tile(P)

        A.at = common_end
        w1, w2 = A.tile(NE * HID), A.tile(NE * EM, P)
        b1, b2 = A.tile(NE * EM), A.tile(NE, P)
        gate, gateb = A.tile(NE), A.tile(NE)
        enorm = A.tile(2)
        assert A.at <= common_end + 3 * HG * T // 2
        hn = [A.tile(NT, P) for _ in range(B)]
        h2T = [A.tile(T) for _ in range(B)]
        hid = [A.tile(NE * EM, 512) for _ in range(2)]
        base = A.tile(NTILE, P)
        bpick = A.tile(NE, P)
        logit, top, left = A.tile(NTILE, NE), A.tile(NTILE), A.tile(NTILE)
        onehot = A.tile(NTILE, NE)

        A.at = common_end
        tw, twp, twn = A.tile(P), A.tile(P), A.tile(P)
        tsum, tsc, thalf = A.tile(1), A.tile(1), A.tile(1)
        ones = A.tile(P)
        t_xT = A.tile(NTILE, P)

        phase_end = sem("phase_end")
        load = {k: sem("load_" + k) for k in ("x", "qk", "rest", "gv", "wo", "mask")}
        dve_step, pool_step, act_step = sem("dve_step"), sem("pool_step"), sem("act_step")
        xT_done, xT_copied = sem("xT_done"), sem("xT_copied")
        qk_done, rot_muls, rot_ready = sem("qk_done"), sem("rot_muls"), sem("rot_ready")
        k_rotated = sem("k_rotated")
        v_done, v_copied = sem("v_done"), sem("v_copied")
        qkT_done, qkT_copied = sem("qkT_done"), sem("qkT_copied")
        sc_done, sc_masked = sem("sc_done"), sem("sc_masked")
        delta_done, state_dec, state_ready = sem("delta_done"), sem("state_dec"), sem("state_ready")
        o_done, o_centred, o_squared = sem("o_done"), sem("o_centred"), sem("o_squared")
        o_rstd, o_normed = sem("o_rstd"), sem("o_normed")
        g_done, g_silu = sem("g_done"), sem("g_silu")
        onT_done, onT_affine, u_ready = sem("onT_done"), sem("onT_affine"), sem("u_ready")
        y_done, y_added = sem("y_done"), sem("y_added")
        ln_rstd, ln_done = sem("ln_rstd"), sem("ln_done")
        stored = sem("stored")
        load2, x_ready, x_squared = sem("load_latent"), sem("x_ready"), sem("x_squared")

        counts = {}

        def chain(eng, s):
            def link(ins):
                counts[s.name] = counts.get(s.name, 0) + 1
                ins.then_inc(s, 1)
                eng.wait_ge(s, counts[s.name])
            return link

        def barrier(eng, n):
            eng.drain().then_inc(phase_end, 1)
            eng.wait_ge(phase_end, 5 * n)

        def rsqrt(eng, link, y, v, tmp, fused=True):
            link(eng.tensor_scalar(y.bitcast(I32), v.bitcast(I32), -0.5, RSQRT_SEED, ALU.mult, ALU.add))
            for k in range(3):
                if fused:
                    link(eng.scalar_tensor_tensor(out=tmp, in0=y, scalar=-0.5, in1=y, op0=ALU.mult, op1=ALU.mult))
                    link(eng.tensor_tensor(tmp, tmp, v, ALU.mult))
                    ins = eng.scalar_tensor_tensor(out=y, in0=tmp, scalar=1.5, in1=y, op0=ALU.add, op1=ALU.mult)
                    if k < 2:
                        link(ins)
                    continue
                link(eng.tensor_tensor(tmp, y, y, ALU.mult))
                link(eng.tensor_tensor(tmp, tmp, v, ALU.mult))
                link(eng.tensor_scalar(tmp, tmp, -0.5, 1.5, ALU.mult, ALU.add))
                ins = eng.tensor_tensor(y, y, tmp, ALU.mult)
                if k < 2:
                    link(ins)
            return ins

        def heads(a, n=RH):
            return a.rearrange("p (h v) -> p h v", h=n)

        def spread(a, n, w):
            return a.unsqueeze(2).to_broadcast([P, n, w])

        def statistics(v_, link, lo, hi):
            for i in range(lo, hi):
                ins = v_.bn_stats(stats[:, i, :], X[:, i, :])
            link(ins)
            for i in range(lo, hi):
                ins = v_.bn_aggr(mv[:, i, :], stats[:, i, :])
            link(ins)

        def layer_norm(dve, link, eps, lo=0, hi=NTILE):
            v_ = nc.vector
            link(v_.tensor_scalar(rstd[:, lo:hi], mv[:, lo:hi, 1], eps, None, ALU.add))
            link(rsqrt(v_, link, newt[:, 1, lo:hi], rstd[:, lo:hi], newt[:, 0, lo:hi]))
            for i in range(lo, hi):
                ins = v_.tensor_scalar(X[:, i, :], X[:, i, :], mv[:, i, 0:1], newt[:, 1, i:i + 1],
                                       ALU.subtract, ALU.mult)
            return ins

        block = ctx.enter_context(nc.Block())

        @block.sync
        def _(sp):
            sp.dma_start(ident, d["c_ident"]).then_inc(load["x"], 16)
            sp.dma_start(X, d["x"].rearrange("(n p) d -> p n d", p=P)).then_inc(load["x"], 16)
            sp.dma_start(wqk, d["r_wqk"]).then_inc(load["qk"], 16)
            sp.dma_start(rcos, d["c_rcos"]).then_inc(load["qk"], 16)
            sp.dma_start(rsin, d["c_rsin"]).then_inc(load["qk"], 16)
            sp.dma_start(gq, d["c_gq"]).then_inc(load["qk"], 16)
            sp.dma_start(gk, d["c_gk"]).then_inc(load["qk"], 16)
            sp.dma_start(wv, d["r_wv"]).then_inc(load["gv"], 16)
            sp.dma_start(wg, d["r_wg"]).then_inc(load["gv"], 16)
            sp.dma_start(decay, d["c_decay"].rearrange("p s t -> p (s t)")).then_inc(load["rest"], 16)
            sp.dma_start(gchunk, d["c_gchunk"].rearrange("p s t -> p (s t)")).then_inc(load["rest"], 16)
            sp.dma_start(wo, d["r_wo"]).then_inc(load["wo"], 16)
            sp.dma_start(gn, d["r_gn"]).then_inc(load["wo"], 16)
            sp.dma_start(maskf, d["c_mask"]).then_inc(load["mask"], 16)
            for t, name in ((tab_cos, "c_kcos"), (tab_sin, "c_ksin"), (wq2, "k_wq"), (wdkv, "k_wdkv"),
                            (wuk2, "k_wuk"), (wuv, "k_wuv"), (wout, "k_wo"), (norms, "k_norm"), (lnp, "k_ln")):
                sp.dma_start(t, d[name]).then_inc(load2, 16)
            barrier(sp, 1)

        def ready(e, s, n):
            if n >= 1:
                e.wait_ge(s, n)

        @block.tensor
        def _(pe):
            pe.wait_ge(load["x"], 32)
            for q in range(4):
                for k in range(4):
                    i = 4 * q + k
                    ins = nc.tensor.transpose(bank(q)[:, k * P:(k + 1) * P], X[:, i, :], ident)
                ins.then_inc(xT_done, 1)
            pe.wait_ge(load["qk"], 80)
            pe.wait_ge(xT_copied, 4)
            for n in range(-1, NTILE + 2):
                this = 0 <= n < NTILE
                first, last = n % NT == 0, n % NT == NT - 1
                if this:
                    pe.wait_ge(rot_ready, n + 1)
                    ready(pe, y_added, n - 2)
                    ready(pe, state_ready, n)
                    for p4 in range(4):
                        nc.tensor.transpose(bank(6)[:, p4 * P:(p4 + 1) * P], qd[n % 2][:, p4 * P:(p4 + 1) * P], ident)
                    for p4 in range(4):
                        ins = nc.tensor.transpose(bank(7)[:, p4 * P:(p4 + 1) * P],
                                                  rot[n % 2][:, 512 + p4 * P:512 + (p4 + 1) * P], ident)
                    ins.then_inc(qkT_done, 1)
                if n + 1 < NTILE:
                    ready(pe, g_silu, n - 1)
                    for c in range(2):
                        ins = nc.tensor.matmul(bank(c), XT[:, n + 1, :], wqk[:, c * 512:(c + 1) * 512],
                                               start=True, stop=True)
                    ins.then_inc(qk_done, 1)
                if this:
                    if n == 0:
                        pe.wait_ge(load["gv"], 32)
                    ready(pe, o_centred, n)
                    for c in range(2):
                        ins = nc.tensor.matmul(bank(2 + c), XT[:, n, :], wv[:, c * 512:(c + 1) * 512],
                                               start=True, stop=True)
                    ins.then_inc(v_done, 1)
                    pe.wait_ge(qkT_copied, n + 1)
                    ready(pe, onT_affine, n - 1)
                    for p4 in range(4):
                        for par in range(2):
                            rows = slice(par * RD, (par + 1) * RD)
                            ins = nc.tensor.matmul(bank(4 + par)[:, p4 * P:(p4 + 1) * P], qkT[rows, 4 + p4, :],
                                                   qkT[rows, p4, :], start=True, stop=True)
                    ins.then_inc(sc_done, 1)
                    pe.wait_ge(v_copied, n + 1)
                    if last:
                        nc.tensor.matmul(bank(6)[:, 0:P], ident, ident, start=True, stop=True).then_inc(delta_done, 1)
                    else:
                        for p4 in range(4):
                            for par in range(2):
                                ins = nc.tensor.matmul(
                                    PS[par * RD:(par + 1) * RD, 6, p4 * P:(p4 + 1) * P],
                                    kd[n % 2][:, (2 * p4 + par) * RD:(2 * p4 + par + 1) * RD],
                                    vv[n % 2][:, 4 * par + p4, :], start=True, stop=True)
                        ins.then_inc(delta_done, 1)
                i = n - 2
                if 0 <= i < NTILE:
                    pe.wait_ge(u_ready, i + 1)
                    ready(pe, y_added, i)
                    for s in range(RH):
                        ins = nc.tensor.matmul(bank(7)[:, 0:P], uu[:, s, :], wo[:, s, :],
                                               start=(s == 0), stop=(s == RH - 1))
                    ins.then_inc(y_done, 1)
                i = n - 1
                if 0 <= i < NTILE:
                    if n + 1 < NTILE:
                        pe.wait_ge(rot_muls, n + 2)
                    else:
                        pe.wait_ge(g_silu, i)
                    for s in range(RH):
                        ins = nc.tensor.matmul(bank(s // 4)[:, (s % 4) * P:(s % 4 + 1) * P],
                                               wg[:, s * P:(s + 1) * P], XT[:, i, :], start=True, stop=True)
                    ins.then_inc(g_done, 1)
                if this:
                    pe.wait_ge(sc_masked, n + 1)
                    ready(pe, state_ready, n)
                    for s in range(RH):
                        par, p4 = divmod(s, 4)
                        rows = slice(par * RD, (par + 1) * RD)
                        o = bank(2 + par)[:, p4 * P:(p4 + 1) * P]
                        if not first:
                            nc.tensor.matmul(o, qkT[rows, p4, :], state[(n - 1) % 2][rows, p4 * P:(p4 + 1) * P],
                                             start=True, stop=False)
                        ins = nc.tensor.matmul(o, sm[:, s, :], vv[n % 2][:, s, :], start=first, stop=True)
                    ins.then_inc(o_done, 1)
                i = n - 1
                if 0 <= i < NTILE:
                    pe.wait_ge(o_normed, i + 1)
                    pe.wait_ge(sc_masked, min(n + 1, NTILE))
                    for s in range(RH):
                        ins = nc.tensor.transpose(bank(4 + s // 4)[:, (s % 4) * P:(s % 4 + 1) * P], on[:, s, :], ident)
                    ins.then_inc(onT_done, 1)
            barrier(pe, 1)

        @block.vector
        def _(dve):
            v_ = nc.vector
            link = chain(dve, dve_step)
            dve.wait_ge(load["qk"], 80)
            for n in range(-1, NTILE + 2):
                this = 0 <= n < NTILE
                i = n - 2
                if 0 <= i < NTILE:
                    dve.wait_ge(onT_affine, i + 1)
                    ready(dve, y_done, i)
                    v_.tensor_tensor(uu, ga, sig, ALU.mult).then_inc(u_ready, 1)
                if n + 1 < NTILE:
                    dve.wait_ge(qk_done, n + 2)
                    ready(dve, rot_ready, n + 1)
                    c = (n + 1) % NT
                    qk3 = pair(0).rearrange("p (g e) -> p g e", e=RD // 2)
                    qk4 = pair(0).rearrange("p (h z e) -> p h z e", h=2 * RH, z=2)
                    rs4 = rs.rearrange("p (h z e) -> p h z e", h=2 * RH, z=2)
                    cosb = rcos[:, c:c + 1, :].to_broadcast([P, 4 * RH, RD // 2])
                    sinb = rsin[:, c:c + 1, :].to_broadcast([P, 2 * RH, RD // 2])
                    v_.tensor_tensor(rc.rearrange("p (g e) -> p g e", e=RD // 2), qk3, cosb, ALU.mult)
                    v_.scalar_tensor_tensor(out=rs4[:, :, 0, :], in0=qk4[:, :, 1, :], scalar=-1.0, in1=sinb,
                                            op0=ALU.mult, op1=ALU.mult)
                    v_.tensor_tensor(rs4[:, :, 1, :], qk4[:, :, 0, :], sinb, ALU.mult).then_inc(rot_muls, 1)
                    dve.wait_ge(rot_muls, n + 2)
                    ready(dve, qkT_done, n)
                    v_.tensor_tensor(rot[(n + 1) % 2][:, 512:1024], rc[:, 512:1024], rs[:, 512:1024],
                                     ALU.add).then_inc(k_rotated, 1)
                if this:
                    if n == 0:
                        dve.wait_ge(load["rest"], 32)
                    dve.wait_ge(sc_done, n + 1)
                    ready(dve, o_done, n)
                    v_.tensor_tensor(sm.rearrange("p s t -> p (s t)"), pair(2), decay, ALU.mult).then_inc(sc_masked, 1)
                    dve.wait_ge(delta_done, n + 1)
                    if n % NT == 0:
                        v_.tensor_copy(state[n % 2], bank(6)).then_inc(state_ready, 1)
                    elif n % NT < NT - 1:
                        dve.wait_ge(state_dec, n + 1)
                        v_.tensor_tensor(state[n % 2], stdec, bank(6), ALU.add).then_inc(state_ready, 1)
                    else:
                        v_.memset(epst[:, 0:1], 0.0).then_inc(state_ready, 1)
                i = n - 1
                if 0 <= i < NTILE:
                    dve.wait_ge(o_rstd, i + 1)
                    ready(dve, onT_done, i)
                    v_.tensor_tensor(on, oc[i % 2], spread(grs, RH, P), ALU.mult).then_inc(o_normed, 1)
                i = n - 2
                if 0 <= i < NTILE:
                    dve.wait_ge(y_done, i + 1)
                    v_.tensor_tensor(X[:, i, :], bank(7)[:, 0:P], X[:, i, :], ALU.add).then_inc(y_added, 1)
                    dve.wait_ge(y_added, i + 1)
                    link(v_.bn_stats(stats[:, i, :], X[:, i, :]))
                    link(v_.bn_aggr(mv[:, i, :], stats[:, i, :]))
                if this:
                    dve.wait_ge(o_done, n + 1)
                    o3 = heads(pair(1))
                    link(v_.tensor_reduce(osum, o3, AX.X, ALU.add))
                    link(v_.tensor_scalar(osum, osum, 1.0 / RV, None, ALU.mult))
                    ready(dve, o_squared, n - 1)
                    v_.tensor_tensor(oc[n % 2], o3, spread(osum, RH, P), ALU.subtract).then_inc(o_centred, 1)
                if n == NT + 2:
                    layer_norm(dve, link, 1e-5, 0, NT).then_inc(x_ready, 1)
                if n == NT + 5:
                    dve.wait_ge(x_squared, 1)
                    link(v_.tensor_scalar(xss[:, 0:NT], xss[:, 0:NT], 1.0 / P, 1e-6, ALU.mult, ALU.add))
                    link(rsqrt(v_, link, xrr[:, 0:NT], xss[:, 0:NT], newt[:, 0, 0:NT]))
            layer_norm(dve, link, 1e-5, NT, NTILE).then_inc(x_ready, 1)
            dve.wait_ge(x_ready, B)
            barrier(dve, 1)

        @block.gpsimd
        def _(pool):
            g_ = nc.gpsimd
            link = chain(pool, pool_step)
            pool.wait_ge(load["qk"], 80)
            for n in range(-1, NTILE + 1):
                if 0 <= n < NTILE:
                    if n == 0:
                        pool.wait_ge(load["rest"], 32)
                    ready(pool, state_ready, n)
                    if n % NT:
                        g_.tensor_tensor(stdec, state[(n - 1) % 2], gchunk, ALU.mult).then_inc(state_dec, 1)
                    else:
                        g_.memset(stdec[:, 0:1], 0.0).then_inc(state_dec, 1)
                i = n - 1
                if 0 <= i < NTILE:
                    pool.wait_ge(o_squared, i + 1)
                    link(g_.tensor_scalar(gvar, gvar, 1.0 / RV, 1e-5, ALU.mult, ALU.add))
                    ready(pool, o_normed, i)
                    rsqrt(g_, link, grs, gvar, gnt[:, 0, :], fused=False).then_inc(o_rstd, 1)
                if n + 1 < NTILE:
                    m = n + 1
                    pool.wait_ge(rot_muls, m + 1)
                    ready(pool, qkT_done, m - 1)
                    link(g_.tensor_tensor(rot[m % 2][:, 0:512], rc[:, 0:512], rs[:, 0:512], ALU.add))
                    g_.tensor_tensor(heads(qd[m % 2]), heads(rot[m % 2][:, 0:512]), spread(gq, RH, RD), ALU.mult)
                    pool.wait_ge(k_rotated, m + 1)
                    ready(pool, delta_done, m - 1)
                    g_.tensor_tensor(heads(kd[m % 2]), heads(rot[m % 2][:, 512:1024]), spread(gk, RH, RD),
                                     ALU.mult).then_inc(rot_ready, 1)
            pool.wait_ge(load["mask"], 16)
            g_.tensor_copy(masks, maskf)
            g_.tensor_copy(identb, ident)
            barrier(pool, 1)

        @block.scalar
        def _(act):
            s_ = nc.scalar
            link = chain(act, act_step)
            for q in range(4):
                act.wait_ge(xT_done, q + 1)
                s_.activation(XT[:, 4 * q:4 * q + 4, :], bank(q).rearrange("p (k t) -> p k t", k=4),
                              ACT.Copy).then_inc(xT_copied, 1)
            act.wait_ge(load["wo"], 32)
            for n in range(NTILE + 2):
                if n < NTILE:
                    act.wait_ge(qkT_done, n + 1)
                    ready(act, o_done, n)
                    s_.activation(qkT.rearrange("p s t -> p (s t)"), pair(3), ACT.Copy).then_inc(qkT_copied, 1)
                i = n - 2
                if 0 <= i < NTILE:
                    act.wait_ge(onT_done, i + 1)
                    ready(act, u_ready, i)
                    for s in range(RH):
                        ins = s_.activation(ga[:, s, :], bank(4 + s // 4)[:, (s % 4) * P:(s % 4 + 1) * P],
                                            ACT.Identity, scale=gn[:, 0, s:s + 1], bias=gn[:, 1, s:s + 1])
                    ins.then_inc(onT_affine, 1)
                if n < NTILE:
                    act.wait_ge(v_done, n + 1)
                    ready(act, o_done, n - 1)
                    s_.activation(vv[n % 2].rearrange("p s t -> p (s t)"), pair(1), ACT.Copy).then_inc(v_copied, 1)
                i = n - 1
                if 0 <= i < NTILE:
                    act.wait_ge(o_centred, i + 1)
                    ready(act, o_rstd, i)
                    for s in range(RH):
                        ins = s_.activation(sq, oc[i % 2][:, s, :], ACT.Square, accum_out=gvar[:, s:s + 1])
                        if s < RH - 1:
                            link(ins)
                    ins.then_inc(o_squared, 1)
                    act.wait_ge(g_done, i + 1)
                    ready(act, u_ready, i)
                    s_.activation(sig.rearrange("p s t -> p (s t)"), pair(0), ACT.Silu).then_inc(g_silu, 1)
                if n in (NT + 3, NTILE + 1):
                    b = int(n > NTILE)
                    act.wait_ge(x_ready, b + 1)
                    act.wait_ge(o_squared, min(n, NTILE))
                    for i in range(b * NT, (b + 1) * NT):
                        ins = s_.activation(sq, X[:, i, :], ACT.Square, accum_out=xss[:, i:i + 1])
                        if i % NT < NT - 1:
                            link(ins)
                        else:
                            ins.then_inc(x_squared, 1)
                            act.wait_ge(x_squared, b + 1)
            barrier(act, 1)

        load3, load4, load5 = sem("load_experts"), sem("load_biased"), sem("load_ternary")
        u_squared, x2_ready = sem("u_squared"), sem("x2_ready")
        KINDS = ("normed", "turned", "turned_copied", "q_made", "lat_made", "lat_normed", "lat_turned",
                 "lat_copied", "k_made", "v_made", "v_kept", "q_rot_done", "q_full", "q_part0", "q_rem",
                 "q_part1", "q_part2", "k_rot_done", "k_full", "k_part0", "k_rem", "k_part1", "k_part2")
        pj = {k: sem("p_" + k) for k in KINDS}
        part_stored = [[sem(f"{w}_parts_stored_{c}") for c in range(2)] for w in "qk"]
        PART_DMAS = (1, 5)
        padded = sem("padded")
        stack = [sem(f"stack_loaded_{k}") for k in range(NG)]
        mrow = [sem(f"max_rows_loaded_{k}") for k in range(2)]
        ones_loaded = sem("ones_loaded")
        ring_full, ring_used = sem("ring_full"), sem("ring_used")
        score_done, exp_done, av_done = sem("score_done"), sem("exp_done"), sem("av_done")
        o_copied, mx_ready, m_split = sem("o_copied"), sem("mx_ready"), sem("m_split")
        LEAD = (12, 10)

        def order(layer):
            units = B * NG * NT
            lead = LEAD[layer]
            seq = []
            for s in range(-lead, units + NT):
                n, j = divmod(s, NT)
                u = s + lead
                for h in range(HG):
                    for c in range(2):
                        if 0 <= s < units and queries(layer, j, c)[0] < 512 * (c + 1):
                            seq.append(("S", (s, h, c)))
                        if u < units and c < chunks(layer, u % NT):
                            seq.append(("A", (u, h, c)))
                        if c == 0 and h % 2 and 0 < s <= units:
                            seq.append(("V", (s - 1, h // 2)))
                    if h == 0 and u % NT == 0 and 0 < u // NT <= B * NG:
                        seq.append(("M", u // NT - 1))
                if u == units + 1:
                    seq.append(("L", 0))
                if j == 1 and n > 0:
                    seq += [("O", (n - 1, 0)), ("O", (n - 1, 1))]
                if j == 3 and n > 0 and n % NG == 0:
                    seq += [("N", (n // NG - 1, 0)), ("N", (n // NG - 1, 1))]
                if j == 5 and n > 0 and n % NG == 0:
                    seq += [("Y", (n // NG - 1, 0)), ("Y", (n // NG - 1, 1))]
            return seq + [("L", 1)]

        def queries(layer, kt, c):
            lo = c * 512 if layer else max(kt * P, c * 512)
            return lo, (c + 1) * 512

        RING = (3, 6, 7)
        SCORES = 3

        def ring_places(layer):
            place, r, q = {}, 0, 0
            for kind, k in order(layer):
                if kind in "AMONY":
                    place[kind, k] = r
                    r += 1
                elif kind == "S":
                    place[kind, k] = q
                    q += 1
                    place["scored", k[0]] = q
            return place, r, q

        def chunks(layer, qt):
            return 2 if layer or qt >= 4 else 1

        places = [ring_places(k) for k in range(2)]
        ring_base = [0, places[0][1]]
        score_base = [0, places[0][2]]
        UNITS = B * NG * NT

        def attention(layer):
            place = {k: v + (score_base if k[0] in ("S", "scored") else ring_base)[layer]
                     for k, v in places[layer][0].items()}
            s0 = layer * UNITS
            n0 = layer * B * NG
            causal = layer == 0

            def ring_bank(r):
                return RING[r % len(RING)]

            def scored(n):
                return place["scored", NT * (n + 1) - 1]

            @block.sync
            def _(sp):
                for b in range(B):
                    for c in range(2):
                        cols = slice(c * C, (c + 1) * C)
                        item = layer * 4 + 2 * b + c
                        sp.wait_ge(pj["q_part2"], item + 1)
                        sp.dma_start(q_dram[layer, b, :, :, cols], parts[0][c]).then_inc(part_stored[0][c], 16)
                        sp.wait_ge(pj["k_part2"], item + 1)
                        for m in range(PARTS):
                            sp.dma_start(k_dram[layer, b, m, :, 0:PARTS - m, cols], parts[1][c][:, m:PARTS, :]) \
                              .then_inc(part_stored[1][c], 16)
                            if m:
                                sp.dma_start(k_dram[layer, b, m, :, PARTS - m:PARTS, cols], parts[1][c][:, 0:m, :]) \
                                  .then_inc(part_stored[1][c], 16)
                    for w in range(2):
                        for c in range(2):
                            sp.wait_ge(part_stored[w][c], 16 * PART_DMAS[w] * (layer * B + b + 1))
                    for g in range(NG):
                        n = b * NG + g
                        if n0 + n >= NG:
                            sp.wait_ge(score_done, score_base[1] if n < NG else scored(n - NG))
                        hs = slice(g * HG, (g + 1) * HG)
                        for m in range(PARTS):
                            rows = slice(PARTS * AD * m, PARTS * AD * (m + 1))
                            for dst, src in ((Qs, q_dram[layer, b]), (Ks, k_dram[layer, b, m])):
                                sp.dma_start(dst[rows, g], src.rearrange("(h d) i t -> (d i) h t", d=AD)[:, hs, :]) \
                                  .then_inc(stack[g], 16)
                sp.wait_ge(score_done, scored(B * NG - 2))
                if layer:
                    sp.dma_start(tw, d["t_w"]).then_inc(load5, 16)
                else:
                    for t, src in ((gate, d["e_gate"]), (enorm, d["k_norm"]), (w1, d["e_w1"]), (w2, d["e_w2"]),
                                   (b1, d["e_b1"]),
                                   (b2.rearrange("p e o -> p (e o)"), d["e_b2"].to_broadcast([P, NE * P])),
                                   (gateb, d["e_gateb"].to_broadcast([P, NE]))):
                        sp.dma_start(t, src).then_inc(load3, 16)
                if not layer:
                    barrier(sp, 2)

            @block.gpsimd
            def _(pool):
                for n in range(B * NG):
                    pool.wait_ge(m_split, n0 + n + 1)
                    if n0 + n >= NG:
                        pool.wait_ge(score_done, score_base[1] if n < NG else scored(n - NG))
                    for i in range(PARTS):
                        row = Qs[SROWS + i:SROWS + i + 1, n % NG].rearrange("o h (j q) -> o (h j) q", q=P)
                        nc.gpsimd.dma_start(row, nmp[n % 2][:, i, :]).then_inc(mrow[n % 2], 16)
                if not layer:
                    barrier(pool, 2)

            @block.tensor
            def _(pe):
                for kind in ("q_full", "k_full", "v_kept"):
                    pe.wait_ge(pj[kind], 4 * layer + 4)
                for kind, k in order(layer):
                    if kind == "A":
                        u, h, c = k
                        n, qt = divmod(u, NT)
                        if qt == 0 and h == 0:
                            pe.wait_ge(stack[n % NG], 2 * PARTS * 16 * ((n0 + n) // NG + 1))
                        r = place[kind, k]
                        ready(pe, ring_used, r - len(RING) + 1)
                        end = min((c + 1) * 512, (qt + 1) * P) if causal else (c + 1) * 512
                        bk = bank(ring_bank(r))
                        diag = causal and end == (qt + 1) * P and end <= (c + 1) * 512 and qt // 4 == c
                        corner = not causal and (qt, c) in ((0, 1), (NT - 1, 0))
                        ins = nc.tensor.matmul(
                            bk[:, 0:end - c * 512], Qs[0:SROWS, n % NG, h, qt * P:(qt + 1) * P],
                            Ks[0:SROWS, n % NG, h, c * 512:end], start=True, stop=not (diag or corner))
                        if diag:
                            o = qt * P - c * 512
                            ins = nc.tensor.matmul(bk[:, o:o + P], identb, masks[:, 0, :],
                                                   start=False, stop=True)
                        if corner:
                            o, m = (384, 2) if qt == 0 else (0, 3)
                            ins = nc.tensor.matmul(bk[:, o:o + P], identb, masks[:, m, :],
                                                   start=False, stop=True)
                        ins.then_inc(ring_full, 1)
                    elif kind == "M":
                        r = place[kind, k]
                        pe.wait_ge(mx_ready, n0 + k + 1)
                        ready(pe, ring_used, r - len(RING) + 1)
                        nc.tensor.transpose(PS[0:HG * NT, ring_bank(r), 0:P], mx[k % 2][:, 0, :], ident) \
                          .then_inc(ring_full, 1)
                    elif kind == "S":
                        u, h, c = k
                        n, kt = divmod(u, NT)
                        if kt == 0 and h == 0 and c == 0:
                            if n == 0:
                                pe.wait_ge(ones_loaded, 16 * (layer + 1))
                            pe.wait_ge(mrow[n % 2], 48 * ((n0 + n) // 2 + 1))
                        q = place[kind, k]
                        bk = bank(q % SCORES)
                        ready(pe, exp_done, q - SCORES + 1)
                        lo, hi = queries(layer, kt, c)
                        o = lo - c * 512
                        diag = causal and kt // 4 == c
                        corner = not causal and (kt, c) in ((0, 1), (NT - 1, 0))
                        ins = nc.tensor.matmul(
                            bk[:, o:512], Ks[0:MROWS, n % NG, h, kt * P:(kt + 1) * P],
                            Qs[0:MROWS, n % NG, h, lo:hi], start=True, stop=not (diag or corner))
                        if diag:
                            ins = nc.tensor.matmul(bk[:, o:o + P], identb, masks[:, 1, :],
                                                   start=False, stop=True)
                        if corner:
                            o, m = (384, 2) if kt == 0 else (0, 3)
                            ins = nc.tensor.matmul(bk[:, o:o + P], identb, masks[:, m, :],
                                                   start=False, stop=True)
                        ins.then_inc(score_done, 1)
                    elif kind == "V":
                        u, c = k
                        n, kt = divmod(u, NT)
                        b, g = divmod(n, NG)
                        if c == 0:
                            pe.wait_ge(exp_done, place["scored", u])
                            if kt == 0:
                                ready(pe, o_copied, n0 + n)
                        lo, hi = queries(layer, kt, c)
                        if lo < hi:
                            last = kt == (4 * c + 3 if causal else NT - 1)
                            for h in range(HG):
                                ins = nc.tensor.matmul(
                                    PS[h * VW:(h + 1) * VW, 4 + c, lo - c * 512:hi - c * 512],
                                    V[:, b, kt, HG * g + h, :], Pr[u % 2][:, h, lo:hi],
                                    start=(kt == 0), stop=last)
                        if c == 1:
                            ins.then_inc(av_done, 1)
                    elif kind == "O":
                        n, c = k
                        r = place[kind, k]
                        pe.wait_ge(o_copied, n0 + n + 1)
                        ready(pe, ring_used, r - len(RING) + 1)
                        for t in range(4):
                            ins = nc.tensor.transpose(bank(ring_bank(r))[:, t * P:(t + 1) * P],
                                                      osb[:, c, t * P:(t + 1) * P], ident)
                        ins.then_inc(ring_full, 1)
                    elif kind == "N":
                        b, c = k
                        r = place[kind, k]
                        pe.wait_ge(ring_used, max(r - len(RING) + 1, place["O", (NG * (b + 1) - 1, 1)] + 1))
                        for t in range(4):
                            ins = nc.tensor.transpose(bank(ring_bank(r))[:, t * P:(t + 1) * P], On[:, 4 * c + t, :], ident)
                        ins.then_inc(ring_full, 1)
                    elif kind == "Y":
                        b, c = k
                        r = place[kind, k]
                        pe.wait_ge(ring_used, max(r - len(RING) + 1, place["N", k] + 1))
                        for t in range(4):
                            ins = nc.tensor.matmul(bank(ring_bank(r))[:, t * P:(t + 1) * P],
                                                   OT[:, c * 512 + t * P:c * 512 + (t + 1) * P], wout,
                                                   start=True, stop=True)
                        ins.then_inc(ring_full, 1)
                if not layer:
                    barrier(pe, 2)

            @block.scalar
            def _(act):
                link = chain(act, act_step)
                for kind, k in order(layer):
                    if kind == "S":
                        u, h, c = k
                        q = place[kind, k]
                        lo, hi = queries(layer, u % NT, c)
                        if h == 0:
                            ready(act, av_done, s0 + u - 1)
                        act.wait_ge(score_done, q + 1)
                        nc.scalar.activation(Pr[u % 2][:, h, lo:hi], bank(q % SCORES)[:, lo - c * 512:512],
                                             ACT.Exp).then_inc(exp_done, 1)
                    elif kind == "V" and k[0] % NT == NT - 1 and k[1] == 1:
                        n = k[0] // NT
                        act.wait_ge(av_done, s0 + k[0] + 1)
                        if n:
                            act.wait_ge(ring_full, place["O", (n - 1, 1)] + 1)
                        nc.scalar.activation(osb.rearrange("p c q -> p (c q)"), pair(2), ACT.Copy) \
                          .then_inc(o_copied, 1)
                    elif kind == "Y" and not layer and k[1] == 1:
                        b = k[0]
                        act.wait_ge(ring_used, place["Y", k] + 1)
                        for i in range(b * NT, (b + 1) * NT):
                            ins = nc.scalar.activation(sq, U[:, i, :], ACT.Square, accum_out=xss[:, i:i + 1])
                            if i % NT < NT - 1:
                                link(ins)
                            else:
                                ins.then_inc(u_squared, 1)
                                act.wait_ge(u_squared, b + 1)
                if not layer:
                    barrier(act, 2)

            @block.vector
            def _(dve):
                v_ = nc.vector
                link = chain(dve, dve_step)
                for kind, k in order(layer):
                    if kind == "A":
                        u, h, c = k
                        n, qt = divmod(u, NT)
                        r = place[kind, k]
                        end = min(512, (qt + 1) * P - c * 512) if causal else 512
                        dve.wait_ge(ring_full, r + 1)
                        v_.tensor_reduce(mx[n % 2][:, c, h * NT + qt:h * NT + qt + 1],
                                         bank(ring_bank(r))[:, 0:end], AX.X, ALU.max).then_inc(ring_used, 1)
                        if qt == NT - 1 and h == HG - 1 and c == 1:
                            dve.wait_ge(ring_used, r + 1)
                            both = [mx[n % 2][:, c, :].rearrange("p (h q) -> p h q", h=HG)[:, :, (4 if causal else 0):]
                                    for c in range(2)]
                            v_.tensor_tensor(both[0], both[0], both[1], ALU.max).then_inc(mx_ready, 1)
                    elif kind == "M":
                        r = place[kind, k]
                        dve.wait_ge(ring_full, r + 1)
                        ready(dve, mrow[k % 2], 48 * ((n0 + k) // 2))
                        row = PS[0:HG * NT, ring_bank(r), 0:P]
                        part = [nmp[k % 2][:, i, :] for i in range(PARTS)]
                        link(v_.tensor_scalar(part[0], row, -1.0, None, ALU.mult))
                        v_.scalar_tensor_tensor(out=nm1, in0=row, scalar=-1.0, in1=part[0],
                                                op0=ALU.mult, op1=ALU.subtract).then_inc(ring_used, 1)
                        dve.wait_ge(ring_used, r + 1)
                        link(v_.tensor_copy(part[1], nm1))
                        v_.tensor_tensor(part[2], nm1, part[1], ALU.subtract).then_inc(m_split, 1)
                    elif kind == "O":
                        n, c = k
                        g = n % NG
                        r = place[kind, k]
                        dve.wait_ge(ring_full, r + 1)
                        o4 = bank(ring_bank(r)).rearrange("p (t h e) -> p t h e", t=4, h=HG)
                        link(v_.reciprocal(rden, o4[:, :, :, AD]))
                        dst = On[:, 4 * c:4 * c + 4, HG * AD * g:HG * AD * (g + 1)]
                        v_.tensor_tensor(dst.rearrange("p t (h e) -> p t h e", h=HG), o4[:, :, :, 0:AD],
                                         rden.unsqueeze(3).to_broadcast([P, 4, HG, AD]),
                                         ALU.mult).then_inc(ring_used, 1)
                        dve.wait_ge(ring_used, r + 1)
                    elif kind == "N":
                        b, c = k
                        r = place[kind, k]
                        dve.wait_ge(ring_full, r + 1)
                        v_.tensor_copy(OT[:, c * 512:(c + 1) * 512], bank(ring_bank(r))).then_inc(ring_used, 1)
                    elif kind == "Y":
                        b, c = k
                        r = place[kind, k]
                        dve.wait_ge(ring_full, r + 1)
                        t = slice(b * NT + 4 * c, b * NT + 4 * c + 4)
                        y = bank(ring_bank(r)).rearrange("p (t e) -> p t e", t=4)
                        v_.tensor_tensor((X if layer else U)[:, t, :], y, X[:, t, :], ALU.add).then_inc(ring_used, 1)
                        if not layer and b and c:
                            dve.wait_ge(u_squared, B)
                            link(v_.tensor_scalar(xss, xss, 1.0 / P, 1e-6, ALU.mult, ALU.add))
                            link(rsqrt(v_, link, xrr, xss, newt[:, 0, :]))
                    elif kind == "L" and layer:
                        dve.wait_ge(ring_used, place["Y", (k, 1)] + 1)
                        statistics(v_, link, k * NT, (k + 1) * NT)
                        layer_norm(dve, link, 1e-5, k * NT, (k + 1) * NT).then_inc(x2_ready, 1)
                        dve.wait_ge(x2_ready, k + 1)
                if not layer:
                    barrier(dve, 2)

        orders = ("""
            normed:0 turned:0 normed:1 turned_copied:0 normed:2 q_made:0 turned:1 q_rot_done:0 lat_made:0
            turned_copied:1 normed:3 q_full:0 q_made:1 q_part0:0 lat_made:1 q_rot_done:1 turned:2 lat_normed:0
            q_full:1 q_part0:1 turned_copied:2 turned:3 q_made:2 turned_copied:3 lat_turned:0 q_rot_done:2
            lat_made:2 lat_copied:0 q_rem:0 q_made:3 q_part1:0 q_rem:1 q_full:2 q_part2:0 q_part1:1 lat_made:3
            q_part2:1 k_made:0 q_rot_done:3 lat_turned:1 k_rot_done:0 q_full:3 v_made:0 lat_copied:1
            lat_normed:1 k_full:0 q_part0:2 k_made:1 k_part0:0 v_kept:0 k_rem:0 k_part1:0 k_part2:0
            k_rot_done:1 lat_turned:2 v_made:1 lat_copied:2 k_full:1 lat_turned:3 k_part0:1 k_made:2
            lat_copied:3 k_rem:1 v_kept:1 k_rot_done:2 k_part1:1 q_part0:3 k_part2:1 k_made:3 k_full:2 v_made:2
            k_part0:2 k_rot_done:3 v_kept:2 q_rem:2 v_made:3 k_full:3 q_rem:3 v_kept:3 k_rem:2 k_part0:3
            k_part1:2 k_rem:3 k_part2:2 k_part1:3 q_part1:2 q_part1:3 q_part2:2 k_part2:3 q_part2:3
        """, """
            turned:0 turned_copied:0 turned:1 k_made:0 turned_copied:1 k_full:0 k_made:1 k_part0:0 q_made:0
            k_full:1 k_rem:0 q_full:0 q_made:1 k_part0:1 q_part0:0 v_made:0 k_rem:1 q_full:1 k_part1:0 q_rem:0
            v_made:1 q_part0:1 k_part2:0 k_part1:1 q_rem:1 turned:2 q_part1:0 k_part2:1 q_part1:1 q_part2:0
            turned_copied:2 q_part2:1 turned:3 v_kept:0 k_made:2 turned_copied:3 v_kept:1 q_made:2 k_full:2
            k_made:3 k_part0:2 q_full:2 k_rem:2 q_made:3 k_full:3 v_made:2 k_part0:3 q_full:3 q_part0:2 k_rem:3
            v_kept:2 v_made:3 q_part0:3 k_part1:2 v_kept:3 k_part1:3 k_part2:2 q_rem:2 q_part1:2 q_rem:3
            k_part2:3 q_part2:2 q_part1:3 q_part2:3
        """)

        def schedule(layer):
            return [(k, int(m)) for k, m in (item.split(":") for item in orders[layer].split())]

        def projector(layer, eng):
            def wait(kind, m):
                if m >= 0:
                    per = B if kind == "lat_normed" else 4
                    eng.wait_ge(pj[kind], per * layer + m + 1)

            def made(ins, kind):
                ins.then_inc(pj[kind], 1)
            return wait, made

        def stored_wait(eng, layer, w, m):
            if layer * 4 + m >= 2:
                eng.wait_ge(part_stored[w][m % 2], 16 * PART_DMAS[w] * (layer * B + m // 2))

        def first_part(eng, wait, made, layer, w, m):
            x = "qk"[w]
            wait(x + "_full", m)
            stored_wait(eng, layer, w, m)
            made(nc.scalar.activation(parts[w][m % 2][:, 0, :], kq[w][m % 2], ACT.Copy), x + "_part0")

        def first_rest(e_, wait, made, w, m):
            x = "qk"[w]
            wait(x + "_part0", m)
            wait(x + "_part1", m - 2)
            wait(x + "_part2", m - 2)
            made(e_.tensor_tensor(rem[w][m % 2], kq[w][m % 2], parts[w][m % 2][:, 0, :], ALU.subtract), x + "_rem")

        def second_part(wait, made, w, m):
            x = "qk"[w]
            wait(x + "_rem", m)
            made(nc.scalar.activation(parts[w][m % 2][:, 1, :], rem[w][m % 2], ACT.Copy), x + "_part1")

        def third_part(e_, wait, made, w, m):
            x = "qk"[w]
            wait(x + "_part1", m)
            made(e_.tensor_tensor(parts[w][m % 2][:, 2, :], rem[w][m % 2], parts[w][m % 2][:, 1, :],
                                  ALU.subtract), x + "_part2")

        def load_ones(sp):
            sp.dma_start(Ks[SROWS:MROWS].rearrange("p g h t -> p (g h t)").bitcast(F32), d["c_ones"]) \
              .then_inc(ones_loaded, 16)

        def pad_values(pool):
            pads = V[:, :, :, :, AD:VW].rearrange("p b t h e -> p (b t h) e")
            nc.gpsimd.memset(pads[:, :, 0:1], 1.0)
            nc.gpsimd.memset(pads[:, :, 1:VW - AD], 0.0).then_inc(padded, 1)

        def latent_projections():
            @block.sync
            def _(sp):
                load_ones(sp)

            @block.gpsimd
            def _(pool):
                g_ = nc.gpsimd
                wait, made = projector(0, pool)
                pad_values(pool)
                for kind, m in schedule(0):
                    if kind in ("q_full", "k_full"):
                        w = "qk".index(kind[0])
                        x = "qk"[w]
                        wait("q_rot_done" if w == 0 else "k_rot_done", m)
                        wait(x + "_rem", m - 2)
                        made(g_.tensor_tensor(kq[w][m % 2], rot1[w], rot2[w], ALU.add), kind)
                    elif kind == "k_rem":
                        first_rest(g_, wait, made, 1, m)
                    elif kind == "k_part2":
                        third_part(g_, wait, made, 1, m)

            @block.tensor
            def _(pe):
                wait, made = projector(0, pe)
                pe.wait_ge(load2, 144)
                for kind, m in schedule(0):
                    c = m % 2
                    if kind == "turned":
                        wait("normed", m)
                        wait("turned_copied", m - 1)
                        for t in range(4):
                            ins = nc.tensor.transpose(bank(0)[:, t * P:(t + 1) * P], hn_[c][:, t, :], ident)
                        made(ins, kind)
                    elif kind == "q_made":
                        wait("turned_copied", m)
                        wait("q_rot_done", m - 1)
                        for z in range(2):
                            ins = nc.tensor.matmul(bank(1 + z), wq2[:, z, :], hT[c], start=True, stop=True)
                        made(ins, kind)
                    elif kind == "lat_made":
                        if m == 2:
                            wait("lat_normed", 0)
                        for t in range(4):
                            ins = nc.tensor.matmul(bank(3)[:, (4 * c + t) * KV:(4 * c + t + 1) * KV],
                                                   hT[c][:, t * P:(t + 1) * P], wdkv, start=True, stop=True)
                        made(ins, kind)
                    elif kind == "lat_turned":
                        wait("lat_normed", m // 2)
                        wait("lat_copied", m - 1)
                        for t in range(4):
                            ins = nc.tensor.transpose(bank(7)[0:KV, t * P:(t + 1) * P], lat[:, 4 * c + t, :], ident)
                        made(ins, kind)
                    elif kind == "k_made":
                        wait("lat_copied", m)
                        wait("k_rot_done", m - 1)
                        for z in range(2):
                            ins = nc.tensor.matmul(bank(4 + z), wuk2[:, z, :], latT[c], start=True, stop=True)
                        made(ins, kind)
                    elif kind == "v_made":
                        wait("v_kept", m - 1)
                        for t in range(4):
                            ins = nc.tensor.matmul(bank(6)[:, t * P:(t + 1) * P], latT[c][:, t * P:(t + 1) * P], wuv,
                                                   start=True, stop=True)
                        made(ins, kind)

            @block.scalar
            def _(act):
                s_ = nc.scalar
                wait, made = projector(0, act)
                link = chain(act, act_step)
                act.wait_ge(load2, 144)
                for kind, m in schedule(0):
                    c = m % 2
                    if kind == "turned_copied":
                        wait("turned", m)
                        wait("lat_made", m - 2)
                        made(s_.activation(hT[c], bank(0), ACT.Copy, scale=norms[:, 0:1]), kind)
                    elif kind == "lat_copied":
                        wait("lat_turned", m)
                        wait("v_made", m - 2)
                        made(s_.activation(latT[c], bank(7)[0:KV, :], ACT.Identity, scale=lnp[:, 0:1],
                                           bias=lnp[:, 1:2]), kind)
                    elif kind == "v_kept":
                        wait("v_made", m)
                        act.wait_ge(padded, 1)
                        made(s_.activation(V[:, m // 2, 4 * c:4 * c + 4, :, 0:AD].rearrange("p t h e -> p (t h) e"),
                                           bank(6).rearrange("p (x e) -> p x e", e=AD), ACT.Copy), kind)
                    elif kind in ("q_part0", "k_part0"):
                        first_part(act, wait, made, 0, "qk".index(kind[0]), m)
                    elif kind in ("q_part1", "k_part1"):
                        second_part(wait, made, "qk".index(kind[0]), m)

            @block.vector
            def _(dve):
                v_ = nc.vector
                wait, made = projector(0, dve)
                link = chain(dve, dve_step)
                dve.wait_ge(load2, 144)
                for kind, m in schedule(0):
                    b, c = divmod(m, 2)
                    if kind == "normed":
                        if m == 2:
                            dve.wait_ge(x_squared, b + 1)
                            t = slice(b * NT, (b + 1) * NT)
                            link(v_.tensor_scalar(xss[:, t], xss[:, t], 1.0 / P, 1e-6, ALU.mult, ALU.add))
                            link(rsqrt(v_, link, xrr[:, t], xss[:, t], newt[:, 0, t]))
                        wait("turned", m - 2)
                        for t in range(4):
                            i = 4 * m + t
                            ins = v_.tensor_scalar(hn_[c][:, t, :], X[:, i, :], xrr[:, i:i + 1], None, ALU.mult)
                        made(ins, kind)
                    elif kind == "lat_normed":
                        wait("lat_made", 2 * m + 1)
                        for t in range(NT):
                            ins = v_.bn_stats(lst[:, t, :], bank(3)[:, t * KV:(t + 1) * KV])
                        link(ins)
                        for t in range(NT):
                            ins = v_.bn_aggr(lmv[:, t, :], lst[:, t, :])
                        link(ins)
                        link(v_.tensor_scalar(lvar, lmv[:, :, 1], 1e-5, None, ALU.add))
                        link(rsqrt(v_, link, lrs, lvar, ltmp))
                        wait("lat_turned", 2 * m - 1)
                        for t in range(NT):
                            ins = v_.tensor_scalar(lat[:, t, :], bank(3)[:, t * KV:(t + 1) * KV], lmv[:, t, 0:1],
                                                   lrs[:, t:t + 1], ALU.subtract, ALU.mult)
                        made(ins, kind)
                    elif kind in ("q_rot_done", "k_rot_done"):
                        w = "qk".index(kind[0])
                        x = "qk"[w]
                        scale = 1.0 if w else QSCALE
                        wait(x + "_made", m)
                        wait(x + "_full", m - 1)
                        cols = slice(c * C, (c + 1) * C)
                        v_.scalar_tensor_tensor(out=rot1[w], in0=bank(3 * w + 1), scalar=scale, in1=tab_cos[:, cols],
                                                op0=ALU.mult, op1=ALU.mult)
                        made(v_.scalar_tensor_tensor(out=rot2[w], in0=bank(3 * w + 2), scalar=scale,
                                                     in1=tab_sin[:, cols], op0=ALU.mult, op1=ALU.mult), kind)
                    elif kind == "q_rem":
                        first_rest(v_, wait, made, 0, m)
                    elif kind == "q_part2":
                        third_part(v_, wait, made, 0, m)

        def biased_projections():
            @block.gpsimd
            def _(pool):
                wait, made = projector(1, pool)
                pad_values(pool)
                for kind, m in schedule(1):
                    if kind == "k_rem":
                        first_rest(nc.gpsimd, wait, made, 1, m)
                    elif kind == "k_part2":
                        third_part(nc.gpsimd, wait, made, 1, m)

            @block.sync
            def _(sp):
                load_ones(sp)

            @block.tensor
            def _(pe):
                wait, made = projector(1, pe)
                for kind, m in schedule(1):
                    c = m % 2
                    if kind == "turned":
                        wait("turned_copied", m - 1)
                        for t in range(4):
                            ins = nc.tensor.transpose(bank(0)[:, t * P:(t + 1) * P], X[:, 4 * m + t, :], ident)
                        made(ins, kind)
                        if m == 0:
                            pe.wait_ge(load4, 64)
                    elif kind in ("q_made", "k_made"):
                        w = "qk".index(kind[0])
                        wait("turned_copied", m)
                        wait(kind[0] + "_full", m - 2)
                        made(nc.tensor.matmul(bank(1 + 2 * w + c), wqkv[:, w, :], hT[c], start=True, stop=True), kind)
                    elif kind == "v_made":
                        wait("v_kept", m - 2)
                        for t in range(4):
                            ins = nc.tensor.matmul(bank(5 + c)[:, t * P:(t + 1) * P], hT[c][:, t * P:(t + 1) * P],
                                                   wqkv[:, 2, :], start=True, stop=True)
                        made(ins, kind)

            @block.scalar
            def _(act):
                s_ = nc.scalar
                wait, made = projector(1, act)
                for kind, m in schedule(1):
                    c = m % 2
                    if kind == "turned_copied":
                        wait("turned", m)
                        wait("v_made", m - 2)
                        made(s_.activation(hT[c], bank(0), ACT.Copy), kind)
                        if m == 0:
                            act.wait_ge(load4, 64)
                    elif kind == "k_full":
                        wait("k_made", m)
                        wait("k_rem", m - 2)
                        made(s_.activation(kq[1][c], bank(3 + c), ACT.Identity, bias=bqk[:, 1:2]), kind)
                    elif kind in ("q_part0", "k_part0"):
                        first_part(act, wait, made, 1, "qk".index(kind[0]), m)
                    elif kind in ("q_part1", "k_part1"):
                        second_part(wait, made, "qk".index(kind[0]), m)

            @block.vector
            def _(dve):
                v_ = nc.vector
                wait, made = projector(1, dve)
                link = chain(dve, dve_step)
                dve.wait_ge(load4, 64)
                for kind, m in schedule(1):
                    b, c = divmod(m, 2)
                    if kind == "q_full":
                        wait("q_made", m)
                        wait("q_part0", m - 2)
                        made(v_.tensor_scalar(kq[0][c], bank(1 + c), bqk[:, 0:1], QSCALE, ALU.add, ALU.mult), kind)
                    elif kind == "q_rem":
                        first_rest(v_, wait, made, 0, m)
                    elif kind == "q_part2":
                        third_part(v_, wait, made, 0, m)
                    elif kind == "v_kept":
                        wait("v_made", m)
                        dve.wait_ge(padded, 2)
                        made(v_.tensor_tensor(V[:, b, 4 * c:4 * c + 4, :, 0:AD],
                                              bank(5 + c).rearrange("p (t h e) -> p t h e", t=4, e=AD),
                                              bv.rearrange("p (h e) -> p h e", e=AD).unsqueeze(1)
                                              .to_broadcast([P, 4, AH, AD]), ALU.add), kind)

        e_normed, e_turned, e_hT = (sem("e_" + k) for k in ("normed", "turned", "hT"))
        e_logits, e_onehot, e_based = (sem("e_" + k) for k in ("logits", "onehot", "based"))
        hid_done, hid_act, hid_dve = sem("hid_done"), sem("hid_act"), sem("hid_dve")
        ey_done, ey_used = sem("ey_done"), sem("ey_used")
        CH = B * T // 512
        HB = NE * EM

        def experts():
            @block.sync
            def _(sp):
                for t, name in ((wqkv, "a_wqkv"), (bqk, "a_bqk"), (wout, "a_wo")):
                    sp.dma_start(t, d[name]).then_inc(load4, 16)
                sp.dma_start(bv, d["a_bv"].to_broadcast([P, P])).then_inc(load4, 16)
                barrier(sp, 3)

            @block.scalar
            def _(act):
                s_ = nc.scalar
                act.wait_ge(load3, 112)
                for b in range(B):
                    act.wait_ge(e_turned, b + 1)
                    s_.activation(h2T[b], pair(b), ACT.Copy, scale=enorm[:, 1:2]).then_inc(e_hT, 1)
                for c in range(CH):
                    for k in range(0, HB, 2):
                        act.wait_ge(hid_done, c * HB + k + 1)
                        ready(act, ey_done, 4 * (c - 1))
                        s_.activation(hid[c % 2][:, k, :], bank(4 + k % 4), ACT.Relu,
                                      bias=b1[:, k:k + 1]).then_inc(hid_act, 1)
                barrier(act, 3)

            @block.gpsimd
            def _(pool):
                g_ = nc.gpsimd
                link = chain(pool, pool_step)
                for i in range(NTILE):
                    pool.wait_ge(e_onehot, i // NT + 1)
                    link(g_.tensor_tensor(base[:, i, :], X[:, i, :], U[:, i, :], ALU.add))
                    link(g_.tensor_tensor(bpick, b2, spread(onehot[:, i, :], NE, P), ALU.mult))
                    for e in range(NE):
                        ins = g_.tensor_tensor(base[:, i, :], base[:, i, :], bpick[:, e, :], ALU.add)
                        if e < NE - 1:
                            link(ins)
                    ins.then_inc(e_based, 1)
                    pool.wait_ge(e_based, i + 1)
                barrier(pool, 3)

            @block.tensor
            def _(pe):
                def turn(b):
                    pe.wait_ge(e_normed, b + 1)
                    for t in range(NT):
                        ins = nc.tensor.transpose(pair(b)[:, t * P:(t + 1) * P], hn[b][:, t, :], ident)
                    ins.then_inc(e_turned, 1)

                def logits(b):
                    pe.wait_ge(e_hT, b + 1)
                    for t in range(NT):
                        ins = nc.tensor.matmul(bank(2 * b)[:, t * NE:(t + 1) * NE], h2T[b][:, t * P:(t + 1) * P],
                                               gate, start=True, stop=True)
                    ins.then_inc(e_logits, 1)

                pe.wait_ge(load3, 112)
                for b in range(B):
                    turn(b)
                logits(0)
                for c in range(CH + 1):
                    for k in range(HB):
                        if c < CH:
                            r = c * HB + k
                            ready(pe, hid_dve if k % 2 else hid_act, r // 2 - 1)
                            nc.tensor.matmul(bank(4 + k % 4), w1[:, k * P:(k + 1) * P],
                                             h2T[c // 2][:, c % 2 * 512:(c % 2 + 1) * 512],
                                             start=True, stop=True).then_inc(hid_done, 1)
                        if c == 0 and k == HB // 2:
                            logits(1)
                        if c and k % 4 == 3:
                            t = 4 * (c - 1) + k // 4
                            if k == 3:
                                pe.wait_ge(hid_act, c * HB // 2)
                                pe.wait_ge(hid_dve, c * HB // 2)
                            if t < 4:
                                pe.wait_ge(e_onehot, t // 2 + 1)
                            ready(pe, ey_used, t - 3)
                            for m in range(HB):
                                e = m // EM
                                ins = nc.tensor.matmul(bank(t % 4)[:, e * P:(e + 1) * P],
                                                       hid[(c - 1) % 2][:, m, k // 4 * P:(k // 4 + 1) * P], w2[:, m, :],
                                                       start=(m % EM == 0), stop=(m % EM == EM - 1))
                            ins.then_inc(ey_done, 1)
                barrier(pe, 3)

            @block.vector
            def _(dve):
                v_ = nc.vector
                link = chain(dve, dve_step)

                def choose(b):
                    t = slice(b * NT, (b + 1) * NT)
                    hot, lg = onehot[:, t, :], logit[:, t, :]
                    dve.wait_ge(e_logits, b + 1)
                    link(v_.tensor_tensor(lg, bank(2 * b)[:, 0:NT * NE].rearrange("p (i e) -> p i e", e=NE),
                                          gateb.unsqueeze(1).to_broadcast([P, NT, NE]), ALU.add))
                    link(v_.tensor_reduce(top[:, t], lg, AX.X, ALU.max))
                    link(v_.tensor_tensor(hot, lg, spread(top[:, t], NT, NE), ALU.is_ge))
                    link(v_.tensor_scalar(left[:, t], hot[:, :, 0], -1.0, 1.0, ALU.mult, ALU.add))
                    for e in range(1, NE):
                        ins = v_.tensor_tensor(hot[:, :, e], hot[:, :, e], left[:, t], ALU.mult)
                        if e < NE - 1:
                            link(ins)
                            link(v_.tensor_tensor(left[:, t], left[:, t], hot[:, :, e], ALU.subtract))
                    ins.then_inc(e_onehot, 1)

                for b in range(B):
                    for t in range(NT):
                        i = b * NT + t
                        ins = v_.tensor_scalar(hn[b][:, t, :], U[:, i, :], xrr[:, i:i + 1], None, ALU.mult)
                    ins.then_inc(e_normed, 1)
                dve.wait_ge(load3, 112)
                for c in range(CH + 1):
                    for k in range(HB):
                        if c == 0 and k in (2, HB // 2 + 2):
                            choose(int(k > 2))
                        if c < CH and k % 2:
                            dve.wait_ge(hid_done, c * HB + k + 1)
                            ready(dve, ey_done, 4 * (c - 1))
                            v_.tensor_scalar(hid[c % 2][:, k, :], bank(4 + k % 4), b1[:, k:k + 1], 0.0,
                                             ALU.add, ALU.max).then_inc(hid_dve, 1)
                        if c and k % 4 == 3:
                            i = 4 * (c - 1) + k // 4
                            dve.wait_ge(ey_done, i + 1)
                            dve.wait_ge(e_based, i + 1)
                            for e in range(NE):
                                ins = v_.scalar_tensor_tensor(
                                    out=X[:, i, :] if e == NE - 1 else base[:, i, :], in0=bank(i % 4)[:, e * P:(e + 1) * P],
                                    scalar=onehot[:, i, e:e + 1], in1=base[:, i, :], op0=ALU.mult, op1=ALU.add)
                                if e < NE - 1:
                                    link(ins)
                            ins.then_inc(ey_used, 1)
                            dve.wait_ge(ey_used, i + 1)
                            link(v_.bn_stats(stats[:, i, :], X[:, i, :]))
                            link(v_.bn_aggr(mv[:, i, :], stats[:, i, :]))
                    if c == 2:
                        link(layer_norm(dve, link, 1e-5, 0, NT))
                    if c == 3:
                        link(layer_norm(dve, link, 1e-5, NT, NT + 4))
                link(layer_norm(dve, link, 1e-5, NT + 4, NTILE))
                barrier(dve, 3)

        t_abs, t_ones, t_sum, t_quant = (sem("t_" + k) for k in ("abs", "ones", "sum", "quant"))
        t_turned, t_copied, t_done, t_added = (sem("t_" + k) for k in ("turned", "copied", "done", "added"))
        t_normed, t_rstd, t_odd = sem("t_normed"), sem("t_rstd"), sem("t_odd")

        def ternary():
            last_score = score_base[1] + places[1][2]
            last_ring = ring_base[1] + places[1][1]

            @block.scalar
            def _(act):
                act.wait_ge(load5, 16)
                nc.scalar.activation(twp, tw, ACT.Abs, accum_out=tsum).then_inc(t_abs, 1)
                for q in range(4):
                    act.wait_ge(t_turned, q + 1)
                    nc.scalar.activation(t_xT[:, 4 * q:4 * q + 4, :], bank(q).rearrange("p (k t) -> p k t", k=4),
                                         ACT.Copy).then_inc(t_copied, 1)
                barrier(act, 4)

            @block.gpsimd
            def _(pool):
                pool.wait_ge(load5, 16)
                nc.gpsimd.memset(ones, 1.0).then_inc(t_ones, 1)
                for q in range(2):
                    pool.wait_ge(t_rstd, q + 1)
                    for i in range(8 * q + 1, 8 * q + 8, 2):
                        ins = nc.gpsimd.tensor_scalar(X[:, i, :], X[:, i, :], mv[:, i, 0:1], newt[:, 1, i:i + 1],
                                                      ALU.subtract, ALU.mult)
                    ins.then_inc(t_odd, 1)
                barrier(pool, 4)

            @block.tensor
            def _(pe):
                def turn(q):
                    for k in range(4):
                        ins = nc.tensor.transpose(bank(q)[:, k * P:(k + 1) * P], X[:, 4 * q + k, :], ident)
                    ins.then_inc(t_turned, 1)

                def product(q):
                    pe.wait_ge(t_copied, q + 1)
                    for k in range(4):
                        ins = nc.tensor.matmul(bank(4 + q)[:, k * P:(k + 1) * P], t_xT[:, 4 * q + k, :], tw,
                                               start=True, stop=True)
                    ins.then_inc(t_done, 1)

                pe.wait_ge(x2_ready, 1)
                pe.wait_ge(exp_done, last_score)
                pe.wait_ge(ring_used, last_ring)
                turn(0)
                turn(1)
                pe.wait_ge(t_abs, 1)
                pe.wait_ge(t_ones, 1)
                nc.tensor.matmul(bank(2)[:, 0:1], ones, tsum, start=True, stop=True).then_inc(t_sum, 1)
                pe.wait_ge(t_quant, 1)
                product(0)
                product(1)
                pe.wait_ge(x2_ready, 2)
                for q in (2, 3):
                    turn(q)
                for q in (2, 3):
                    product(q)
                barrier(pe, 4)

            @block.vector
            def _(dve):
                v_ = nc.vector
                link = chain(dve, dve_step)
                dve.wait_ge(t_sum, 1)
                link(v_.tensor_scalar(tsc, bank(2)[:, 0:1], 1.0 / (P * P), 1e-5, ALU.mult, ALU.max))
                link(v_.tensor_scalar(thalf, tsc, 0.5, None, ALU.mult))
                v_.tensor_scalar(twp, tw, thalf, None, ALU.is_gt)
                link(v_.tensor_scalar(twn, tw, -1.0, thalf, ALU.mult, ALU.is_gt))
                link(v_.tensor_tensor(twp, twp, twn, ALU.subtract))
                v_.tensor_scalar(tw, twp, tsc, None, ALU.mult).then_inc(t_quant, 1)
                for b in range(2):
                    for q in (2 * b, 2 * b + 1):
                        dve.wait_ge(t_done, q + 1)
                        t = slice(4 * q, 4 * q + 4)
                        v_.tensor_tensor(X[:, t, :], bank(4 + q).rearrange("p (k o) -> p k o", k=4), X[:, t, :],
                                         ALU.add).then_inc(t_added, 1)
                    dve.wait_ge(t_added, 2 * b + 2)
                    statistics(v_, link, 8 * b, 8 * b + 8)
                    t = slice(8 * b, 8 * b + 8)
                    link(v_.tensor_scalar(rstd[:, t], mv[:, t, 1], 1e-5, None, ALU.add))
                    rsqrt(v_, link, newt[:, 1, t], rstd[:, t], newt[:, 0, t]).then_inc(t_rstd, 1)
                    dve.wait_ge(t_rstd, b + 1)
                    for i in range(8 * b, 8 * b + 8, 2):
                        ins = v_.tensor_scalar(X[:, i, :], X[:, i, :], mv[:, i, 0:1], newt[:, 1, i:i + 1],
                                               ALU.subtract, ALU.mult)
                    ins.then_inc(t_normed, 1)
                barrier(dve, 4)

            @block.sync
            def _(sp):
                rows = out.rearrange("(n p) d -> p n d", p=P)
                for q in range(2):
                    sp.wait_ge(t_normed, q + 1)
                    sp.wait_ge(t_odd, q + 1)
                    sp.dma_start(rows[:, 8 * q:8 * q + 8, :], X[:, 8 * q:8 * q + 8, :]).then_inc(stored, 16)
                sp.wait_ge(stored, 32)
                barrier(sp, 4)

        if phases >= 2:
            latent_projections()
            attention(0)
        if phases >= 3:
            experts()
        if phases >= 4:
            biased_projections()
            attention(1)
        if phases >= 5:
            ternary()

        if phases == 5:
            return

        @block.sync
        def _(sp):
            res = U if phases == 2 else X
            sp.dma_start(out.rearrange("(n p) d -> p n d", p=P), res).then_inc(stored, 16)
            sp.wait_ge(stored, 16)


_OUT = (B, T, P)


def kernel(**inputs):
    import concourse.bacc as _bacc
    from concourse.bass_utils import run_bass_kernel_spmd as _run

    nc = _bacc.Bacc("TRN2", target_bir_lowering=False, num_devices=1)
    arrays = layout(inputs)
    d = {k: nc.dram_tensor(k, v.shape, mybir.dt.from_np(v.dtype), kind="ExternalInput").ap()
         for k, v in arrays.items()}
    out = nc.dram_tensor("out", (B * T, P), F32, kind="ExternalOutput").ap()
    build(nc, d, out)
    r = _run(nc, [arrays], core_ids=[0])
    return r.results[0]["out"].reshape(_OUT)
```

```python
from contextlib import ExitStack

import concourse.bass as bass
from concourse import mybir
import numpy as np

F32 = mybir.dt.float32
BF16 = mybir.dt.bfloat16
I32 = mybir.dt.int32
ALU = mybir.AluOpType
ACT = mybir.ActivationFunctionType
AX = mybir.AxisListType

P = 128
B, T = 2, 1024
NT = T // P
NTILE = B * NT
RH, RD, RV = 8, 64, 128
AH, AD = 16, 8
HG = 4
NG = AH // HG
VW = 32
KV = 64
NE, HID = 4, 512
EM = HID // P
PARTS = 3
SROWS = PARTS * PARTS * AD
MROWS = SROWS + PARTS
RSQRT_SEED = float(0x5F3759DF)
MASKED = -1e30
TWO_ONES = float(np.array([0x3F803F80], np.uint32).view(np.float32)[0])
NEG = -1e9
QSCALE = AD ** -0.5
C = 512
QT = C // P
MAXIMA = HG * QT
O_LAG, N_LAG, Y_LAG = 2, 4, 6
E_BY_O, E_BY_N, E_BY_Y, E_BY_H, EARLY = 4, 8, 12, 20, 24
PROBS = 3


def constants():
    f = np.float32
    c = {}
    c["c_ident"] = np.eye(P, dtype=f)
    t = np.arange(T, dtype=f)
    inv = (1.0 / np.power(f(10000.0), np.arange(0, RD, 2, dtype=f) / f(RD))).astype(f)
    ang = (t[:, None] * inv[None, :]).astype(f)
    by_tile = lambda a: np.ascontiguousarray(a.reshape(NT, P, -1).transpose(1, 0, 2))
    c["c_rcos"] = by_tile(np.cos(ang).astype(f))
    c["c_rsin"] = by_tile(np.sin(ang).astype(f))
    gamma = 1.0 - np.exp2(-5.0 - np.arange(RH, dtype=np.float64))
    i = np.arange(P, dtype=np.float64)
    slots = [2 * (s % 4) + s // 4 for s in range(RH)]
    c["c_gq"] = (gamma[None, :] ** (i[:, None] + 1) * RD ** -0.5).astype(f)
    c["c_gk"] = (gamma[None, :] ** (P - 1 - i[:, None])).astype(f)
    dm = np.zeros((P, RH, P))
    for s, h in enumerate(slots):
        dm[:, s, :] = (gamma[h] ** -(i[:, None] + 1)) * (i[None, :] >= i[:, None])
    c["c_decay"] = dm.astype(f)
    gc = np.zeros((P, 4, P))
    for h in range(RH):
        gc[(h % 2) * RD:(h % 2 + 1) * RD, h // 2, :] = gamma[h] ** P
    c["c_gchunk"] = gc.astype(f)
    half = AD // 2
    inv = (1.0 / np.power(f(10000.0), np.arange(half, dtype=f) / f(half))).astype(f)
    ang = (t[:, None] * inv[None, :]).astype(f)
    cos = np.cos(ang).astype(f).T
    sin = np.sin(ang).astype(f).T
    cos8 = np.concatenate([cos, cos])
    sin8 = np.concatenate([-sin, sin])
    c["c_kcos"] = np.tile(cos8, (AH, 1)).astype(f)
    c["c_ksin"] = np.tile(sin8, (AH, 1)).astype(f)
    m = np.zeros((P, 4, P), dtype=f)
    m[:, 0] = np.where(i[None, :] > i[:, None], MASKED, 0)
    m[:, 1] = np.where(i[:, None] > i[None, :], MASKED, 0)
    m[0, 2, P - 1] = NEG
    m[P - 1, 3, 0] = NEG
    c["c_mask"] = m
    c["c_ones"] = np.full((PARTS, NG * HG * T // 2), TWO_ONES, dtype=f)
    return c


def swap_halves(w):
    return w.reshape(AH, 2, AD // 2, -1)[:, ::-1].reshape(AH * AD, -1)


def layout(x):
    a = {k: np.asarray(v) for k, v in x.items()}
    slots = [2 * (s % 4) + s // 4 for s in range(RH)]
    c = np.ascontiguousarray
    d = dict(constants())
    d["x"] = a["L0_attn_x"].reshape(B * T, P)
    d["r_wqk"] = c(np.concatenate([a["L0_attn_Wq"], a["L0_attn_Wk"]]).T)
    byslot = lambda w: w.reshape(RH, RV, -1)[slots]
    d["r_wv"] = c(byslot(a["L0_attn_Wv"]).reshape(RH * RV, P).T)
    d["r_wg"] = c(byslot(a["L0_attn_Wg"]).reshape(RH * RV, P).T)
    d["r_wo"] = c(byslot(c(a["L0_attn_Wo"].T)).transpose(1, 0, 2))
    gn = np.stack([a["L0_attn_gn_weight"], a["L0_attn_gn_bias"]])
    d["r_gn"] = c(gn.reshape(2, RH, RV)[:, slots].transpose(2, 0, 1))
    n1, n2 = a["L0_ffn_norm1_w"], a["L0_ffn_norm2_w"]
    wq, wuk = a["L0_ffn_Wq"], a["L0_ffn_Wuk"]
    d["k_wq"] = c(np.stack([wq.T, swap_halves(wq).T], axis=1))
    d["k_wdkv"] = c(a["L0_ffn_Wdkv"].T)
    d["k_wuk"] = c(np.stack([wuk.T, swap_halves(wuk).T], axis=1))
    d["k_wuv"] = c(a["L0_ffn_Wuv"].T)
    d["k_wo"] = c(a["L0_ffn_Wo"].T)
    d["k_norm"] = c(np.stack([n1, n2], axis=1))
    d["k_ln"] = c(np.stack([a["L0_ffn_ln_g"], a["L0_ffn_ln_b"]], axis=1))
    d["e_gate"] = c(a["L0_ffn_gate_w"].T)
    d["e_gateb"] = a["L0_ffn_gate_b"].reshape(1, NE)
    d["e_w1"] = c(a["L0_ffn_W1"].reshape(NE * HID, P).T)
    d["e_b1"] = c(a["L0_ffn_b1"].reshape(NE * EM, P).T)
    w2 = a["L0_ffn_W2"].reshape(NE, P, EM, P)
    d["e_w2"] = c(w2.transpose(3, 0, 2, 1).reshape(P, NE * EM, P))
    d["e_b2"] = a["L0_ffn_b2"].reshape(1, NE * P)
    d["a_wqkv"] = c(np.stack([a["L1_attn_Wq"].T, a["L1_attn_Wk"].T, a["L1_attn_Wv"].T], axis=1))
    d["a_bqk"] = c(np.stack([a["L1_attn_bq"], a["L1_attn_bk"]], axis=1))
    d["a_bv"] = a["L1_attn_bv"].reshape(1, P)
    d["a_wo"] = c(a["L1_attn_Wo"].T)
    d["t_w"] = c(a["L1_ffn_weight"].T)
    return {k: np.ascontiguousarray(v) for k, v in d.items()}


class Arena:

    def __init__(self, tensor, words):
        self.tensor, self.words, self.at, self.most = tensor, words, 0, 0

    def tile(self, *shape, dtype=F32, rows=P):
        n = int(np.prod(shape))
        words = n if dtype != BF16 else (n + 1) // 2
        a = self.tensor[0:rows, self.at:self.at + words]
        self.at += words
        self.most = max(self.most, self.at)
        assert self.at <= self.words, (self.at, self.words)
        if dtype != F32:
            a = a.bitcast(dtype)
        if len(shape) == 1:
            return a
        names = " ".join("abcde"[:len(shape)])
        sizes = {k: s for k, s in zip("abcde", shape)}
        return a.rearrange(f"p ({names}) -> p {names}", **sizes)


def build(nc, d, out):
    ctx = ExitStack()
    with ctx:
        words = 52000
        A = Arena(ctx.enter_context(nc.sbuf_tensor("arena", [P, words], F32)), words)
        PS = ctx.enter_context(nc.psum_tensor("banks", [P, 8, 512], F32))

        def sem(name):
            return ctx.enter_context(nc.semaphore(name))

        def bank(b):
            return PS[:, b, :]

        def pair(q):
            return PS[:, 2 * q:2 * q + 2, :].rearrange("p b n -> p (b n)")

        q_dram = nc.dram_tensor("q_parts", [2, B, P, PARTS, T], BF16, kind="Internal").ap()
        k_dram = nc.dram_tensor("k_parts", [2, B, PARTS, P, PARTS, T], BF16, kind="Internal").ap()

        X = A.tile(NTILE, P)
        ident = A.tile(P)
        identb = A.tile(P, dtype=BF16)
        masks = A.tile(4, P, dtype=BF16)
        stats = A.tile(NTILE, 6)
        mv = A.tile(NTILE, 2)
        newton = A.tile(2, 16)
        rstd = A.tile(16)
        unused = A.tile(2)
        sq = A.tile(P)
        square_sum, inv_rms = A.tile(NTILE), A.tile(NTILE)
        U = A.tile(NTILE, P)
        common_end = A.at

        wqk, wv, wg = A.tile(2 * RH * RD), A.tile(RH * RV), A.tile(RH * RV)
        wo = A.tile(RH, P)
        gn = A.tile(2, RH)
        decay, gchunk = A.tile(RH * P), A.tile(4 * P)
        rcos, rsin = A.tile(NT, RD // 2), A.tile(NT, RD // 2)
        gq, gk = A.tile(RH), A.tile(RH)
        XT = A.tile(NTILE, P)
        rc, rs = A.tile(2 * RH * RD), A.tile(2 * RH * RD)
        rot = [A.tile(2 * RH * RD) for _ in range(2)]
        qd = [A.tile(RH * RD) for _ in range(2)]
        kd = [A.tile(RH * RD) for _ in range(2)]
        qkT = A.tile(8, P)
        vv = [A.tile(RH, P) for _ in range(2)]
        sm = A.tile(RH, P)
        state = [A.tile(4 * P) for _ in range(2)]
        stdec = A.tile(4 * P)
        oc = [A.tile(RH, P) for _ in range(2)]
        osum, gvar, grs, gnt = A.tile(RH), A.tile(RH), A.tile(RH), A.tile(2, RH)
        on = A.tile(RH, P)
        sig = A.tile(RH, P)
        ga = A.tile(RH, P)
        uu = A.tile(RH, P)
        maskf = A.tile(4, P)
        retention_end = A.at

        A.at = common_end
        Qs = A.tile(NG, 2, HG, C, dtype=BF16)
        Ks = A.tile(NG, HG, T, dtype=BF16)
        turned_at = A.at
        Pr = [A.tile(HG, C) for _ in range(PROBS)]
        V = A.tile(B, NT, AH, VW)
        values_end = A.at
        mx = [A.tile(2, MAXIMA) for _ in range(2)]
        nm1 = A.tile(P, rows=MAXIMA)
        nmp = [A.tile(PARTS, P, dtype=BF16, rows=MAXIMA) for _ in range(2)]
        osb = A.tile(2, 512)
        rden = A.tile(NT // 2, HG)
        On = A.tile(NT, P)
        OT = A.tile(T)
        kq = [[A.tile(C) for _ in range(2)] for _ in range(2)]
        rem = [[A.tile(C) for _ in range(2)] for _ in range(2)]
        parts = [[A.tile(PARTS, C, dtype=BF16) for _ in range(2)] for _ in range(2)]
        lat = osb[:, 0, :].rearrange("p (t e) -> p t e", e=KV)
        latT = [On[0:KV, 4 * c:4 * c + 4, :].rearrange("p t e -> p (t e)") for c in range(2)]
        lvar, lrs, ltmp = A.tile(NT), A.tile(NT), A.tile(NT)
        at = A.at
        A.at = turned_at
        xn, hT = [A.tile(4, P) for _ in range(2)], [A.tile(C) for _ in range(2)]
        rot1, rot2 = ([A.tile(C) for _ in range(2)] for _ in range(2))
        assert A.at <= turned_at + PROBS * HG * C
        A.at = at
        assert A.at >= retention_end
        wq2, wuk2 = A.tile(2, P), A.tile(2, P, rows=KV)
        wdkv, wuv = A.tile(KV), A.tile(P, rows=KV)
        wout = A.tile(P)
        norms, lnp = A.tile(2), A.tile(2, rows=KV)
        lst, lmv = A.tile(NT, 6), A.tile(NT, 2)
        latent_at = A.at
        tab_cos, tab_sin = A.tile(T), A.tile(T)
        A.at = latent_at
        wqkv, bqk, bv = A.tile(3, P), A.tile(2), A.tile(P)

        A.at = common_end
        w1, w2 = A.tile(NE * HID), A.tile(NE * EM, P)
        b1, b2 = A.tile(NE * EM), A.tile(NE, P)
        gate, gateb = A.tile(NE), A.tile(NE)
        enorm = A.tile(2)
        bpick = A.tile(NE, P)
        logit, top, left = A.tile(NTILE, NE), A.tile(NTILE), A.tile(NTILE)
        onehot = A.tile(NTILE, NE)
        slot = HG * T // 2
        assert A.at <= common_end + 3 * slot
        A.at = common_end + NG * slot
        hn = [A.tile(NT, P) for _ in range(B)]
        h2T = [A.tile(T) for _ in range(B)]
        assert A.at <= common_end + (NG + 3) * slot
        hid = [A.tile(NE * EM, 512) for _ in range(2)]
        base = A.tile(NTILE, P)
        assert A.at <= values_end

        A.at = common_end
        tw, twp, twn = A.tile(P), A.tile(P), A.tile(P)
        tsum, tsc, thalf = A.tile(1), A.tile(1), A.tile(1)
        ones = A.tile(P)
        t_xT = A.tile(NTILE, P)

        phase_end = sem("phase_end")
        load = {k: sem("load_" + k) for k in ("x_first", "x", "qk", "rest", "gv", "wo", "mask")}
        dve_step, pool_step, act_step = sem("dve_step"), sem("pool_step"), sem("act_step")
        xT_done, xT_copied = sem("xT_done"), sem("xT_copied")
        qk_done, rot_muls, rot_ready = sem("qk_done"), sem("rot_muls"), sem("rot_ready")
        k_rotated = sem("k_rotated")
        v_done, v_copied = sem("v_done"), sem("v_copied")
        qkT_done, qkT_copied = sem("qkT_done"), sem("qkT_copied")
        sc_done, sc_masked = sem("sc_done"), sem("sc_masked")
        delta_done, state_dec, state_ready = sem("delta_done"), sem("state_dec"), sem("state_ready")
        o_done, o_centred, o_squared = sem("o_done"), sem("o_centred"), sem("o_squared")
        o_rstd, o_normed = sem("o_rstd"), sem("o_normed")
        g_done, g_silu = sem("g_done"), sem("g_silu")
        onT_done, onT_affine, u_ready = sem("onT_done"), sem("onT_affine"), sem("u_ready")
        y_done, y_added = sem("y_done"), sem("y_added")
        stored = sem("stored")
        e_normed, e_onehot, e_based = (sem("e_" + k) for k in ("normed", "onehot", "based"))
        hid_done, hid_act, hid_dve = sem("hid_done"), sem("hid_act"), sem("hid_dve")
        ey_done, ey_used = sem("ey_done"), sem("ey_used")
        t_abs, t_ones, t_quant = sem("t_abs"), sem("t_ones"), sem("t_quant")
        t_rstd, t_normed, t_odd = sem("t_rstd"), sem("t_normed"), sem("t_odd")
        load_latent, x_ready, x_squared = sem("load_latent"), sem("x_ready"), sem("x_squared")

        counts = {}

        def chain(eng, s):
            def link(ins):
                counts[s.name] = counts.get(s.name, 0) + 1
                ins.then_inc(s, 1)
                eng.wait_ge(s, counts[s.name])
            return link

        def barrier(eng):
            eng.drain().then_inc(phase_end, 1)
            eng.wait_ge(phase_end, 5)

        def rsqrt(eng, link, y, v, tmp, fused=True):
            link(eng.tensor_scalar(y.bitcast(I32), v.bitcast(I32), -0.5, RSQRT_SEED, ALU.mult, ALU.add))
            for k in range(3):
                if fused:
                    link(eng.scalar_tensor_tensor(out=tmp, in0=y, scalar=-0.5, in1=y, op0=ALU.mult, op1=ALU.mult))
                    link(eng.tensor_tensor(tmp, tmp, v, ALU.mult))
                    ins = eng.scalar_tensor_tensor(out=y, in0=tmp, scalar=1.5, in1=y, op0=ALU.add, op1=ALU.mult)
                    if k < 2:
                        link(ins)
                    continue
                link(eng.tensor_tensor(tmp, y, y, ALU.mult))
                link(eng.tensor_tensor(tmp, tmp, v, ALU.mult))
                link(eng.tensor_scalar(tmp, tmp, -0.5, 1.5, ALU.mult, ALU.add))
                ins = eng.tensor_tensor(y, y, tmp, ALU.mult)
                if k < 2:
                    link(ins)
            return ins

        def heads(a, n=RH):
            return a.rearrange("p (h v) -> p h v", h=n)

        def spread(a, n, w):
            return a.unsqueeze(2).to_broadcast([P, n, w])

        def statistics(v_, link, lo, hi):
            for i in range(lo, hi):
                ins = v_.bn_stats(stats[:, i, :], X[:, i, :])
            link(ins)
            for i in range(lo, hi):
                ins = v_.bn_aggr(mv[:, i, :], stats[:, i, :])
            link(ins)

        def layer_norm(dve, link, eps, lo=0, hi=NTILE):
            v_ = nc.vector
            link(v_.tensor_scalar(rstd[:, lo:hi], mv[:, lo:hi, 1], eps, None, ALU.add))
            link(rsqrt(v_, link, newton[:, 1, lo:hi], rstd[:, lo:hi], newton[:, 0, lo:hi]))
            for i in range(lo, hi):
                ins = v_.tensor_scalar(X[:, i, :], X[:, i, :], mv[:, i, 0:1], newton[:, 1, i:i + 1],
                                       ALU.subtract, ALU.mult)
            return ins

        def squares_of_x(act, link, b):
            act.wait_ge(x_ready, b + 1)
            for i in range(b * NT, (b + 1) * NT):
                ins = nc.scalar.activation(sq, X[:, i, :], ACT.Square, accum_out=square_sum[:, i:i + 1])
                if i % NT < NT - 1:
                    link(ins)
                else:
                    ins.then_inc(x_squared, 1)
                    act.wait_ge(x_squared, b + 1)

        block = ctx.enter_context(nc.Block())

        @block.sync
        def _(sp):
            sp.dma_start(ident, d["c_ident"]).then_inc(load["x_first"], 16)
            x_in = d["x"].rearrange("(n p) d -> p n d", p=P)
            sp.dma_start(X[:, 0:4, :], x_in[:, 0:4, :]).then_inc(load["x_first"], 16)
            sp.dma_start(wqk, d["r_wqk"]).then_inc(load["qk"], 16)
            sp.dma_start(rcos, d["c_rcos"]).then_inc(load["qk"], 16)
            sp.dma_start(rsin, d["c_rsin"]).then_inc(load["qk"], 16)
            sp.dma_start(gq, d["c_gq"]).then_inc(load["qk"], 16)
            sp.dma_start(gk, d["c_gk"]).then_inc(load["qk"], 16)
            sp.dma_start(X[:, 4:, :], x_in[:, 4:, :]).then_inc(load["x"], 16)
            sp.dma_start(wv, d["r_wv"]).then_inc(load["gv"], 16)
            sp.dma_start(wg, d["r_wg"]).then_inc(load["gv"], 16)
            sp.dma_start(decay, d["c_decay"].rearrange("p s t -> p (s t)")).then_inc(load["rest"], 16)
            sp.dma_start(gchunk, d["c_gchunk"].rearrange("p s t -> p (s t)")).then_inc(load["rest"], 16)
            sp.dma_start(wo, d["r_wo"]).then_inc(load["wo"], 16)
            sp.dma_start(gn, d["r_gn"]).then_inc(load["wo"], 16)
            sp.dma_start(maskf, d["c_mask"]).then_inc(load["mask"], 16)
            for t, name in ((tab_cos, "c_kcos"), (tab_sin, "c_ksin"), (wq2, "k_wq"), (wdkv, "k_wdkv"),
                            (wuk2, "k_wuk"), (wuv, "k_wuv"), (wout, "k_wo"), (norms, "k_norm"), (lnp, "k_ln")):
                sp.dma_start(t, d[name]).then_inc(load_latent, 16)
            barrier(sp)

        def ready(e, s, n):
            if n >= 1:
                e.wait_ge(s, n)

        @block.tensor
        def _(pe):
            def turn_x(q):
                for k in range(4):
                    i = 4 * q + k
                    ins = nc.tensor.transpose(bank(2 + q)[:, k * P:(k + 1) * P], X[:, i, :], ident)
                ins.then_inc(xT_done, 1)

            pe.wait_ge(load["x_first"], 32)
            turn_x(0)
            pe.wait_ge(load["qk"], 80)
            pe.wait_ge(xT_copied, 1)
            for n in range(-1, NTILE + 2):
                this = 0 <= n < NTILE
                first, last = n % NT == 0, n % NT == NT - 1
                if this:
                    pe.wait_ge(rot_ready, n + 1)
                    ready(pe, y_added, n - 2)
                    ready(pe, state_ready, n)
                    for p4 in range(4):
                        nc.tensor.transpose(bank(6)[:, p4 * P:(p4 + 1) * P], qd[n % 2][:, p4 * P:(p4 + 1) * P], ident)
                    for p4 in range(4):
                        ins = nc.tensor.transpose(bank(7)[:, p4 * P:(p4 + 1) * P],
                                                  rot[n % 2][:, 512 + p4 * P:512 + (p4 + 1) * P], ident)
                    ins.then_inc(qkT_done, 1)
                if n + 1 < NTILE:
                    ready(pe, g_silu, n - 1)
                    for c in range(2):
                        ins = nc.tensor.matmul(bank(c), XT[:, n + 1, :], wqk[:, c * 512:(c + 1) * 512],
                                               start=True, stop=True)
                    ins.then_inc(qk_done, 1)
                if n == -1:
                    pe.wait_ge(load["x"], 16)
                    for q in range(1, 4):
                        turn_x(q)
                    pe.wait_ge(xT_copied, 4)
                if this:
                    if n == 0:
                        pe.wait_ge(load["gv"], 32)
                    ready(pe, o_centred, n)
                    for c in range(2):
                        ins = nc.tensor.matmul(bank(2 + c), XT[:, n, :], wv[:, c * 512:(c + 1) * 512],
                                               start=True, stop=True)
                    ins.then_inc(v_done, 1)
                    pe.wait_ge(qkT_copied, n + 1)
                    ready(pe, onT_affine, n - 1)
                    for p4 in range(4):
                        for par in range(2):
                            rows = slice(par * RD, (par + 1) * RD)
                            ins = nc.tensor.matmul(bank(4 + par)[:, p4 * P:(p4 + 1) * P], qkT[rows, 4 + p4, :],
                                                   qkT[rows, p4, :], start=True, stop=True)
                    ins.then_inc(sc_done, 1)
                    pe.wait_ge(v_copied, n + 1)
                    if last:
                        nc.tensor.matmul(bank(6)[:, 0:P], ident, ident, start=True, stop=True).then_inc(delta_done, 1)
                    else:
                        for p4 in range(4):
                            for par in range(2):
                                ins = nc.tensor.matmul(
                                    PS[par * RD:(par + 1) * RD, 6, p4 * P:(p4 + 1) * P],
                                    kd[n % 2][:, (2 * p4 + par) * RD:(2 * p4 + par + 1) * RD],
                                    vv[n % 2][:, 4 * par + p4, :], start=True, stop=True)
                        ins.then_inc(delta_done, 1)
                i = n - 2
                if 0 <= i < NTILE:
                    pe.wait_ge(u_ready, i + 1)
                    ready(pe, y_added, i)
                    for s in range(RH):
                        ins = nc.tensor.matmul(bank(7)[:, 0:P], uu[:, s, :], wo[:, s, :],
                                               start=(s == 0), stop=(s == RH - 1))
                    ins.then_inc(y_done, 1)
                i = n - 1
                if 0 <= i < NTILE:
                    if n + 1 < NTILE:
                        pe.wait_ge(rot_muls, n + 2)
                    else:
                        pe.wait_ge(g_silu, i)
                    for s in range(RH):
                        ins = nc.tensor.matmul(bank(s // 4)[:, (s % 4) * P:(s % 4 + 1) * P],
                                               wg[:, s * P:(s + 1) * P], XT[:, i, :], start=True, stop=True)
                    ins.then_inc(g_done, 1)
                if this:
                    pe.wait_ge(sc_masked, n + 1)
                    ready(pe, state_ready, n)
                    for s in range(RH):
                        par, p4 = divmod(s, 4)
                        rows = slice(par * RD, (par + 1) * RD)
                        o = bank(2 + par)[:, p4 * P:(p4 + 1) * P]
                        if not first:
                            nc.tensor.matmul(o, qkT[rows, p4, :], state[(n - 1) % 2][rows, p4 * P:(p4 + 1) * P],
                                             start=True, stop=False)
                        ins = nc.tensor.matmul(o, sm[:, s, :], vv[n % 2][:, s, :], start=first, stop=True)
                    ins.then_inc(o_done, 1)
                i = n - 1
                if 0 <= i < NTILE:
                    pe.wait_ge(o_normed, i + 1)
                    pe.wait_ge(sc_masked, min(n + 1, NTILE))
                    for s in range(RH):
                        ins = nc.tensor.transpose(bank(4 + s // 4)[:, (s % 4) * P:(s % 4 + 1) * P], on[:, s, :], ident)
                    ins.then_inc(onT_done, 1)
            barrier(pe)

        @block.vector
        def _(dve):
            v_ = nc.vector
            link = chain(dve, dve_step)
            dve.wait_ge(load["qk"], 80)
            for n in range(-1, NTILE + 2):
                this = 0 <= n < NTILE
                i = n - 2
                if 0 <= i < NTILE:
                    dve.wait_ge(onT_affine, i + 1)
                    ready(dve, y_done, i)
                    v_.tensor_tensor(uu, ga, sig, ALU.mult).then_inc(u_ready, 1)
                if n + 1 < NTILE:
                    dve.wait_ge(qk_done, n + 2)
                    ready(dve, rot_ready, n + 1)
                    c = (n + 1) % NT
                    qk3 = pair(0).rearrange("p (g e) -> p g e", e=RD // 2)
                    qk4 = pair(0).rearrange("p (h z e) -> p h z e", h=2 * RH, z=2)
                    rs4 = rs.rearrange("p (h z e) -> p h z e", h=2 * RH, z=2)
                    cosb = rcos[:, c:c + 1, :].to_broadcast([P, 4 * RH, RD // 2])
                    sinb = rsin[:, c:c + 1, :].to_broadcast([P, 2 * RH, RD // 2])
                    v_.tensor_tensor(rc.rearrange("p (g e) -> p g e", e=RD // 2), qk3, cosb, ALU.mult)
                    v_.scalar_tensor_tensor(out=rs4[:, :, 0, :], in0=qk4[:, :, 1, :], scalar=-1.0, in1=sinb,
                                            op0=ALU.mult, op1=ALU.mult)
                    v_.tensor_tensor(rs4[:, :, 1, :], qk4[:, :, 0, :], sinb, ALU.mult).then_inc(rot_muls, 1)
                    dve.wait_ge(rot_muls, n + 2)
                    ready(dve, qkT_done, n)
                    v_.tensor_tensor(rot[(n + 1) % 2][:, 512:1024], rc[:, 512:1024], rs[:, 512:1024],
                                     ALU.add).then_inc(k_rotated, 1)
                if this:
                    if n == 0:
                        dve.wait_ge(load["rest"], 32)
                    dve.wait_ge(sc_done, n + 1)
                    ready(dve, o_done, n)
                    v_.tensor_tensor(sm.rearrange("p s t -> p (s t)"), pair(2), decay, ALU.mult).then_inc(sc_masked, 1)
                    dve.wait_ge(delta_done, n + 1)
                    if n % NT == 0:
                        v_.tensor_copy(state[n % 2], bank(6)).then_inc(state_ready, 1)
                    elif n % NT < NT - 1:
                        dve.wait_ge(state_dec, n + 1)
                        v_.tensor_tensor(state[n % 2], stdec, bank(6), ALU.add).then_inc(state_ready, 1)
                    else:
                        v_.memset(unused[:, 0:1], 0.0).then_inc(state_ready, 1)
                i = n - 1
                if 0 <= i < NTILE:
                    dve.wait_ge(o_rstd, i + 1)
                    ready(dve, onT_done, i)
                    v_.tensor_tensor(on, oc[i % 2], spread(grs, RH, P), ALU.mult).then_inc(o_normed, 1)
                i = n - 2
                if 0 <= i < NTILE:
                    dve.wait_ge(y_done, i + 1)
                    v_.tensor_tensor(X[:, i, :], bank(7)[:, 0:P], X[:, i, :], ALU.add).then_inc(y_added, 1)
                    dve.wait_ge(y_added, i + 1)
                    link(v_.bn_stats(stats[:, i, :], X[:, i, :]))
                    link(v_.bn_aggr(mv[:, i, :], stats[:, i, :]))
                if this:
                    dve.wait_ge(o_done, n + 1)
                    o3 = heads(pair(1))
                    link(v_.tensor_reduce(osum, o3, AX.X, ALU.add))
                    link(v_.tensor_scalar(osum, osum, 1.0 / RV, None, ALU.mult))
                    ready(dve, o_squared, n - 1)
                    v_.tensor_tensor(oc[n % 2], o3, spread(osum, RH, P), ALU.subtract).then_inc(o_centred, 1)
                if n == NT + 2:
                    layer_norm(dve, link, 1e-5, 0, NT).then_inc(x_ready, 1)
                if n == NT + 5:
                    dve.wait_ge(x_squared, 1)
                    link(v_.tensor_scalar(square_sum[:, 0:NT], square_sum[:, 0:NT], 1.0 / P, 1e-6, ALU.mult, ALU.add))
                    link(rsqrt(v_, link, inv_rms[:, 0:NT], square_sum[:, 0:NT], newton[:, 0, 0:NT]))
            dve.wait_ge(x_ready, 1)
            barrier(dve)

        @block.gpsimd
        def _(pool):
            g_ = nc.gpsimd
            link = chain(pool, pool_step)
            pool.wait_ge(load["qk"], 80)
            for n in range(-1, NTILE + 1):
                if 0 <= n < NTILE:
                    if n == 0:
                        pool.wait_ge(load["rest"], 32)
                    ready(pool, state_ready, n)
                    if n % NT:
                        g_.tensor_tensor(stdec, state[(n - 1) % 2], gchunk, ALU.mult).then_inc(state_dec, 1)
                    else:
                        g_.memset(stdec[:, 0:1], 0.0).then_inc(state_dec, 1)
                i = n - 1
                if 0 <= i < NTILE:
                    pool.wait_ge(o_squared, i + 1)
                    link(g_.tensor_scalar(gvar, gvar, 1.0 / RV, 1e-5, ALU.mult, ALU.add))
                    ready(pool, o_normed, i)
                    rsqrt(g_, link, grs, gvar, gnt[:, 0, :], fused=False).then_inc(o_rstd, 1)
                if n + 1 < NTILE:
                    m = n + 1
                    pool.wait_ge(rot_muls, m + 1)
                    ready(pool, qkT_done, m - 1)
                    link(g_.tensor_tensor(rot[m % 2][:, 0:512], rc[:, 0:512], rs[:, 0:512], ALU.add))
                    g_.tensor_tensor(heads(qd[m % 2]), heads(rot[m % 2][:, 0:512]), spread(gq, RH, RD), ALU.mult)
                    pool.wait_ge(k_rotated, m + 1)
                    ready(pool, delta_done, m - 1)
                    g_.tensor_tensor(heads(kd[m % 2]), heads(rot[m % 2][:, 512:1024]), spread(gk, RH, RD),
                                     ALU.mult).then_inc(rot_ready, 1)
            pool.wait_ge(load["mask"], 16)
            g_.tensor_copy(masks, maskf)
            g_.tensor_copy(identb, ident)
            barrier(pool)

        @block.scalar
        def _(act):
            s_ = nc.scalar
            link = chain(act, act_step)
            for q in range(4):
                act.wait_ge(xT_done, q + 1)
                s_.activation(XT[:, 4 * q:4 * q + 4, :], bank(2 + q).rearrange("p (k t) -> p k t", k=4),
                              ACT.Copy).then_inc(xT_copied, 1)
            act.wait_ge(load["wo"], 32)
            for n in range(NTILE + 2):
                if n < NTILE:
                    act.wait_ge(qkT_done, n + 1)
                    ready(act, o_done, n)
                    s_.activation(qkT.rearrange("p s t -> p (s t)"), pair(3), ACT.Copy).then_inc(qkT_copied, 1)
                i = n - 2
                if 0 <= i < NTILE:
                    act.wait_ge(onT_done, i + 1)
                    ready(act, u_ready, i)
                    for s in range(RH):
                        ins = s_.activation(ga[:, s, :], bank(4 + s // 4)[:, (s % 4) * P:(s % 4 + 1) * P],
                                            ACT.Identity, scale=gn[:, 0, s:s + 1], bias=gn[:, 1, s:s + 1])
                    ins.then_inc(onT_affine, 1)
                if n < NTILE:
                    act.wait_ge(v_done, n + 1)
                    ready(act, o_done, n - 1)
                    s_.activation(vv[n % 2].rearrange("p s t -> p (s t)"), pair(1), ACT.Copy).then_inc(v_copied, 1)
                i = n - 1
                if 0 <= i < NTILE:
                    act.wait_ge(o_centred, i + 1)
                    ready(act, o_rstd, i)
                    for s in range(RH):
                        ins = s_.activation(sq, oc[i % 2][:, s, :], ACT.Square, accum_out=gvar[:, s:s + 1])
                        if s < RH - 1:
                            link(ins)
                    ins.then_inc(o_squared, 1)
                    act.wait_ge(g_done, i + 1)
                    ready(act, u_ready, i)
                    s_.activation(sig.rearrange("p s t -> p (s t)"), pair(0), ACT.Silu).then_inc(g_silu, 1)
                if n == NT + 3:
                    act.wait_ge(o_squared, n)
                    squares_of_x(act, link, 0)
            barrier(act)

        load_experts, load_biased, load_ternary = sem("load_experts"), sem("load_biased"), sem("load_ternary")
        load_gate = sem("load_gate")
        x1_ready = sem("x1_ready")
        u_squared, x2_ready = sem("u_squared"), sem("x2_ready")
        KINDS = ("normed", "turned", "turned_copied", "q_made", "lat_made", "lat_normed", "lat_turned",
                 "lat_copied", "k_made", "v_made", "v_kept", "q_rot_done", "q_full", "q_part0", "q_rem",
                 "q_part1", "q_part2", "k_rot_done", "k_full", "k_part0", "k_rem", "k_part1", "k_part2")
        stage_done = {k: sem("p_" + k) for k in KINDS}
        part_stored = [[sem(f"{w}_parts_stored_{c}") for c in range(2)] for w in "qk"]
        PART_DMAS = (1, 5)
        padded = sem("padded")
        stack = [sem(f"stack_loaded_{k}") for k in range(NG)]
        mrow = [sem(f"max_rows_loaded_{k}") for k in range(2)]
        ones_loaded = sem("ones_loaded")
        ring_full, ring_used = sem("ring_full"), sem("ring_used")
        score_done, exp_done, av_done = sem("score_done"), sem("exp_done"), sem("av_done")
        o_copied, mx_ready, m_split = sem("o_copied"), sem("mx_ready"), sem("m_split")
        LEAD = (11, 12)
        BLOCKS = 2 * B * NG
        CH = B * T // C
        HB = NE * EM
        HID_BANKS, EY_BANKS = (0, 1, 4, 5), (2, 3, 6, 7)
        RING = (3, 6, 7)
        SCORES = 3

        def tiles(layer, c):
            return NT if layer or c else QT

        def first_unit(layer, m):
            return sum(tiles(layer, k % 2) for k in range(m))

        def units(layer):
            return [(m, j) for m in range(BLOCKS) for j in range(tiles(layer, m % 2))]

        def maxima_of(layer, m, j):
            c = m % 2
            return (j, 0) if tiles(layer, c) == QT else (QT * c + j // 2, j % 2)

        def queries(layer, kt, c):
            return (c * C if layer else max(kt * P, c * C)), (c + 1) * C

        def order(layer):
            us = units(layer)
            lead = LEAD[layer]
            after = {}
            for m in range(BLOCKS):
                end = first_unit(layer, m + 1)
                after.setdefault(end - lead, []).append(("M", m))
                after.setdefault(end + 1 + O_LAG, []).append(("O", m))
                if m // 2 % NG == NG - 1:
                    bc = (m // 2 // NG, m % 2)
                    after.setdefault(end + 1 + N_LAG, []).append(("N", bc))
                    after.setdefault(end + 1 + Y_LAG, []).append(("Y", bc))
            if layer:
                for step, e in ((-10, ("L", 0)), (-10, ("L", 1)), (-9, ("W", 0)), (-8, ("T", 0)), (-7, ("T", 1)),
                                (-6, ("P", 0)), (-5, ("P", 1)), (-4, ("R", 0)), (-3, ("R", 1)),
                                (0, ("L", 2)), (3, ("T", 2)), (5, ("P", 2))):
                    after.setdefault(len(us) + step, []).append(e)
            else:
                for step, e in ((-8, ("B", 0)), (-6, ("H", (0, 0))), (-5, ("H", (0, 1))), (-3, ("G", 0))):
                    after.setdefault(len(us) + step, []).append(e)
                for step, rs in ((O_LAG + 1, range(E_BY_O)), (N_LAG + 1, range(E_BY_O, E_BY_N)), (Y_LAG + 1, range(E_BY_N, E_BY_Y))):
                    after.setdefault(len(us) + step, []).extend(("E", r) for r in rs)
            seq = []
            for s in range(-lead, len(us) + Y_LAG + 2):
                u = s + lead
                for h in range(HG):
                    if 0 <= s < len(us):
                        seq.append(("S", (s, h)))
                    if u < len(us):
                        seq.append(("A", (u, h)))
                    if h == 1:
                        seq += [e for e in after.get(s, []) if e[0] == "M"]
                    if h == 1 and 0 < s <= len(us):
                        seq.append(("V", s - 1))
                seq += [e for e in after.get(s, []) if e[0] != "M"]
            if layer:
                seq += [("L", 3), ("T", 3), ("R", 2), ("P", 3), ("R", 3)]
            else:
                seq += [("B", 1)] + [("E", r) for r in range(E_BY_Y, E_BY_H)]
                seq += [("H", (1, 0)), ("H", (1, 1))] + [("E", r) for r in range(E_BY_H, EARLY)] + [("G", 1)]
            return seq

        def ring_places(layer):
            events = [e for e in order(layer) if e[0] in "AMONYWTPHG"]
            return {e: r for r, e in enumerate(events)}, len(events)

        places = [ring_places(k) for k in range(2)]
        ring_base = [0, places[0][1]]
        UNITS = [len(units(k)) for k in range(2)]
        score_base = [0, HG * UNITS[0]]

        def hidden(pe, c, k):
            r = c * HB + k
            ready(pe, hid_dve if k % 2 else hid_act, r // 2 - 1)
            nc.tensor.matmul(bank(HID_BANKS[k % 4]), w1[:, k * P:(k + 1) * P],
                             h2T[c // 2][:, c % 2 * C:(c % 2 + 1) * C], start=True, stop=True) \
              .then_inc(hid_done, 1)

        def relu_act(act, c, k):
            act.wait_ge(hid_done, c * HB + k + 1)
            ready(act, ey_done, 4 * (c - 1))
            nc.scalar.activation(hid[c % 2][:, k, :], bank(HID_BANKS[k % 4]), ACT.Relu,
                                 bias=b1[:, k:k + 1]).then_inc(hid_act, 1)

        def relu_dve(dve, c, k):
            dve.wait_ge(hid_done, c * HB + k + 1)
            ready(dve, ey_done, 4 * (c - 1))
            nc.vector.tensor_scalar(hid[c % 2][:, k, :], bank(HID_BANKS[k % 4]), b1[:, k:k + 1], 0.0,
                                    ALU.add, ALU.max).then_inc(hid_dve, 1)

        def attention(layer):
            place = {k: v + ring_base[layer] for k, v in places[layer][0].items()}
            us = units(layer)
            s0 = layer * UNITS[0]
            m0 = layer * BLOCKS
            n0 = layer * B * NG
            q0 = score_base[layer]
            causal = layer == 0

            def ring_bank(r):
                return RING[r % len(RING)]

            def scored(m):
                return q0 + HG * first_unit(layer, m + 1)

            @block.sync
            def _(sp):
                for b in range(B):
                    for c in range(2):
                        cols = slice(c * C, (c + 1) * C)
                        item = layer * 4 + 2 * b + c
                        sp.wait_ge(stage_done["q_part2"], item + 1)
                        sp.dma_start(q_dram[layer, b, :, :, cols], parts[0][c]).then_inc(part_stored[0][c], 16)
                        sp.wait_ge(stage_done["k_part2"], item + 1)
                        for m in range(PARTS):
                            sp.dma_start(k_dram[layer, b, m, :, 0:PARTS - m, cols], parts[1][c][:, m:PARTS, :]) \
                              .then_inc(part_stored[1][c], 16)
                            if m:
                                sp.dma_start(k_dram[layer, b, m, :, PARTS - m:PARTS, cols], parts[1][c][:, 0:m, :]) \
                                  .then_inc(part_stored[1][c], 16)
                    for w in range(2):
                        for c in range(2):
                            sp.wait_ge(part_stored[w][c], 16 * PART_DMAS[w] * (layer * B + b + 1))
                    for g in range(NG):
                        n = b * NG + g
                        if layer and n == 0:
                            sp.wait_ge(hid_done, CH * HB)
                        if layer and n == 1:
                            sp.wait_ge(ey_done, NTILE)
                            sp.wait_ge(ey_used, NTILE)
                            load_ones(sp)
                        if n0 + n >= NG:
                            sp.wait_ge(score_done, score_base[1] if n < NG else scored(2 * (n - NG) + 1))
                        hs = slice(g * HG, (g + 1) * HG)
                        for m in range(PARTS):
                            rows = slice(PARTS * AD * m, PARTS * AD * (m + 1))
                            src = k_dram[layer, b, m].rearrange("(h d) i t -> (d i) h t", d=AD)
                            sp.dma_start(Ks[rows, g], src[:, hs, :]).then_inc(stack[g], 16)
                            for c in range(2):
                                src = q_dram[layer, b].rearrange("(h d) i t -> (d i) h t", d=AD)
                                sp.dma_start(Qs[rows, g, c], src[:, hs, c * C:(c + 1) * C]).then_inc(stack[g], 16)
                sp.wait_ge(score_done, scored(BLOCKS - 3))
                if layer:
                    sp.dma_start(tw, d["t_w"]).then_inc(load_ternary, 16)
                else:
                    for t, src in ((gate, d["e_gate"]), (enorm, d["k_norm"]), (b1, d["e_b1"]),
                                   (gateb, d["e_gateb"].to_broadcast([P, NE]))):
                        sp.dma_start(t, src).then_inc(load_gate, 16)
                    for t, src in ((w1, d["e_w1"]), (w2, d["e_w2"]),
                                   (b2.rearrange("p e o -> p (e o)"), d["e_b2"].to_broadcast([P, NE * P]))):
                        sp.dma_start(t, src).then_inc(load_experts, 16)

            @block.gpsimd
            def _(pool):
                link = chain(pool, pool_step)
                for m in range(BLOCKS):
                    n, c = divmod(m, 2)
                    part = [nmp[m % 2][:, i, :] for i in range(PARTS)]
                    pool.wait_ge(ring_used, place["M", m] + 1)
                    link(nc.gpsimd.tensor_copy(part[1], nm1))
                    nc.gpsimd.tensor_tensor(part[2], nm1, part[1], ALU.subtract).then_inc(m_split, 1)
                    pool.wait_ge(m_split, m0 + m + 1)
                    if n0 + n >= NG:
                        pool.wait_ge(score_done, score_base[1] if n < NG else scored(m - 2 * NG))
                    for i in range(PARTS):
                        row = Qs[SROWS + i:SROWS + i + 1, n % NG, c].rearrange("o h (j q) -> o (h j) q", q=P)
                        nc.gpsimd.dma_start(row, nmp[m % 2][:, i, :]).then_inc(mrow[m % 2], 16)
                if layer:
                    pool.wait_ge(load_ternary, 16)
                    nc.gpsimd.memset(ones, 1.0).then_inc(t_ones, 1)

            @block.tensor
            def _(pe):
                for kind in ("q_full", "k_full", "v_kept"):
                    pe.wait_ge(stage_done[kind], 4 * layer + 4)
                if layer:
                    pe.wait_ge(ey_used, NTILE)
                for kind, k in order(layer):
                    if (kind, k) in place:
                        r = place[kind, k]
                        bk = bank(ring_bank(r))
                        ready(pe, ring_used, r - len(RING) + 1)
                    if kind == "A":
                        u, h = k
                        m, j = us[u]
                        n, c = divmod(m, 2)
                        if h == 0 and j == 0 and c == 0:
                            pe.wait_ge(stack[n % NG], 3 * PARTS * 16 * ((n0 + n) // NG + 1))
                        qt, kc = maxima_of(layer, m, j)
                        lo, hi = kc * C, (min((kc + 1) * C, (qt + 1) * P) if causal else (kc + 1) * C)
                        diag = causal and kc == c
                        corner = not causal and (qt, kc) in ((0, 1), (NT - 1, 0))
                        q = (qt - QT * c) * P
                        ins = nc.tensor.matmul(bk[:, 0:hi - lo], Qs[0:SROWS, n % NG, c, h, q:q + P],
                                               Ks[0:SROWS, n % NG, h, lo:hi], start=True, stop=not (diag or corner))
                        if diag or corner:
                            o, w = (qt * P - lo, 0) if diag else ((384, 2) if qt == 0 else (0, 3))
                            ins = nc.tensor.matmul(bk[:, o:o + P], identb, masks[:, w, :], start=False, stop=True)
                        ins.then_inc(ring_full, 1)
                    elif kind == "M":
                        pe.wait_ge(mx_ready, m0 + k + 1)
                        nc.tensor.transpose(bk[0:MAXIMA, 0:P], mx[k % 2][:, 0, :], ident).then_inc(ring_full, 1)
                    elif kind == "S":
                        s, h = k
                        m, kt = us[s]
                        n, c = divmod(m, 2)
                        if h == 0 and kt == 0:
                            if s == 0:
                                pe.wait_ge(ones_loaded, 16 * (layer + 1))
                            pe.wait_ge(mrow[m % 2], PARTS * 16 * ((m0 + m) // 2 + 1))
                        q = q0 + HG * s + h
                        bq = bank(q % SCORES)
                        ready(pe, exp_done, q - SCORES + 1)
                        lo, hi = queries(layer, kt, c)
                        o = lo - c * C
                        diag = causal and kt // QT == c
                        corner = not causal and (kt, c) in ((0, 1), (NT - 1, 0))
                        ins = nc.tensor.matmul(bq[:, o:C], Ks[0:MROWS, n % NG, h, kt * P:(kt + 1) * P],
                                               Qs[0:MROWS, n % NG, c, h, o:C], start=True, stop=not (diag or corner))
                        if diag or corner:
                            o, w = (o, 1) if diag else ((384, 2) if kt == 0 else (0, 3))
                            ins = nc.tensor.matmul(bq[:, o:o + P], identb, masks[:, w, :], start=False, stop=True)
                        ins.then_inc(score_done, 1)
                    elif kind == "V":
                        m, kt = us[k]
                        n, c = divmod(m, 2)
                        b, g = divmod(n, NG)
                        pe.wait_ge(exp_done, q0 + HG * (k + 1))
                        if kt == 0:
                            ready(pe, o_copied, m0 + m - 1)
                        lo, hi = queries(layer, kt, c)
                        o = lo - c * C
                        for h in range(HG):
                            ins = nc.tensor.matmul(PS[h * VW:(h + 1) * VW, 4 + c, o:C], V[:, b, kt, HG * g + h, :],
                                                   Pr[k % PROBS][:, h, o:C],
                                                   start=(kt == 0), stop=(kt == tiles(layer, c) - 1))
                        ins.then_inc(av_done, 1)
                    elif kind == "O":
                        pe.wait_ge(o_copied, m0 + k + 1)
                        for t in range(QT):
                            ins = nc.tensor.transpose(bk[:, t * P:(t + 1) * P], osb[:, k % 2, t * P:(t + 1) * P], ident)
                        ins.then_inc(ring_full, 1)
                    elif kind == "H":
                        b, c = k
                        pe.wait_ge(e_normed, b + 1)
                        for t in range(QT):
                            ins = nc.tensor.transpose(bk[:, t * P:(t + 1) * P], hn[b][:, QT * c + t, :], ident)
                        ins.then_inc(ring_full, 1)
                    elif kind == "G":
                        pe.wait_ge(ring_used, max(r - len(RING) + 1, place["H", (k, 1)] + 1))
                        for t in range(NT):
                            ins = nc.tensor.matmul(bk[:, t * NE:(t + 1) * NE], h2T[k][:, t * P:(t + 1) * P],
                                                   gate, start=True, stop=True)
                        ins.then_inc(ring_full, 1)
                    elif kind == "E":
                        if k == 0:
                            pe.wait_ge(exp_done, score_base[1])
                            pe.wait_ge(o_copied, BLOCKS)
                            pe.wait_ge(ring_used, place["H", (0, 0)] + 1)
                            pe.wait_ge(load_experts, 48)
                        hidden(pe, *divmod(k, HB))
                    elif kind == "W":
                        pe.wait_ge(t_abs, 1)
                        pe.wait_ge(t_ones, 1)
                        nc.tensor.matmul(bk[:, 0:1], ones, tsum, start=True, stop=True).then_inc(ring_full, 1)
                    elif kind == "T":
                        pe.wait_ge(x2_ready, k + 1)
                        for t in range(QT):
                            ins = nc.tensor.transpose(bk[:, t * P:(t + 1) * P], X[:, QT * k + t, :], ident)
                        ins.then_inc(ring_full, 1)
                    elif kind == "P":
                        pe.wait_ge(t_quant, 1)
                        pe.wait_ge(ring_used, max(r - len(RING) + 1, place["T", k] + 1))
                        for t in range(QT):
                            ins = nc.tensor.matmul(bk[:, t * P:(t + 1) * P], t_xT[:, QT * k + t, :], tw,
                                                   start=True, stop=True)
                        ins.then_inc(ring_full, 1)
                    elif kind == "N":
                        b, c = k
                        pe.wait_ge(ring_used, max(r - len(RING) + 1, place["O", 2 * (NG * (b + 1) - 1) + c] + 1))
                        for t in range(QT):
                            ins = nc.tensor.transpose(bk[:, t * P:(t + 1) * P], On[:, QT * c + t, :], ident)
                        ins.then_inc(ring_full, 1)
                    elif kind == "Y":
                        b, c = k
                        pe.wait_ge(ring_used, max(r - len(RING) + 1, place["N", k] + 1))
                        for t in range(QT):
                            ins = nc.tensor.matmul(bk[:, t * P:(t + 1) * P], OT[:, c * C + t * P:c * C + (t + 1) * P],
                                                   wout, start=True, stop=True)
                        ins.then_inc(ring_full, 1)

            @block.scalar
            def _(act):
                link = chain(act, act_step)
                for kind, k in order(layer):
                    if kind == "S":
                        s, h = k
                        m, kt = us[s]
                        q = q0 + HG * s + h
                        lo, hi = queries(layer, kt, m % 2)
                        o = lo - m % 2 * C
                        if h == 0:
                            ready(act, av_done, s0 + s - PROBS + 1)
                        act.wait_ge(score_done, q + 1)
                        nc.scalar.activation(Pr[s % PROBS][:, h, o:C], bank(q % SCORES)[:, o:C],
                                             ACT.Exp).then_inc(exp_done, 1)
                    elif kind == "E" and k % 2 == 0:
                        act.wait_ge(load_gate, 64)
                        relu_act(act, *divmod(k, HB))
                    elif kind == "W":
                        act.wait_ge(load_ternary, 16)
                        nc.scalar.activation(twp, tw, ACT.Abs, accum_out=tsum).then_inc(t_abs, 1)
                    elif kind == "V":
                        m, kt = us[k]
                        if kt == tiles(layer, m % 2) - 1:
                            act.wait_ge(av_done, s0 + k + 1)
                            if m >= 2:
                                act.wait_ge(ring_full, place["O", m - 2] + 1)
                            nc.scalar.activation(osb[:, m % 2, :], bank(4 + m % 2), ACT.Copy).then_inc(o_copied, 1)
                    elif kind == "Y" and not layer and k[1] == 1:
                        b = k[0]
                        act.wait_ge(ring_used, place["Y", k] + 1)
                        for i in range(b * NT, (b + 1) * NT):
                            ins = nc.scalar.activation(sq, U[:, i, :], ACT.Square, accum_out=square_sum[:, i:i + 1])
                            if i % NT < NT - 1:
                                link(ins)
                            else:
                                ins.then_inc(u_squared, 1)
                                act.wait_ge(u_squared, b + 1)

            @block.vector
            def _(dve):
                v_ = nc.vector
                link = chain(dve, dve_step)
                for kind, k in order(layer):
                    if (kind, k) in place:
                        r = place[kind, k]
                        bk = bank(ring_bank(r))
                        dve.wait_ge(ring_full, r + 1)
                    if kind == "A":
                        u, h = k
                        m, j = us[u]
                        qt, kc = maxima_of(layer, m, j)
                        width = min(C, (qt + 1) * P - kc * C) if causal else C
                        col = h * QT + qt % QT
                        v_.tensor_reduce(mx[m % 2][:, kc, col:col + 1], bk[:, 0:width], AX.X, ALU.max) \
                          .then_inc(ring_used, 1)
                        if h == HG - 1 and j == tiles(layer, m % 2) - 1:
                            dve.wait_ge(ring_used, r + 1)
                            one, two = (mx[m % 2][:, kc, :] for kc in range(2))
                            if tiles(layer, m % 2) == QT:
                                two = one
                            v_.tensor_tensor(one, one, two, ALU.max).then_inc(mx_ready, 1)
                    elif kind == "M":
                        ready(dve, mrow[k % 2], PARTS * 16 * ((m0 + k) // 2))
                        row = bk[0:MAXIMA, 0:P]
                        part = [nmp[k % 2][:, i, :] for i in range(PARTS)]
                        link(v_.tensor_scalar(part[0], row, -1.0, None, ALU.mult))
                        ready(dve, m_split, m0 + k)
                        v_.scalar_tensor_tensor(out=nm1, in0=row, scalar=-1.0, in1=part[0],
                                                op0=ALU.mult, op1=ALU.subtract).then_inc(ring_used, 1)
                    elif kind == "O":
                        n, c = divmod(k, 2)
                        g = n % NG
                        o4 = bk.rearrange("p (t h e) -> p t h e", t=QT, h=HG)
                        link(v_.reciprocal(rden, o4[:, :, :, AD]))
                        dst = On[:, QT * c:QT * (c + 1), HG * AD * g:HG * AD * (g + 1)]
                        v_.tensor_tensor(dst.rearrange("p t (h e) -> p t h e", h=HG), o4[:, :, :, 0:AD],
                                         rden.unsqueeze(3).to_broadcast([P, QT, HG, AD]),
                                         ALU.mult).then_inc(ring_used, 1)
                        dve.wait_ge(ring_used, r + 1)
                    elif kind == "N":
                        b, c = k
                        v_.tensor_copy(OT[:, c * C:(c + 1) * C], bk).then_inc(ring_used, 1)
                    elif kind == "Y":
                        b, c = k
                        t = slice(b * NT + QT * c, b * NT + QT * (c + 1))
                        y = bk.rearrange("p (t e) -> p t e", t=QT)
                        v_.tensor_tensor((X if layer else U)[:, t, :], y, X[:, t, :], ALU.add).then_inc(ring_used, 1)
                    elif kind == "B":
                        dve.wait_ge(u_squared, k + 1)
                        dve.wait_ge(load_gate, 64)
                        t = slice(k * NT, (k + 1) * NT)
                        link(v_.tensor_scalar(square_sum[:, t], square_sum[:, t], 1.0 / P, 1e-6, ALU.mult, ALU.add))
                        link(rsqrt(v_, link, inv_rms[:, t], square_sum[:, t], newton[:, 0, t]))
                        for t in range(NT):
                            i = k * NT + t
                            ins = v_.tensor_scalar(hn[k][:, t, :], U[:, i, :], inv_rms[:, i:i + 1], None, ALU.mult)
                        ins.then_inc(e_normed, 1)
                    elif kind == "H":
                        b, c = k
                        v_.tensor_scalar(h2T[b][:, c * C:(c + 1) * C], bk, enorm[:, 1:2], None, ALU.mult) \
                          .then_inc(ring_used, 1)
                    elif kind == "G":
                        t = slice(k * NT, (k + 1) * NT)
                        hot, lg = onehot[:, t, :], logit[:, t, :]
                        v_.tensor_tensor(lg, bk[:, 0:NT * NE].rearrange("p (i e) -> p i e", e=NE),
                                         gateb.unsqueeze(1).to_broadcast([P, NT, NE]), ALU.add).then_inc(ring_used, 1)
                        dve.wait_ge(ring_used, r + 1)
                        link(v_.tensor_reduce(top[:, t], lg, AX.X, ALU.max))
                        link(v_.tensor_tensor(hot, lg, spread(top[:, t], NT, NE), ALU.is_ge))
                        link(v_.tensor_scalar(left[:, t], hot[:, :, 0], -1.0, 1.0, ALU.mult, ALU.add))
                        for e in range(1, NE):
                            ins = v_.tensor_tensor(hot[:, :, e], hot[:, :, e], left[:, t], ALU.mult)
                            if e < NE - 1:
                                link(ins)
                                link(v_.tensor_tensor(left[:, t], left[:, t], hot[:, :, e], ALU.subtract))
                        ins.then_inc(e_onehot, 1)
                        dve.wait_ge(e_onehot, k + 1)
                    elif kind == "E" and k % 2:
                        relu_dve(dve, *divmod(k, HB))
                    elif kind == "W":
                        link(v_.tensor_scalar(tsc, bk[:, 0:1], 1.0 / (P * P), 1e-5, ALU.mult, ALU.max))
                        v_.tensor_scalar(thalf, tsc, 0.5, None, ALU.mult).then_inc(ring_used, 1)
                        dve.wait_ge(ring_used, r + 1)
                        v_.tensor_scalar(twp, tw, thalf, None, ALU.is_gt)
                        link(v_.tensor_scalar(twn, tw, -1.0, thalf, ALU.mult, ALU.is_gt))
                        link(v_.tensor_tensor(twp, twp, twn, ALU.subtract))
                        v_.tensor_scalar(tw, twp, tsc, None, ALU.mult).then_inc(t_quant, 1)
                    elif kind == "T":
                        v_.tensor_copy(t_xT[:, QT * k:QT * (k + 1), :], bk.rearrange("p (t o) -> p t o", t=QT)) \
                          .then_inc(ring_used, 1)
                    elif kind == "P":
                        t = slice(QT * k, QT * (k + 1))
                        v_.tensor_tensor(X[:, t, :], bk.rearrange("p (t o) -> p t o", t=QT), X[:, t, :], ALU.add) \
                          .then_inc(ring_used, 1)
                    elif kind == "R":
                        dve.wait_ge(ring_used, place["P", k] + 1)
                        lo, hi = k * QT, (k + 1) * QT
                        statistics(v_, link, lo, hi)
                        link(v_.tensor_scalar(rstd[:, lo:hi], mv[:, lo:hi, 1], 1e-5, None, ALU.add))
                        rsqrt(v_, link, newton[:, 1, lo:hi], rstd[:, lo:hi], newton[:, 0, lo:hi]).then_inc(t_rstd, 1)
                        dve.wait_ge(t_rstd, k + 1)
                        for i in range(lo, hi, 2):
                            ins = v_.tensor_scalar(X[:, i, :], X[:, i, :], mv[:, i, 0:1], newton[:, 1, i:i + 1],
                                                   ALU.subtract, ALU.mult)
                        ins.then_inc(t_normed, 1)
                    elif kind == "L" and layer:
                        dve.wait_ge(ring_used, place["Y", divmod(k, 2)] + 1)
                        statistics(v_, link, k * QT, (k + 1) * QT)
                        layer_norm(dve, link, 1e-5, k * QT, (k + 1) * QT).then_inc(x2_ready, 1)
                        dve.wait_ge(x2_ready, k + 1)

        orders = ("""
            normed:0 turned:0 normed:1 x_normed:1 turned_copied:0 x_squared:1 q_made:0 turned:1 q_rot_done:0
            normed:2 lat_made:0 turned_copied:1 q_full:0 q_made:1 q_part0:0 lat_made:1 q_rot_done:1 normed:3
            turned:2 lat_normed:0 q_full:1 q_part0:1 turned_copied:2 turned:3 q_made:2 turned_copied:3
            lat_turned:0 q_rot_done:2 lat_made:2 lat_copied:0 q_rem:0 q_made:3 q_part1:0 q_rem:1 q_full:2
            q_part2:0 q_part1:1 lat_made:3 q_part2:1 k_made:0 q_rot_done:3 lat_turned:1 k_rot_done:0 q_full:3
            v_made:0 lat_copied:1 lat_normed:1 k_full:0 q_part0:2 k_made:1 k_part0:0 v_kept:0 k_rem:0 k_part1:0
            k_part2:0 k_rot_done:1 lat_turned:2 v_made:1 lat_copied:2 k_full:1 lat_turned:3 k_part0:1 k_made:2
            lat_copied:3 k_rem:1 v_kept:1 k_rot_done:2 k_part1:1 q_part0:3 k_part2:1 k_made:3 k_full:2 v_made:2
            k_part0:2 k_rot_done:3 v_kept:2 q_rem:2 v_made:3 k_full:3 q_rem:3 v_kept:3 k_rem:2 k_part0:3
            k_part1:2 k_rem:3 k_part2:2 k_part1:3 q_part1:2 q_part1:3 q_part2:2 k_part2:3 q_part2:3
        """, """
            turned:0 turned_copied:0 turned:1 k_made:0 turned_copied:1 k_full:0 k_made:1 k_part0:0 q_made:0
            k_full:1 k_rem:0 q_full:0 q_made:1 k_part0:1 q_part0:0 v_made:0 k_rem:1 q_full:1 k_part1:0 q_rem:0
            v_made:1 q_part0:1 k_part2:0 k_part1:1 q_rem:1 turned:2 q_part1:0 k_part2:1 q_part1:1 q_part2:0
            turned_copied:2 q_part2:1 turned:3 v_kept:0 k_made:2 turned_copied:3 v_kept:1 q_made:2 k_full:2
            k_made:3 k_part0:2 q_full:2 k_rem:2 q_made:3 k_full:3 v_made:2 k_part0:3 q_full:3 q_part0:2 k_rem:3
            v_kept:2 v_made:3 q_part0:3 k_part1:2 v_kept:3 k_part1:3 k_part2:2 q_rem:2 q_part1:2 q_rem:3
            k_part2:3 q_part2:2 q_part1:3 q_part2:3
        """)

        def schedule(layer):
            return [(k, int(m)) for k, m in (item.split(":") for item in orders[layer].split())]

        def projector(layer, eng):
            def wait(kind, m):
                if m >= 0:
                    per = B if kind == "lat_normed" else 4
                    eng.wait_ge(stage_done[kind], per * layer + m + 1)

            def made(ins, kind):
                ins.then_inc(stage_done[kind], 1)
            return wait, made

        def stored_wait(eng, layer, w, m):
            if layer * 4 + m >= 2:
                eng.wait_ge(part_stored[w][m % 2], 16 * PART_DMAS[w] * (layer * B + m // 2))

        def first_part(eng, wait, made, layer, w, m):
            x = "qk"[w]
            wait(x + "_full", m)
            stored_wait(eng, layer, w, m)
            made(nc.scalar.activation(parts[w][m % 2][:, 0, :], kq[w][m % 2], ACT.Copy), x + "_part0")

        def first_rest(e_, wait, made, w, m):
            x = "qk"[w]
            wait(x + "_part0", m)
            wait(x + "_part1", m - 2)
            wait(x + "_part2", m - 2)
            made(e_.tensor_tensor(rem[w][m % 2], kq[w][m % 2], parts[w][m % 2][:, 0, :], ALU.subtract), x + "_rem")

        def second_part(wait, made, w, m):
            x = "qk"[w]
            wait(x + "_rem", m)
            made(nc.scalar.activation(parts[w][m % 2][:, 1, :], rem[w][m % 2], ACT.Copy), x + "_part1")

        def third_part(e_, wait, made, w, m):
            x = "qk"[w]
            wait(x + "_part1", m)
            made(e_.tensor_tensor(parts[w][m % 2][:, 2, :], rem[w][m % 2], parts[w][m % 2][:, 1, :],
                                  ALU.subtract), x + "_part2")

        def load_ones(sp):
            sp.dma_start(Ks[SROWS:MROWS].rearrange("p g h t -> p (g h t)").bitcast(F32), d["c_ones"]) \
              .then_inc(ones_loaded, 16)

        def pad_values(pool):
            pads = V[:, :, :, :, AD:VW].rearrange("p b t h e -> p (b t h) e")
            nc.gpsimd.memset(pads[:, :, 0:1], 1.0)
            nc.gpsimd.memset(pads[:, :, 1:VW - AD], 0.0).then_inc(padded, 1)

        def latent_projections():
            @block.sync
            def _(sp):
                load_ones(sp)

            @block.gpsimd
            def _(pool):
                g_ = nc.gpsimd
                wait, made = projector(0, pool)
                pad_values(pool)
                for kind, m in schedule(0):
                    if kind in ("q_full", "k_full"):
                        w = "qk".index(kind[0])
                        x = "qk"[w]
                        wait("q_rot_done" if w == 0 else "k_rot_done", m)
                        wait(x + "_rem", m - 2)
                        made(g_.tensor_tensor(kq[w][m % 2], rot1[w], rot2[w], ALU.add), kind)
                    elif kind == "k_rem":
                        first_rest(g_, wait, made, 1, m)
                    elif kind == "k_part2":
                        third_part(g_, wait, made, 1, m)

            @block.tensor
            def _(pe):
                wait, made = projector(0, pe)
                pe.wait_ge(load_latent, 144)
                for kind, m in schedule(0):
                    c = m % 2
                    if kind == "turned":
                        wait("normed", m)
                        wait("turned_copied", m - 1)
                        for t in range(4):
                            ins = nc.tensor.transpose(bank(0)[:, t * P:(t + 1) * P], xn[c][:, t, :], ident)
                        made(ins, kind)
                    elif kind == "q_made":
                        wait("turned_copied", m)
                        wait("q_rot_done", m - 1)
                        for z in range(2):
                            ins = nc.tensor.matmul(bank(1 + z), wq2[:, z, :], hT[c], start=True, stop=True)
                        made(ins, kind)
                    elif kind == "lat_made":
                        if m == 2:
                            wait("lat_normed", 0)
                        for t in range(4):
                            ins = nc.tensor.matmul(bank(3)[:, (4 * c + t) * KV:(4 * c + t + 1) * KV],
                                                   hT[c][:, t * P:(t + 1) * P], wdkv, start=True, stop=True)
                        made(ins, kind)
                    elif kind == "lat_turned":
                        wait("lat_normed", m // 2)
                        wait("lat_copied", m - 1)
                        for t in range(4):
                            ins = nc.tensor.transpose(bank(7)[0:KV, t * P:(t + 1) * P], lat[:, 4 * c + t, :], ident)
                        made(ins, kind)
                    elif kind == "k_made":
                        wait("lat_copied", m)
                        wait("k_rot_done", m - 1)
                        for z in range(2):
                            ins = nc.tensor.matmul(bank(4 + z), wuk2[:, z, :], latT[c], start=True, stop=True)
                        made(ins, kind)
                    elif kind == "v_made":
                        wait("v_kept", m - 1)
                        for t in range(4):
                            ins = nc.tensor.matmul(bank(6)[:, t * P:(t + 1) * P], latT[c][:, t * P:(t + 1) * P], wuv,
                                                   start=True, stop=True)
                        made(ins, kind)

            @block.scalar
            def _(act):
                s_ = nc.scalar
                wait, made = projector(0, act)
                link = chain(act, act_step)
                act.wait_ge(load_latent, 144)
                for kind, m in schedule(0):
                    c = m % 2
                    if kind == "x_squared":
                        squares_of_x(act, link, m)
                    elif kind == "turned_copied":
                        wait("turned", m)
                        wait("lat_made", m - 2)
                        made(s_.activation(hT[c], bank(0), ACT.Copy, scale=norms[:, 0:1]), kind)
                    elif kind == "lat_copied":
                        wait("lat_turned", m)
                        wait("v_made", m - 2)
                        made(s_.activation(latT[c], bank(7)[0:KV, :], ACT.Identity, scale=lnp[:, 0:1],
                                           bias=lnp[:, 1:2]), kind)
                    elif kind == "v_kept":
                        wait("v_made", m)
                        act.wait_ge(padded, 1)
                        made(s_.activation(V[:, m // 2, 4 * c:4 * c + 4, :, 0:AD].rearrange("p t h e -> p (t h) e"),
                                           bank(6).rearrange("p (x e) -> p x e", e=AD), ACT.Copy), kind)
                    elif kind in ("q_part0", "k_part0"):
                        first_part(act, wait, made, 0, "qk".index(kind[0]), m)
                    elif kind in ("q_part1", "k_part1"):
                        second_part(wait, made, "qk".index(kind[0]), m)

            @block.vector
            def _(dve):
                v_ = nc.vector
                wait, made = projector(0, dve)
                link = chain(dve, dve_step)
                dve.wait_ge(load_latent, 144)
                for kind, m in schedule(0):
                    b, c = divmod(m, 2)
                    if kind == "x_normed":
                        layer_norm(dve, link, 1e-5, NT, NTILE).then_inc(x_ready, 1)
                        dve.wait_ge(x_ready, B)
                    elif kind == "normed":
                        if m == 2:
                            dve.wait_ge(x_squared, b + 1)
                            t = slice(b * NT, (b + 1) * NT)
                            link(v_.tensor_scalar(square_sum[:, t], square_sum[:, t], 1.0 / P, 1e-6, ALU.mult, ALU.add))
                            link(rsqrt(v_, link, inv_rms[:, t], square_sum[:, t], newton[:, 0, t]))
                        wait("turned", m - 2)
                        for t in range(4):
                            i = 4 * m + t
                            ins = v_.tensor_scalar(xn[c][:, t, :], X[:, i, :], inv_rms[:, i:i + 1], None, ALU.mult)
                        made(ins, kind)
                    elif kind == "lat_normed":
                        wait("lat_made", 2 * m + 1)
                        for t in range(NT):
                            ins = v_.bn_stats(lst[:, t, :], bank(3)[:, t * KV:(t + 1) * KV])
                        link(ins)
                        for t in range(NT):
                            ins = v_.bn_aggr(lmv[:, t, :], lst[:, t, :])
                        link(ins)
                        link(v_.tensor_scalar(lvar, lmv[:, :, 1], 1e-5, None, ALU.add))
                        link(rsqrt(v_, link, lrs, lvar, ltmp))
                        wait("lat_turned", 2 * m - 1)
                        for t in range(NT):
                            ins = v_.tensor_scalar(lat[:, t, :], bank(3)[:, t * KV:(t + 1) * KV], lmv[:, t, 0:1],
                                                   lrs[:, t:t + 1], ALU.subtract, ALU.mult)
                        made(ins, kind)
                    elif kind in ("q_rot_done", "k_rot_done"):
                        w = "qk".index(kind[0])
                        x = "qk"[w]
                        scale = 1.0 if w else QSCALE
                        wait(x + "_made", m)
                        wait(x + "_full", m - 1)
                        cols = slice(c * C, (c + 1) * C)
                        v_.scalar_tensor_tensor(out=rot1[w], in0=bank(3 * w + 1), scalar=scale, in1=tab_cos[:, cols],
                                                op0=ALU.mult, op1=ALU.mult)
                        made(v_.scalar_tensor_tensor(out=rot2[w], in0=bank(3 * w + 2), scalar=scale,
                                                     in1=tab_sin[:, cols], op0=ALU.mult, op1=ALU.mult), kind)
                    elif kind == "q_rem":
                        first_rest(v_, wait, made, 0, m)
                    elif kind == "q_part2":
                        third_part(v_, wait, made, 0, m)

        def biased_pe(pe, kind, m):
            wait, made = projector(1, pe)
            c = m % 2
            if kind == "turned":
                pe.wait_ge(x1_ready, m // 2 + 1)
                wait("turned_copied", m - 1)
                for t in range(4):
                    ins = nc.tensor.transpose(bank(0)[:, t * P:(t + 1) * P], X[:, 4 * m + t, :], ident)
                made(ins, kind)
            elif kind in ("q_made", "k_made"):
                w = "qk".index(kind[0])
                pe.wait_ge(load_biased, 64)
                wait("turned_copied", m)
                wait(kind[0] + "_full", m - 1)
                made(nc.tensor.matmul(bank((1, 4)[w]), wqkv[:, w, :], hT[c], start=True, stop=True), kind)
            elif kind == "v_made":
                wait("turned_copied", m)
                wait("v_kept", m - 1)
                for t in range(4):
                    ins = nc.tensor.matmul(bank(5)[:, t * P:(t + 1) * P], hT[c][:, t * P:(t + 1) * P],
                                           wqkv[:, 2, :], start=True, stop=True)
                made(ins, kind)

        def biased_act(act, kind, m):
            wait, made = projector(1, act)
            c = m % 2
            if kind == "turned_copied":
                wait("turned", m)
                wait("v_made", m - 2)
                act.wait_ge(ey_done, NTILE - 4)
                made(nc.scalar.activation(hT[c], bank(0), ACT.Copy), kind)
            elif kind == "k_full":
                act.wait_ge(load_biased, 64)
                wait("k_made", m)
                wait("k_rem", m - 2)
                made(nc.scalar.activation(kq[1][c], bank(4), ACT.Identity, bias=bqk[:, 1:2]), kind)
            elif kind in ("q_part0", "k_part0"):
                first_part(act, wait, made, 1, "qk".index(kind[0]), m)
            elif kind in ("q_part1", "k_part1"):
                second_part(wait, made, "qk".index(kind[0]), m)

        def biased_dve(dve, kind, m):
            v_ = nc.vector
            wait, made = projector(1, dve)
            b, c = divmod(m, 2)
            if kind == "q_full":
                dve.wait_ge(load_biased, 64)
                wait("q_made", m)
                wait("q_part0", m - 2)
                made(v_.tensor_scalar(kq[0][c], bank(1), bqk[:, 0:1], QSCALE, ALU.add, ALU.mult), kind)
            elif kind == "q_rem":
                first_rest(v_, wait, made, 0, m)
            elif kind == "q_part2":
                third_part(v_, wait, made, 0, m)
            elif kind == "v_kept":
                wait("v_made", m)
                dve.wait_ge(padded, 2)
                made(v_.tensor_tensor(V[:, b, 4 * c:4 * c + 4, :, 0:AD],
                                      bank(5).rearrange("p (t h e) -> p t h e", t=4, e=AD),
                                      bv.rearrange("p (h e) -> p h e", e=AD).unsqueeze(1)
                                      .to_broadcast([P, 4, AH, AD]), ALU.add), kind)

        def biased_pool(pool, kind, m):
            wait, made = projector(1, pool)
            if kind == "k_rem":
                first_rest(nc.gpsimd, wait, made, 1, m)
            elif kind == "k_part2":
                third_part(nc.gpsimd, wait, made, 1, m)

        EARLY_BIASED = [item for item in schedule(1) if item[1] < 2 and item[0][0] != "v"]
        LATE_BIASED = [item for item in schedule(1) if item not in EARLY_BIASED]

        def biased_projections():
            @block.gpsimd
            def _(pool):
                pool.wait_ge(ey_used, NTILE)
                pad_values(pool)
                for kind, m in LATE_BIASED:
                    biased_pool(pool, kind, m)

            @block.tensor
            def _(pe):
                for kind, m in LATE_BIASED:
                    biased_pe(pe, kind, m)

            @block.scalar
            def _(act):
                for kind, m in LATE_BIASED:
                    biased_act(act, kind, m)

            @block.vector
            def _(dve):
                for kind, m in LATE_BIASED:
                    biased_dve(dve, kind, m)

        PE_EARLY = ([("turned", 0)], [("turned", 1), ("q_made", 0), ("k_made", 0)], [("q_made", 1), ("k_made", 1)], [])
        DVE_EARLY = ([], [("q_full", 0)], [("q_rem", 0), ("q_full", 1)],
                     [("q_part2", 0), ("q_rem", 1), ("q_part2", 1)])

        def experts():
            @block.sync
            def _(sp):
                sp.wait_ge(ring_used, ring_base[1])
                for t, name in ((wqkv, "a_wqkv"), (bqk, "a_bqk"), (wout, "a_wo")):
                    sp.dma_start(t, d[name]).then_inc(load_biased, 16)
                sp.dma_start(bv, d["a_bv"].to_broadcast([P, P])).then_inc(load_biased, 16)

            @block.scalar
            def _(act):
                for c in range(1, CH):
                    for k in range(0, HB, 2):
                        if c * HB + k >= EARLY:
                            relu_act(act, c, k)
                for item in EARLY_BIASED:
                    biased_act(act, *item)

            @block.gpsimd
            def _(pool):
                g_ = nc.gpsimd
                link = chain(pool, pool_step)
                pool.wait_ge(load_experts, 48)
                pool.wait_ge(av_done, UNITS[0])
                for i in range(NTILE):
                    pool.wait_ge(e_onehot, i // NT + 1)
                    link(g_.tensor_tensor(base[:, i, :], X[:, i, :], U[:, i, :], ALU.add))
                    link(g_.tensor_tensor(bpick, b2, spread(onehot[:, i, :], NE, P), ALU.mult))
                    for e in range(NE):
                        ins = g_.tensor_tensor(base[:, i, :], base[:, i, :], bpick[:, e, :], ALU.add)
                        if e < NE - 1:
                            link(ins)
                    ins.then_inc(e_based, 1)
                    pool.wait_ge(e_based, i + 1)
                for item in EARLY_BIASED:
                    biased_pool(pool, *item)

            @block.tensor
            def _(pe):
                pe.wait_ge(ring_used, ring_base[1])
                for c in range(1, CH + 1):
                    for k in range(HB):
                        if EARLY <= c * HB + k < CH * HB:
                            hidden(pe, c, k)
                        if c == CH and k == 0:
                            pe.wait_ge(hid_act, CH * HB // 2)
                            pe.wait_ge(hid_dve, CH * HB // 2)
                        if c == CH and k % 4 == 3:
                            for item in PE_EARLY[k // 4]:
                                biased_pe(pe, *item)
                        if k % 4 == 3:
                            t = 4 * (c - 1) + k // 4
                            if k == 3:
                                pe.wait_ge(hid_act, c * HB // 2)
                                pe.wait_ge(hid_dve, c * HB // 2)
                            ready(pe, ey_used, t - 3)
                            for m in range(HB):
                                e = m // EM
                                ins = nc.tensor.matmul(bank(EY_BANKS[t % 4])[:, e * P:(e + 1) * P],
                                                       hid[(c - 1) % 2][:, m, k // 4 * P:(k // 4 + 1) * P], w2[:, m, :],
                                                       start=(m % EM == 0), stop=(m % EM == EM - 1))
                            ins.then_inc(ey_done, 1)

            @block.vector
            def _(dve):
                v_ = nc.vector
                link = chain(dve, dve_step)

                for c in range(1, CH + 1):
                    for k in range(HB):
                        if EARLY <= c * HB + k < CH * HB and k % 2:
                            relu_dve(dve, c, k)
                        if k % 4 == 3:
                            i = 4 * (c - 1) + k // 4
                            dve.wait_ge(ey_done, i + 1)
                            dve.wait_ge(e_based, i + 1)
                            for e in range(NE):
                                ins = v_.scalar_tensor_tensor(
                                    out=X[:, i, :] if e == NE - 1 else base[:, i, :], in0=bank(EY_BANKS[i % 4])[:, e * P:(e + 1) * P],
                                    scalar=onehot[:, i, e:e + 1], in1=base[:, i, :], op0=ALU.mult, op1=ALU.add)
                                if e < NE - 1:
                                    link(ins)
                            ins.then_inc(ey_used, 1)
                            dve.wait_ge(ey_used, i + 1)
                            link(v_.bn_stats(stats[:, i, :], X[:, i, :]))
                            link(v_.bn_aggr(mv[:, i, :], stats[:, i, :]))
                        if c == CH and k % 4 == 3:
                            for item in DVE_EARLY[k // 4]:
                                biased_dve(dve, *item)
                    if c == 2:
                        layer_norm(dve, link, 1e-5, 0, NT).then_inc(x1_ready, 1)
                        dve.wait_ge(x1_ready, 1)
                    if c == 3:
                        link(layer_norm(dve, link, 1e-5, NT, NT + 4))
                layer_norm(dve, link, 1e-5, NT + 4, NTILE).then_inc(x1_ready, 1)
                dve.wait_ge(x1_ready, 2)

        def finish():
            @block.gpsimd
            def _(pool):
                for q in range(NTILE // QT):
                    pool.wait_ge(t_rstd, q + 1)
                    for i in range(QT * q + 1, QT * (q + 1), 2):
                        ins = nc.gpsimd.tensor_scalar(X[:, i, :], X[:, i, :], mv[:, i, 0:1], newton[:, 1, i:i + 1],
                                                      ALU.subtract, ALU.mult)
                    ins.then_inc(t_odd, 1)

            @block.sync
            def _(sp):
                rows = out.rearrange("(n p) d -> p n d", p=P)
                for q in range(NTILE // QT):
                    t = slice(q * QT, (q + 1) * QT)
                    sp.wait_ge(t_normed, q + 1)
                    sp.wait_ge(t_odd, q + 1)
                    sp.dma_start(rows[:, t, :], X[:, t, :]).then_inc(stored, 16)
                sp.wait_ge(stored, 16 * NTILE // QT)

        latent_projections()
        attention(0)
        experts()
        biased_projections()
        attention(1)
        finish()


def kernel(**inputs):
    import concourse.bacc as _bacc
    from concourse.bass_utils import run_bass_kernel_spmd as _run

    nc = _bacc.Bacc("TRN2", target_bir_lowering=False, num_devices=1)
    arrays = layout(inputs)
    d = {k: nc.dram_tensor(k, v.shape, mybir.dt.from_np(v.dtype), kind="ExternalInput").ap()
         for k, v in arrays.items()}
    out = nc.dram_tensor("out", (B * T, P), F32, kind="ExternalOutput").ap()
    build(nc, d, out)
    r = _run(nc, [arrays], core_ids=[0])
    return r.results[0]["out"].reshape(B, T, P)
```
